# Optimizing a Trainium2 kernel written in Bass

```python
import numpy as np
import jax
import jax.numpy as jnp

def _softmax(x, axis=-1):
    return jax.nn.softmax(x, axis=axis)

def _gelu(x):
    return jax.nn.gelu(x, approximate=True)

def _silu(x):
    return jax.nn.silu(x)

def _sigmoid(x):
    return jax.nn.sigmoid(x)

def _layernorm(x, axis=-1, eps=1e-05):
    m = jnp.mean(x, axis=axis, keepdims=True)
    v = jnp.var(x, axis=axis, keepdims=True)
    return (x - m) / jnp.sqrt(v + eps)

def _scatter_add(tgt, idx, src, axis=0):
    return tgt.at[idx].add(src)

def _segment_sum(src, seg, n):
    return jax.ops.segment_sum(src, seg, n)
kernel_name = 'mk_decoder_preln_d2_seqx_r4_eeadc5'

def setup_inputs(seed: int=0):
    np.random.seed(seed)
    _w = jnp.asarray

    def _rec_inputs():
        import jax
        import jax.numpy as jnp
        _rk = jax.random.key(seed)
        x = -0.0002928 + 1 * jax.random.normal(jax.random.fold_in(_rk, 1), (32, 256, 256), jnp.float32)
        _lenS = 256 - jax.random.randint(jax.random.fold_in(_rk, 7), (32,), 0, max(1, 256 // 4) + 1, jnp.int32)
        _lenS2 = 256 - jax.random.randint(jax.random.fold_in(_rk, 8), (32,), 0, max(1, 256 // 4) + 1, jnp.int32)
        _ctx_1024P = jax.random.normal(jax.random.fold_in(_rk, 11), (32, 16, 256), jnp.float32)
        _ctx_1024c = jax.random.dirichlet(jax.random.fold_in(_rk, 511), 0.3 * jnp.ones((16,), jnp.float32), (32, 256))
        _ctx_1024t = jnp.einsum('bsk,bkd->bsd', _ctx_1024c, _ctx_1024P)
        _ctx_1024t = _ctx_1024t * jax.lax.rsqrt(jnp.mean(jnp.square(_ctx_1024t)) + 1e-12) * 0.953939
        ctx_1024 = -1.39393e-06 + 0.999914 * (_ctx_1024t + 0.3 * jax.random.normal(jax.random.fold_in(_rk, 611), (32, 256, 256), jnp.float32))
        return (x, ctx_1024)
    x, ctx_1024 = _rec_inputs()

    def _L0_attn_setup():
        import jax, jax.numpy as jnp
        import numpy as np
        NUM_HEADS = 1
        LN_EPS = 1e-05
        key = jax.random.key(seed)
        ks = jax.random.split(key, 4)
        B, L, D = (8, 1024, 256)
        x = jax.random.normal(ks[0], (B, L, D), dtype=jnp.float32)
        qkv_w = jax.random.normal(ks[1], (3 * D, D), dtype=jnp.float32) * np.float32(np.sqrt(1.0 / D))
        qkv_b = jnp.zeros((3 * D,), dtype=jnp.float32)
        proj_w = jax.random.normal(ks[2], (D, D), dtype=jnp.float32) * np.float32(np.sqrt(1.0 / D))
        proj_b = jnp.zeros((D,), dtype=jnp.float32)
        return {'x': x, 'norm_w': jnp.ones((D,), dtype=jnp.float32), 'norm_b': jnp.zeros((D,), dtype=jnp.float32), 'qkv_w': qkv_w, 'qkv_b': qkv_b, 'proj_w': proj_w, 'proj_b': proj_b}
    _L0_attn_all = _L0_attn_setup()
    _L0_attn_in = {k: v for k, v in _L0_attn_all.items() if k in ('norm_w', 'norm_b', 'qkv_w', 'qkv_b', 'proj_w', 'proj_b')}
    del _L0_attn_all

    def _L0_xattn_setup():
        import jax, jax.numpy as jnp
        import numpy as np
        B, S, DIM, NH = (2, 512, 256, 8)
        DH = DIM // NH
        GATE_SOFT_CAP = 15.0
        BACKEND_EPS = 5e-05
        NORM_EPS = 1e-06

        def _mlstm_parallel(q, k, v, i_pre, f_pre):
            log_fg = jax.nn.log_sigmoid(f_pre)
            lf_cs = jnp.cumsum(log_fg, axis=-1)
            lf = jnp.concatenate([jnp.zeros_like(lf_cs[..., :1]), lf_cs], axis=-1)
            log_d = lf[..., 1:, None] - lf[..., None, 1:] + i_pre[..., None, :]
            t_idx = jnp.arange(q.shape[2])
            mask = t_idx[:, None] >= t_idx[None, :]
            log_d = jnp.where(mask, log_d, -jnp.inf)
            m = jnp.max(log_d, axis=-1, keepdims=True)
            d_mat = jnp.exp(log_d - m)
            scores = jnp.einsum('bhtd,bhsd->bhts', q, k) * (1.0 / np.sqrt(DH))
            s_mat = scores * d_mat
            denom = jnp.maximum(jnp.abs(jnp.sum(s_mat, axis=-1, keepdims=True)), jnp.exp(-m)) + BACKEND_EPS
            return jnp.einsum('bhts,bhsd->bhtd', s_mat, v) / denom
        key = jax.random.key(seed)
        kq, kk, kv, kw = jax.random.split(key, 4)
        q = jax.random.normal(kq, (B, S, DIM), dtype=jnp.float32)
        k = jax.random.normal(kk, (B, S, DIM), dtype=jnp.float32)
        v = jax.random.normal(kv, (B, S, DIM), dtype=jnp.float32)
        ifgate_w = 0.02 * jax.random.normal(kw, (2 * NH, 3 * DIM), dtype=jnp.float32)
        ifgate_b = jnp.concatenate([jnp.full((NH,), -10.0, dtype=jnp.float32), jnp.linspace(3.0, 6.0, NH, dtype=jnp.float32)])
        outnorm_w = jnp.zeros((DIM,), dtype=jnp.float32)
        return {'q': q, 'k': k, 'v': v, 'ifgate_w': ifgate_w, 'ifgate_b': ifgate_b, 'outnorm_w': outnorm_w}
    _L0_xattn_all = _L0_xattn_setup()
    _L0_xattn_in = {k: v for k, v in _L0_xattn_all.items() if k in ('ifgate_w', 'ifgate_b', 'outnorm_w')}
    del _L0_xattn_all

    def _L0_ffn_setup():
        import jax, jax.numpy as jnp
        import numpy as np
        S, B, H, F, E, K = (512, 2, 256, 512, 8, 2)

        def _moe_forward(hidden_states, router_w, w1, b1, w2, b2):
            s, b, h = hidden_states.shape
            T = s * b
            x = hidden_states.reshape(T, h)
            logits = jnp.einsum('th,eh->te', x, router_w)
            topk_logits, topk_idx = jax.lax.top_k(logits, K)
            probs = jax.nn.softmax(topk_logits, axis=-1)
            combine = jnp.zeros((T, E), dtype=x.dtype)
            combine = combine.at[jnp.arange(T)[:, None], topk_idx].add(probs.astype(x.dtype))
            hmid = jnp.einsum('th,efh->etf', x, w1) + b1[:, None, :]
            hmid = jax.nn.gelu(hmid, approximate=False)
            y = jnp.einsum('etf,ehf->eth', hmid, w2) + b2[:, None, :]
            out = jnp.einsum('eth,te->th', y, combine)
            return out.reshape(s, b, h)
        key = jax.random.key(seed)
        ks = jax.random.split(key, 6)
        std = 0.02
        return {'hidden_states': jax.random.normal(ks[0], (S, B, H), dtype=jnp.float32), 'router_w': jax.random.normal(ks[1], (E, H), dtype=jnp.float32) * std, 'w1': jax.random.normal(ks[2], (E, F, H), dtype=jnp.float32) * (1.0 / np.sqrt(H)), 'b1': jnp.zeros((E, F), dtype=jnp.float32), 'w2': jax.random.normal(ks[3], (E, H, F), dtype=jnp.float32) * (1.0 / np.sqrt(F)), 'b2': jnp.zeros((E, H), dtype=jnp.float32)}
    _L0_ffn_all = _L0_ffn_setup()
    _L0_ffn_in = {k: v for k, v in _L0_ffn_all.items() if k in ('router_w', 'w1', 'b1', 'w2', 'b2')}
    del _L0_ffn_all

    def _L1_attn_setup():
        import jax, jax.numpy as jnp
        import numpy as np
        B, S, D = (4, 512, 256)

        def _wkv(k, v, time_decay, u):
            w = -jnp.exp(time_decay)
            b, s, d = k.shape
            aa = jnp.zeros((b, d), k.dtype)
            bb = jnp.zeros((b, d), k.dtype)
            pp = jnp.full((b, d), -1e+30, k.dtype)

            def step(carry, kv):
                aa, bb, pp = carry
                kk, vv = kv
                ww = u + kk
                p = jnp.maximum(pp, ww)
                e1 = jnp.exp(pp - p)
                e2 = jnp.exp(ww - p)
                out = (e1 * aa + e2 * vv) / (e1 * bb + e2)
                ww2 = w + pp
                p2 = jnp.maximum(ww2, kk)
                e1b = jnp.exp(ww2 - p2)
                e2b = jnp.exp(kk - p2)
                return ((e1b * aa + e2b * vv, e1b * bb + e2b, p2), out)
            _, outs = jax.lax.scan(step, (aa, bb, pp), (k.transpose(1, 0, 2), v.transpose(1, 0, 2)))
            return outs.transpose(1, 0, 2)
        key = jax.random.key(seed)
        ks = jax.random.split(key, 10)
        s = 0.02
        return {'x': jax.random.normal(ks[0], (B, S, D), jnp.float32), 'time_mix_k': jax.random.uniform(ks[1], (1, 1, D), jnp.float32), 'time_mix_v': jax.random.uniform(ks[2], (1, 1, D), jnp.float32), 'time_mix_r': jax.random.uniform(ks[3], (1, 1, D), jnp.float32), 'time_decay': jax.random.normal(ks[4], (D,), jnp.float32) * 0.1, 'time_first': jax.random.normal(ks[5], (D,), jnp.float32) * 0.1, 'Wk': jax.random.normal(ks[6], (D, D), jnp.float32) * s, 'Wv': jax.random.normal(ks[7], (D, D), jnp.float32) * s, 'Wr': jax.random.normal(ks[8], (D, D), jnp.float32) * s, 'Wo': jax.random.normal(ks[9], (D, D), jnp.float32) * s}
    _L1_attn_all = _L1_attn_setup()
    _L1_attn_in = {k: v for k, v in _L1_attn_all.items() if k in ('time_mix_k', 'time_mix_v', 'time_mix_r', 'time_decay', 'time_first', 'Wk', 'Wv', 'Wr', 'Wo')}
    del _L1_attn_all

    def _L1_xattn_setup():
        import jax, jax.numpy as jnp
        import numpy as np
        B, SQ, SKV, E, H = (4, 512, 512, 256, 16)
        HD = E // H

        def stablemax(x):
            s = jnp.where(x >= 0, x + 1.0, 1.0 / (1.0 - x))
            return s / jnp.sum(s, axis=-1, keepdims=True)
        key = jax.random.key(seed)
        ks = jax.random.split(key, 6)
        scale = 1.0 / np.sqrt(E)
        return {'query': jax.random.normal(ks[0], (B, SQ, E), jnp.float32), 'key_value': jax.random.normal(ks[1], (B, SKV, E), jnp.float32), 'Wq': jax.random.normal(ks[2], (E, E), jnp.float32) * scale, 'bq': jnp.zeros((E,), jnp.float32), 'Wk': jax.random.normal(ks[3], (E, E), jnp.float32) * scale, 'bk': jnp.zeros((E,), jnp.float32), 'Wv': jax.random.normal(ks[4], (E, E), jnp.float32) * scale, 'bv': jnp.zeros((E,), jnp.float32), 'Wo': jax.random.normal(ks[5], (E, E), jnp.float32) * scale, 'bo': jnp.zeros((E,), jnp.float32)}
    _L1_xattn_all = _L1_xattn_setup()
    _L1_xattn_in = {k: v for k, v in _L1_xattn_all.items() if k in ('Wq', 'bq', 'Wk', 'bk', 'Wv', 'bv', 'Wo', 'bo')}
    del _L1_xattn_all

    def _L1_ffn_setup():
        import jax, jax.numpy as jnp
        import numpy as np

        def _ste(w, w_q):
            return w + jax.lax.stop_gradient(w_q - w)

        def quantize_w8_per(w, axis):
            amax = jnp.clip(jnp.max(jnp.abs(w), axis=axis, keepdims=True), 1e-08, None)
            scale = 127.0 / amax
            w_q = jnp.clip(jnp.round(w * scale), -128.0, 127.0) / scale
            return _ste(w, w_q)

        def quantize_a16(x):
            amax = jnp.clip(jnp.max(jnp.abs(x)), 1e-08, None)
            scale = 32767.0 / amax
            x_q = jnp.clip(jnp.round(x * scale), -32768.0, 32767.0) / scale
            return _ste(x, x_q)
        key = jax.random.key(seed)
        k1, k2, k3 = jax.random.split(key, 3)
        d_model, d_ff = (256, 1024)
        x = jax.random.normal(k1, (4, 512, d_model), dtype=jnp.float32)
        W_in = jax.random.normal(k2, (d_model, d_ff), dtype=jnp.float32) / np.sqrt(d_model)
        b_in = jnp.zeros((d_ff,), dtype=jnp.float32)
        W_out = jax.random.normal(k3, (d_ff, d_model), dtype=jnp.float32) / np.sqrt(d_ff)
        b_out = jnp.zeros((d_model,), dtype=jnp.float32)
        return {'x': x, 'W_in': W_in, 'b_in': b_in, 'W_out': W_out, 'b_out': b_out}
    _L1_ffn_all = _L1_ffn_setup()
    _L1_ffn_in = {k: v for k, v in _L1_ffn_all.items() if k in ('W_in', 'b_in', 'W_out', 'b_out')}
    del _L1_ffn_all
    return {'x': x, 'ctx_1024': ctx_1024, 'L0_attn_norm_w': _L0_attn_in['norm_w'], 'L0_attn_norm_b': _L0_attn_in['norm_b'], 'L0_attn_qkv_w': _L0_attn_in['qkv_w'], 'L0_attn_qkv_b': _L0_attn_in['qkv_b'], 'L0_attn_proj_w': _L0_attn_in['proj_w'], 'L0_attn_proj_b': _L0_attn_in['proj_b'], 'L0_xattn_ifgate_w': _L0_xattn_in['ifgate_w'], 'L0_xattn_ifgate_b': _L0_xattn_in['ifgate_b'], 'L0_xattn_outnorm_w': _L0_xattn_in['outnorm_w'], 'L0_ffn_router_w': _L0_ffn_in['router_w'], 'L0_ffn_w1': _L0_ffn_in['w1'], 'L0_ffn_b1': _L0_ffn_in['b1'], 'L0_ffn_w2': _L0_ffn_in['w2'], 'L0_ffn_b2': _L0_ffn_in['b2'], 'L1_attn_time_mix_k': _L1_attn_in['time_mix_k'], 'L1_attn_time_mix_v': _L1_attn_in['time_mix_v'], 'L1_attn_time_mix_r': _L1_attn_in['time_mix_r'], 'L1_attn_time_decay': _L1_attn_in['time_decay'], 'L1_attn_time_first': _L1_attn_in['time_first'], 'L1_attn_Wk': _L1_attn_in['Wk'], 'L1_attn_Wv': _L1_attn_in['Wv'], 'L1_attn_Wr': _L1_attn_in['Wr'], 'L1_attn_Wo': _L1_attn_in['Wo'], 'L1_xattn_Wq': _L1_xattn_in['Wq'], 'L1_xattn_bq': _L1_xattn_in['bq'], 'L1_xattn_Wk': _L1_xattn_in['Wk'], 'L1_xattn_bk': _L1_xattn_in['bk'], 'L1_xattn_Wv': _L1_xattn_in['Wv'], 'L1_xattn_bv': _L1_xattn_in['bv'], 'L1_xattn_Wo': _L1_xattn_in['Wo'], 'L1_xattn_bo': _L1_xattn_in['bo'], 'L1_ffn_W_in': _L1_ffn_in['W_in'], 'L1_ffn_b_in': _L1_ffn_in['b_in'], 'L1_ffn_W_out': _L1_ffn_in['W_out'], 'L1_ffn_b_out': _L1_ffn_in['b_out']}

def reference(x, ctx_1024, L0_attn_norm_w, L0_attn_norm_b, L0_attn_qkv_w, L0_attn_qkv_b, L0_attn_proj_w, L0_attn_proj_b, L0_xattn_ifgate_w, L0_xattn_ifgate_b, L0_xattn_outnorm_w, L0_ffn_router_w, L0_ffn_w1, L0_ffn_b1, L0_ffn_w2, L0_ffn_b2, L1_attn_time_mix_k, L1_attn_time_mix_v, L1_attn_time_mix_r, L1_attn_time_decay, L1_attn_time_first, L1_attn_Wk, L1_attn_Wv, L1_attn_Wr, L1_attn_Wo, L1_xattn_Wq, L1_xattn_bq, L1_xattn_Wk, L1_xattn_bk, L1_xattn_Wv, L1_xattn_bv, L1_xattn_Wo, L1_xattn_bo, L1_ffn_W_in, L1_ffn_b_in, L1_ffn_W_out, L1_ffn_b_out):
    import jax
    import jax.numpy as jnp

    def _L0_attn_ref(x, norm_w, norm_b, qkv_w, qkv_b, proj_w, proj_b):
        import jax, jax.numpy as jnp
        import numpy as np
        NUM_HEADS = 1
        LN_EPS = 1e-05
        B, L, D = x.shape
        H = NUM_HEADS
        mu = jnp.mean(x, axis=-1, keepdims=True)
        var = jnp.mean(jnp.square(x - mu), axis=-1, keepdims=True)
        h = (x - mu) / jnp.sqrt(var + LN_EPS) * norm_w + norm_b
        qkv = h @ qkv_w.T + qkv_b
        qkv = qkv.reshape(B * H, L // H, 3, D)
        q, k, v = (qkv[..., 0, :], qkv[..., 1, :], qkv[..., 2, :])
        scale = np.float32(1.0 / np.sqrt(L // H))
        w = jax.nn.softmax(jnp.einsum('ncq,nck->nqk', q, k * scale), axis=2)
        a = jnp.einsum('nqk,nck->ncq', w, v)
        a = a.reshape(B, L, D)
        return a @ proj_w.T + proj_b + x

    def _L0_xattn_ref(q, k, v, ifgate_w, ifgate_b, outnorm_w):
        import jax, jax.numpy as jnp
        import numpy as np
        B, S, DIM, NH = (2, 512, 256, 8)
        DH = DIM // NH
        GATE_SOFT_CAP = 15.0
        BACKEND_EPS = 5e-05
        NORM_EPS = 1e-06

        def _mlstm_parallel(q, k, v, i_pre, f_pre):
            log_fg = jax.nn.log_sigmoid(f_pre)
            lf_cs = jnp.cumsum(log_fg, axis=-1)
            lf = jnp.concatenate([jnp.zeros_like(lf_cs[..., :1]), lf_cs], axis=-1)
            log_d = lf[..., 1:, None] - lf[..., None, 1:] + i_pre[..., None, :]
            t_idx = jnp.arange(q.shape[2])
            mask = t_idx[:, None] >= t_idx[None, :]
            log_d = jnp.where(mask, log_d, -jnp.inf)
            m = jnp.max(log_d, axis=-1, keepdims=True)
            d_mat = jnp.exp(log_d - m)
            scores = jnp.einsum('bhtd,bhsd->bhts', q, k) * (1.0 / np.sqrt(DH))
            s_mat = scores * d_mat
            denom = jnp.maximum(jnp.abs(jnp.sum(s_mat, axis=-1, keepdims=True)), jnp.exp(-m)) + BACKEND_EPS
            return jnp.einsum('bhts,bhsd->bhtd', s_mat, v) / denom
        b, s, dim = q.shape
        gate_in = jnp.concatenate([q, k, v], axis=-1)
        pre = gate_in @ ifgate_w.T + ifgate_b
        pre = GATE_SOFT_CAP * jnp.tanh(pre / GATE_SOFT_CAP)
        i_pre = pre[..., :NH].transpose(0, 2, 1)
        f_pre = pre[..., NH:].transpose(0, 2, 1)
        qh = q.reshape(b, s, NH, DH).transpose(0, 2, 1, 3)
        kh = k.reshape(b, s, NH, DH).transpose(0, 2, 1, 3)
        vh = v.reshape(b, s, NH, DH).transpose(0, 2, 1, 3)
        h = _mlstm_parallel(qh, kh, vh, i_pre, f_pre)
        rrms = jax.lax.rsqrt(jnp.mean(h * h, axis=-1, keepdims=True) + NORM_EPS)
        gain = (1.0 + outnorm_w).reshape(1, NH, 1, DH)
        h = h * rrms * gain
        return h.transpose(0, 2, 1, 3).reshape(b, s, dim)

    def _L0_ffn_ref(hidden_states, router_w, w1, b1, w2, b2):
        import jax, jax.numpy as jnp
        import numpy as np
        S, B, H, F, E, K = (512, 2, 256, 512, 8, 2)

        def _moe_forward(hidden_states, router_w, w1, b1, w2, b2):
            s, b, h = hidden_states.shape
            T = s * b
            x = hidden_states.reshape(T, h)
            logits = jnp.einsum('th,eh->te', x, router_w)
            topk_logits, topk_idx = jax.lax.top_k(logits, K)
            probs = jax.nn.softmax(topk_logits, axis=-1)
            combine = jnp.zeros((T, E), dtype=x.dtype)
            combine = combine.at[jnp.arange(T)[:, None], topk_idx].add(probs.astype(x.dtype))
            hmid = jnp.einsum('th,efh->etf', x, w1) + b1[:, None, :]
            hmid = jax.nn.gelu(hmid, approximate=False)
            y = jnp.einsum('etf,ehf->eth', hmid, w2) + b2[:, None, :]
            out = jnp.einsum('eth,te->th', y, combine)
            return out.reshape(s, b, h)
        return _moe_forward(hidden_states, router_w, w1, b1, w2, b2)

    def _L1_attn_ref(x, time_mix_k, time_mix_v, time_mix_r, time_decay, time_first, Wk, Wv, Wr, Wo):
        import jax, jax.numpy as jnp
        import numpy as np
        B, S, D = (4, 512, 256)

        def _wkv(k, v, time_decay, u):
            w = -jnp.exp(time_decay)
            b, s, d = k.shape
            aa = jnp.zeros((b, d), k.dtype)
            bb = jnp.zeros((b, d), k.dtype)
            pp = jnp.full((b, d), -1e+30, k.dtype)

            def step(carry, kv):
                aa, bb, pp = carry
                kk, vv = kv
                ww = u + kk
                p = jnp.maximum(pp, ww)
                e1 = jnp.exp(pp - p)
                e2 = jnp.exp(ww - p)
                out = (e1 * aa + e2 * vv) / (e1 * bb + e2)
                ww2 = w + pp
                p2 = jnp.maximum(ww2, kk)
                e1b = jnp.exp(ww2 - p2)
                e2b = jnp.exp(kk - p2)
                return ((e1b * aa + e2b * vv, e1b * bb + e2b, p2), out)
            _, outs = jax.lax.scan(step, (aa, bb, pp), (k.transpose(1, 0, 2), v.transpose(1, 0, 2)))
            return outs.transpose(1, 0, 2)
        shifted = jnp.concatenate([jnp.zeros_like(x[:, :1, :]), x[:, :-1, :]], axis=1)
        xk = x * time_mix_k + shifted * (1.0 - time_mix_k)
        xv = x * time_mix_v + shifted * (1.0 - time_mix_v)
        xr = x * time_mix_r + shifted * (1.0 - time_mix_r)
        k = jnp.einsum('bsd,ed->bse', xk, Wk)
        v = jnp.einsum('bsd,ed->bse', xv, Wv)
        r = jax.nn.sigmoid(jnp.einsum('bsd,ed->bse', xr, Wr))
        wkv = _wkv(k, v, time_decay, time_first)
        out = jnp.einsum('bsd,ed->bse', r * wkv, Wo)
        return out

    def _L1_xattn_ref(query, key_value, Wq, bq, Wk, bk, Wv, bv, Wo, bo):
        import jax, jax.numpy as jnp
        import numpy as np
        B, SQ, SKV, E, H = (4, 512, 512, 256, 16)
        HD = E // H

        def stablemax(x):
            s = jnp.where(x >= 0, x + 1.0, 1.0 / (1.0 - x))
            return s / jnp.sum(s, axis=-1, keepdims=True)
        b = query.shape[0]
        q = query @ Wq.T + bq
        k = key_value @ Wk.T + bk
        v = key_value @ Wv.T + bv
        q = q.reshape(b, -1, H, HD).transpose(0, 2, 1, 3)
        k = k.reshape(b, -1, H, HD).transpose(0, 2, 1, 3)
        v = v.reshape(b, -1, H, HD).transpose(0, 2, 1, 3)
        scores = jnp.einsum('bhqd,bhkd->bhqk', q, k) / np.sqrt(HD).astype(np.float32)
        attn = stablemax(scores)
        context = jnp.einsum('bhqk,bhkd->bhqd', attn, v)
        context = context.transpose(0, 2, 1, 3).reshape(b, -1, E)
        return context @ Wo.T + bo

    def _L1_ffn_ref(x, W_in, b_in, W_out, b_out):
        import jax, jax.numpy as jnp
        import numpy as np

        def _ste(w, w_q):
            return w + jax.lax.stop_gradient(w_q - w)

        def quantize_w8_per(w, axis):
            amax = jnp.clip(jnp.max(jnp.abs(w), axis=axis, keepdims=True), 1e-08, None)
            scale = 127.0 / amax
            w_q = jnp.clip(jnp.round(w * scale), -128.0, 127.0) / scale
            return _ste(w, w_q)

        def quantize_a16(x):
            amax = jnp.clip(jnp.max(jnp.abs(x)), 1e-08, None)
            scale = 32767.0 / amax
            x_q = jnp.clip(jnp.round(x * scale), -32768.0, 32767.0) / scale
            return _ste(x, x_q)
        W_in_sim = quantize_w8_per(W_in, axis=0)
        W_out_sim = quantize_w8_per(W_out, axis=1)
        x_sim = quantize_a16(x)
        hidden = jax.nn.gelu(x_sim @ W_in_sim + b_in, approximate=False)
        hidden_sim = quantize_a16(hidden)
        out = hidden_sim @ W_out_sim + b_out
        return out
    x = x + _L0_attn_ref(_layernorm(x, axis=-1), L0_attn_norm_w, L0_attn_norm_b, L0_attn_qkv_w, L0_attn_qkv_b, L0_attn_proj_w, L0_attn_proj_b)
    x = x + _L0_xattn_ref(_layernorm(x, axis=-1), ctx_1024, ctx_1024, L0_xattn_ifgate_w, L0_xattn_ifgate_b, L0_xattn_outnorm_w)
    x = x + _L0_ffn_ref(_layernorm(x, axis=-1), L0_ffn_router_w, L0_ffn_w1, L0_ffn_b1, L0_ffn_w2, L0_ffn_b2)
    x = x + _L1_attn_ref(_layernorm(x, axis=-1), L1_attn_time_mix_k, L1_attn_time_mix_v, L1_attn_time_mix_r, L1_attn_time_decay, L1_attn_time_first, L1_attn_Wk, L1_attn_Wv, L1_attn_Wr, L1_attn_Wo)
    x = x + _L1_xattn_ref(_layernorm(x, axis=-1), ctx_1024, L1_xattn_Wq, L1_xattn_bq, L1_xattn_Wk, L1_xattn_bk, L1_xattn_Wv, L1_xattn_bv, L1_xattn_Wo, L1_xattn_bo)
    x = x + _L1_ffn_ref(_layernorm(x, axis=-1), L1_ffn_W_in, L1_ffn_b_in, L1_ffn_W_out, L1_ffn_b_out)
    return x

_drawn_inputs = setup_inputs


def setup_inputs(seed=0):
    import zlib

    import numpy as np

    out = dict(_drawn_inputs(seed))
    spreads = {'L0_attn_norm_w': (1.0, 0.2),
     'L0_attn_norm_b': (0.0, 0.1),
     'L0_attn_qkv_b': (0.0, 0.1),
     'L0_attn_proj_b': (0.0, 0.1),
     'L0_xattn_outnorm_w': (0.0, 0.1),
     'L0_ffn_b1': (0.0, 0.433),
     'L0_ffn_b2': (0.0, 0.296),
     'L1_xattn_bq': (0.0, 2.0),
     'L1_xattn_bk': (0.0, 2.0),
     'L1_xattn_bv': (0.0, 0.8),
     'L1_xattn_bo': (0.0, 0.8),
     'L1_ffn_b_in': (0.0, 1.384),
     'L1_ffn_b_out': (0.0, 0.8)}
    factors = {'L1_attn_time_mix_k': 8.0,
     'L1_attn_time_mix_v': 8.0,
     'L1_attn_time_mix_r': 8.0,
     'L1_attn_time_decay': 8.0,
     'L1_attn_time_first': 8.0,
     'L1_attn_Wk': 8.0,
     'L1_attn_Wv': 5.333,
     'L1_attn_Wr': 8.0,
     'L1_attn_Wo': 5.359,
     'L1_xattn_Wq': 6.797,
     'L1_xattn_Wk': 5.487}
    for name, (base, spread) in spreads.items():
        noise = np.random.default_rng([zlib.crc32(name.encode()), seed]).standard_normal(out[name].shape)
        drawn = base * np.exp(spread * noise) if base else spread * noise
        out[name] = jnp.asarray(drawn.astype(out[name].dtype))
    for name, factor in factors.items():
        out[name] = (out[name] * factor).astype(out[name].dtype)
    return out
```

```python
import concourse.bass as bass
from concourse import mybir
from contextlib import ExitStack

FP = mybir.dt.float32
BF = mybir.dt.bfloat16
ALU = mybir.AluOpType
ACT = mybir.ActivationFunctionType
AX = mybir.AxisListType

B, S, D = 32, 256, 256
P = 128
NT = B * S // P
TB = S // P
DC = D // P
PAIR = 2
TRIPS = B // PAIR
EPS = 1e-5


def batch_of(i, p):
    return i * PAIR + (p + 1)


class Chain:

    def __init__(self, eng, sem, per=0, trip=0, before=0):
        self.eng, self.sem, self.base, self.per, self.n = eng, sem, trip * per + before, per, 0

    def did(self, ins):
        self.n += 1
        ins.then_inc(self.sem, 1)
        return self

    def see(self):
        self.eng.wait_ge(self.sem, self.base + self.n)

    def end(self):
        assert self.n == self.per, (self.sem, self.n, self.per)


def signals(nc, ctx, prefix):
    held = []

    def give_back():
        nc.clear_and_free_semaphores(held)
        nc.all_engine_barrier()

    def sem(name):
        held.append(nc.alloc_semaphore(prefix + name))
        return held[-1]

    ctx.callback(give_back)
    return sem


def load_everything(nc, t, d):
    ctx = ExitStack()
    with ctx:
        sem = signals(nc, ctx, "ld_")
        QUARTERS = 4
        x_in, const_in, stats_done = [sem(f"x_in{q}") for q in range(QUARTERS)], sem("const_in"), sem("ld_stats")
        block = ctx.enter_context(nc.Block())

        @block.sync
        def _(sp):
            for name, dram in (("ident", d["ident"]), ("maskneg", d["maskneg"]), ("identb", d["identb"])):
                sp.dma_start(t[name][:], dram).then_inc(const_in, 16)
            view = d["x"].rearrange("(n p) d -> p n d", p=P)
            for q in range(QUARTERS):
                n0 = q * NT // QUARTERS
                sp.dma_start(t["X"][:, n0:n0 + NT // QUARTERS, :], view[:, n0:n0 + NT // QUARTERS, :]).then_inc(x_in[q], 16)
            sp.wait_ge(const_in, 48)

        @block.vector
        def _(dve):
            nc.vector.memset(t["eps"][:], EPS)
            for q in range(QUARTERS):
                dve.wait_ge(x_in[q], 16)
                with dve.Fori(q * NT // QUARTERS, (q + 1) * NT // QUARTERS) as n:
                    nc.vector.bn_stats(t["bn"][:, bass.ds(n, 1), :].rearrange("p o s -> p (o s)"),
                                       t["X"][:, bass.ds(n, 1), :].rearrange("p o d -> p (o d)")).then_inc(stats_done, 1)
            dve.wait_ge(stats_done, NT)


def row_stats(nc, t, tag):
    ctx = ExitStack()
    with ctx:
        sem = signals(nc, ctx, tag)
        root, done = sem("_root"), sem("_steps")
        block = ctx.enter_context(nc.Block())
        VAR_STEPS = 6

        @block.scalar
        def _(act):
            act.wait_ge(done, VAR_STEPS)
            nc.scalar.activation(t["rstd"][:], t["var"][:], ACT.Sqrt, bias=t["eps"][:]).then_inc(root, 1)

        @block.vector
        def _(dve):
            even, odd = (t["bn"][:, :, 3 * h + 1] for h in range(2))
            spread, mean, var = t["rstd"], t["mean"], t["var"]
            ch = Chain(dve, done, VAR_STEPS + 1)
            ch.did(nc.vector.tensor_tensor(mean[:], even, odd, ALU.add))
            ch.did(nc.vector.tensor_tensor(spread[:], even, odd, ALU.subtract))
            ch.did(nc.vector.tensor_tensor(var[:], t["bn"][:, :, 2], t["bn"][:, :, 5], ALU.add)).see()
            nc.vector.tensor_scalar(mean[:], mean[:], 0.5, None, ALU.mult)
            ch.did(nc.vector.tensor_tensor(spread[:], spread[:], spread[:], ALU.mult))
            ch.did(nc.vector.tensor_scalar(var[:], var[:], 1.0 / D, None, ALU.mult)).see()
            ch.did(nc.vector.scalar_tensor_tensor(var[:], spread[:], 0.25, var[:], ALU.mult, ALU.add))
            dve.wait_ge(root, 1)
            ch.did(nc.vector.reciprocal(t["rstd"][:], t["rstd"][:])).see()
            ch.end()


def update_stats(nc, t, tile, took_wait):
    nc.vector.sem_inc(took_wait, 1)
    for c in range(TB):
        nc.vector.bn_stats(t["bn"][:, bass.ds(tile + c, 1), :].rearrange("p o s -> p (o s)"),
                           t["X"][:, bass.ds(tile + c, 1), :].rearrange("p o d -> p (o d)"))


def layer0_attention(nc, t, d, bank):
    ctx = ExitStack()
    with ctx:
        sem = signals(nc, ctx, "a_")
        sb = lambda n, shape, dt=FP: ctx.enter_context(nc.sbuf_tensor("a_" + n, shape, dt))
        wqk, wv, wproj = sb("wqk", [P, DC, 2 * D]), sb("wv", [P, DC, D]), sb("wproj", [P, DC, D])
        bqk, bproj = sb("bqk", [P, 2 * D]), sb("bproj", [P, D])
        cols = sb("cols", [P, 3, DC])
        var2, r2 = sb("var2", [P, NT]), sb("r2", [P, NT])
        r12, gain, shift = sb("r12", [P, NT]), sb("gain", [P, NT]), sb("shift", [P, NT])
        z = [sb(f"z{p}", [P, TB, D]) for p in range(PAIR)]
        hT = [sb(f"hT{p}", [P, DC, S]) for p in range(PAIR)]
        qk = [sb(f"qk{p}", [P, TB, 2 * D]) for p in range(PAIR)]
        vT = [sb(f"vT{p}", [P, DC, S]) for p in range(PAIR)]
        top = sb("top", [P, PAIR, DC])
        ntop = sb("ntop", [P, PAIR, DC])
        e = [sb(f"e{p}", [P, DC, D]) for p in range(PAIR)]
        esum, rsum = sb("esum", [P, PAIR, DC]), sb("rsum", [P, PAIR, DC])
        eT = [sb(f"eT{p}", [P, DC, D]) for p in range(PAIR)]
        aT = [sb(f"aT{p}", [P, DC, S]) for p in range(PAIR)]
        res = [sb(f"res{p}", [P, TB, D]) for p in range(PAIR)]
        w_in, root = sem("w_in"), sem("root")
        z_ready, zT_ready, hT_ready = sem("z"), sem("zT"), sem("hT")
        qk_raw, qk_ready, v_raw, v_ready = sem("qk_raw"), sem("qk"), sem("v_raw"), sem("v")
        sc_raw, ntop_ready, e_ready = sem("sc_raw"), sem("ntop"), sem("e")
        eT_raw, eT_ready, rsum_ready = sem("eT_raw"), sem("eT"), sem("rsum")
        a_raw, a_ready, o_raw, x_done = sem("a_raw"), sem("a"), sem("o_raw"), sem("x_done")
        res_scaled, res_ready, v_steps = sem("res_scaled"), sem("res"), sem("v_steps")
        took_wait = sem("took_wait")
        zB, qB, vB = (lambda p: bank[4 * p]), (lambda p: (bank[4 * p + 1], bank[4 * p + 2])), (lambda p: bank[4 * p + 3])
        ONCE, PER = 7, 2
        block = ctx.enter_context(nc.Block())

        @block.sync
        def _(sp):
            for dst, src in ((wqk, "wqk"), (wv, "wv"), (wproj, "wproj"), (cols, "acols"), (bqk, "bqk"), (bproj, "bproj")):
                sp.dma_start(dst[:], d[src]).then_inc(w_in, 16)

        @block.gpsimd
        def _(pool):
            pool.wait_ge(w_in, 96)
            with pool.Fori(0, TRIPS) as i:
                for p in range(PAIR):
                    pool.wait_ge(res_scaled, batch_of(i, p) * TB)
                    nc.gpsimd.tensor_tensor(res[p][:], res[p][:], bproj[:, None, :].to_broadcast([P, TB, D]), ALU.add).then_inc(res_ready, 1)

        @block.scalar
        def _(act):
            act.wait_ge(v_steps, 2)
            nc.scalar.activation(r2[:], var2[:], ACT.Sqrt, bias=t["eps"][:]).then_inc(root, 1)
            nc.scalar.preload_act_table(ACT.Exp)
            act.wait_ge(w_in, 96)
            with act.Fori(0, TRIPS) as i:
                for p in range(PAIR):
                    act.wait_ge(zT_ready, batch_of(i, p))
                    for c in range(DC):
                        nc.scalar.activation(hT[p][:, c, :], zB(p)[:, c * S:(c + 1) * S], ACT.Identity,
                                             bias=cols[:, 1, c:c + 1], scale=cols[:, 0, c:c + 1]).then_inc(hT_ready, 1)
                for p in range(PAIR):
                    act.wait_ge(v_raw, batch_of(i, p))
                    for c in range(DC):
                        nc.scalar.activation(vT[p][:, c, :], vB(p)[:, c * S:(c + 1) * S], ACT.Identity,
                                             bias=cols[:, 2, c:c + 1]).then_inc(v_ready, 1)
                for p in range(PAIR):
                    act.wait_ge(ntop_ready, batch_of(i, p))
                    for c in range(DC):
                        nc.scalar.activation(e[p][:, c, :], zB(p)[:, c * D:(c + 1) * D], ACT.Exp,
                                             bias=ntop[:, p, c:c + 1], scale=1.0 / 16,
                                             accum_out=esum[:, p, c:c + 1]).then_inc(e_ready, 1)
                for p in range(PAIR):
                    act.wait_ge(a_raw, batch_of(i, p))
                    act.wait_ge(rsum_ready, batch_of(i, p))
                    for c in range(DC):
                        nc.scalar.activation(aT[p][:, c, :], qB(p)[1][:, c * S:(c + 1) * S], ACT.Identity,
                                             scale=rsum[:, p, c:c + 1]).then_inc(a_ready, 1)

        @block.tensor
        def _(pe):
            pe.wait_ge(w_in, 96)
            with pe.Fori(0, TRIPS) as i:
                for p in range(PAIR):
                    pe.wait_ge(z_ready, batch_of(i, p) * TB)
                    for c in range(DC):
                        for n in range(TB):
                            last = nc.tensor.transpose(zB(p)[:, c * S + n * P:c * S + (n + 1) * P],
                                                       z[p][:, n, c * P:(c + 1) * P], t["ident"][:])
                    last.then_inc(zT_ready, 1)
                for p in range(PAIR):
                    pe.wait_ge(hT_ready, batch_of(i, p) * DC)
                    for n in range(TB):
                        for c in range(DC):
                            last = nc.tensor.matmul(qB(p)[n][:], hT[p][:, c, n * P:(n + 1) * P], wqk[:, c, :],
                                                    start=c == 0, stop=c == DC - 1)
                    last.then_inc(qk_raw, 1)
                    pe.wait_ge(x_done, batch_of(i, p))
                    for k in range(DC):
                        for c in range(DC):
                            last = nc.tensor.matmul(vB(p)[:, k * S:(k + 1) * S], wv[:, c, k * P:(k + 1) * P], hT[p][:, c, :],
                                                    start=c == 0, stop=c == DC - 1)
                    last.then_inc(v_raw, 1)
                for p in range(PAIR):
                    pe.wait_ge(qk_ready, batch_of(i, p))
                    for q in range(DC):
                        for n in range(TB):
                            last = nc.tensor.matmul(zB(p)[:, q * D:(q + 1) * D], qk[p][:, n, q * P:(q + 1) * P], qk[p][:, n, D:2 * D],
                                                    start=n == 0, stop=n == TB - 1)
                    last.then_inc(sc_raw, 1)
                for p in range(PAIR):
                    pe.wait_ge(e_ready, batch_of(i, p) * DC)
                    for k in range(DC):
                        for q in range(DC):
                            last = nc.tensor.transpose(qB(p)[0][:, k * D + q * P:k * D + (q + 1) * P],
                                                       e[p][:, q, k * P:(k + 1) * P], t["ident"][:])
                    last.then_inc(eT_raw, 1)
                for p in range(PAIR):
                    pe.wait_ge(eT_ready, batch_of(i, p))
                    pe.wait_ge(v_ready, batch_of(i, p) * DC)
                    for q in range(DC):
                        for k in range(DC):
                            last = nc.tensor.matmul(qB(p)[1][:, q * S:(q + 1) * S], eT[p][:, k, q * P:(q + 1) * P], vT[p][:, k, :],
                                                    start=k == 0, stop=k == DC - 1)
                    last.then_inc(a_raw, 1)
                for p in range(PAIR):
                    pe.wait_ge(a_ready, batch_of(i, p) * DC)
                    for n in range(TB):
                        for q in range(DC):
                            last = nc.tensor.matmul(vB(p)[:, n * D:(n + 1) * D], aT[p][:, q, n * P:(n + 1) * P], wproj[:, q, :],
                                                    start=q == 0, stop=q == DC - 1)
                    last.then_inc(o_raw, 1)

        @block.vector
        def _(dve):
            one = Chain(dve, v_steps, ONCE)
            one.did(nc.vector.tensor_tensor(var2[:], t["var"][:], t["rstd"][:], ALU.mult)); one.see()
            one.did(nc.vector.tensor_tensor(var2[:], var2[:], t["rstd"][:], ALU.mult))
            dve.wait_ge(root, 1)
            one.did(nc.vector.reciprocal(r2[:], r2[:])); one.see()
            one.did(nc.vector.tensor_tensor(r12[:], r2[:], t["rstd"][:], ALU.mult))
            one.did(nc.vector.tensor_scalar(gain[:], t["rstd"][:], 1.0, None, ALU.add))
            one.did(nc.vector.tensor_tensor(shift[:], t["mean"][:], t["rstd"][:], ALU.mult)); one.see()
            one.did(nc.vector.tensor_scalar(shift[:], shift[:], -1.0, None, ALU.mult)); one.see()
            one.end()
            nc.vector.sem_inc(x_done, PAIR)
            dve.wait_ge(w_in, 96)
            with dve.Fori(0, TRIPS) as i:
                ch = Chain(dve, v_steps, PER, i, ONCE)
                for p in range(PAIR):
                    tile = (i * PAIR + p) * TB
                    for c in range(TB):
                        nc.vector.tensor_scalar(z[p][:, c, :], t["X"][:, bass.ds(tile + c, 1), :].rearrange("p o d -> p (o d)"),
                                                t["mean"][:, bass.ds(tile + c, 1)], r12[:, bass.ds(tile + c, 1)],
                                                ALU.subtract, ALU.mult).then_inc(z_ready, 1)
                        nc.vector.tensor_scalar(res[p][:, c, :], t["X"][:, bass.ds(tile + c, 1), :].rearrange("p o d -> p (o d)"),
                                                gain[:, bass.ds(tile + c, 1)], shift[:, bass.ds(tile + c, 1)],
                                                ALU.mult, ALU.add).then_inc(res_scaled, 1)
                for p in range(PAIR):
                    dve.wait_ge(qk_raw, batch_of(i, p))
                    for n in range(TB):
                        last = nc.vector.tensor_tensor(qk[p][:, n, :], qB(p)[n][:], bqk[:], ALU.add)
                    last.then_inc(qk_ready, 1)
                for p in range(PAIR):
                    dve.wait_ge(sc_raw, batch_of(i, p))
                    ch.did(nc.vector.tensor_reduce(top[:, p, :], zB(p)[:].rearrange("p (c k) -> p c k", c=DC), AX.X, ALU.max)); ch.see()
                    nc.vector.tensor_scalar(ntop[:, p, :], top[:, p, :], -1.0 / 16, None, ALU.mult).then_inc(ntop_ready, 1)
                for p in range(PAIR):
                    dve.wait_ge(e_ready, batch_of(i, p) * DC)
                    nc.vector.reciprocal(rsum[:, p, :], esum[:, p, :]).then_inc(rsum_ready, 1)
                    dve.wait_ge(eT_raw, batch_of(i, p))
                    nc.vector.tensor_copy(eT[p][:], qB(p)[0][:].rearrange("p (c k) -> p c k", c=DC)).then_inc(eT_ready, 1)
                for p in range(PAIR):
                    tile = (i * PAIR + p) * TB
                    dve.wait_ge(o_raw, batch_of(i, p))
                    dve.wait_ge(res_ready, batch_of(i, p))
                    nc.vector.tensor_tensor(t["X"][:, bass.ds(tile, TB), :], vB(p)[:].rearrange("p (c k) -> p c k", c=TB),
                                            res[p][:], ALU.add).then_inc(x_done, 1)
                    dve.wait_ge(x_done, batch_of(i, p) + PAIR)
                    update_stats(nc, t, tile, took_wait)
                ch.end()


LANES4 = 4
GROUPS = B // LANES4
HEADS = 8
HD = D // HEADS
CAP = 15.0


def lane_count(g, j):
    return g * LANES4 + (j + 1)


def mlstm_gates(nc, t, d, bank, s):
    ctx = ExitStack()
    with ctx:
        sem = signals(nc, ctx, "g_")
        sb = lambda n, shape, dt=FP: ctx.enter_context(nc.sbuf_tensor("g_" + n, shape, dt))
        LANES = range(LANES4)
        gw = sb("gw", [P, 6, 2, 32])
        gc = sb("gc", [P, DC, 2, 32])
        z = [sb(f"z{j}", [P, TB, D]) for j in LANES]
        qT = [sb(f"qT{j}", [P, DC, S]) for j in LANES]
        cT = [sb(f"cT{j}", [P, DC, S]) for j in LANES]
        w_in, gc_ready, z_ready, zT_raw, qT_ready, pre_raw, pre_ready = (sem(n) for n in ("w_in", "gc", "z", "zT", "qT", "pre_raw", "pre"))
        c_in = [sem(f"c_in{j}") for j in LANES]
        T, G = (lambda j: bank[4 + j]), bank[0]
        halves = lambda b: b[:].rearrange("p (c s) -> p c s", c=DC)
        block = ctx.enter_context(nc.Block())

        @block.sync
        def _(sp):
            sp.dma_start(gw[:], d["gw"]).then_inc(w_in, 16)
            with sp.Fori(0, GROUPS) as g:
                for j in LANES:
                    sp.wait_ge(pre_raw, g + 1)
                    sp.dma_start(cT[j][:], d["ctxT"][bass.ds(g * LANES4 + j, 1)].rearrange("o p c s -> p (o c) s")).then_inc(c_in[j], 16)

        @block.vector
        def _(dve):
            dve.wait_ge(w_in, 16)
            nc.vector.tensor_tensor(gc[:], gw[:, 2:4], gw[:, 4:6], ALU.add).then_inc(gc_ready, 1)
            nc.vector.sem_inc(pre_ready, 1)
            with dve.Fori(0, GROUPS) as g:
                for j in LANES:
                    tile = (g * LANES4 + j) * TB
                    for c in range(TB):
                        nc.vector.tensor_scalar(z[j][:, c, :], t["X"][:, bass.ds(tile + c, 1), :].rearrange("p o d -> p (o d)"),
                                                t["mean"][:, bass.ds(tile + c, 1)], t["rstd"][:, bass.ds(tile + c, 1)],
                                                ALU.subtract, ALU.mult).then_inc(z_ready, 1)
                dve.wait_ge(pre_raw, g + 2)
                nc.vector.tensor_copy(s["pre"][:, :, bass.ds(g, 1), :].rearrange("p a o s -> p a (o s)"),
                                      G[:].rearrange("p (a s) -> p a s", a=2)).then_inc(pre_ready, 1)

        @block.tensor
        def _(pe):
            pe.wait_ge(gc_ready, 1)
            nc.tensor.sem_inc(pre_raw, 1)
            with pe.Fori(0, GROUPS) as g:
                for j in LANES:
                    pe.wait_ge(z_ready, lane_count(g, j) * TB)
                    for c in range(DC):
                        for n in range(TB):
                            last = nc.tensor.transpose(T(j)[:, c * S + n * P:c * S + (n + 1) * P],
                                                       z[j][:, n, c * P:(c + 1) * P], t["ident"][:])
                    last.then_inc(zT_raw, 1)
                pe.wait_ge(pre_ready, g + 1)
                for j in LANES:
                    pe.wait_ge(qT_ready, lane_count(g, j))
                    pe.wait_ge(c_in[j], (g + 1) * 16)
                    for a in range(2):
                        out = G[32 * j:32 * j + 32, a * S:(a + 1) * S]
                        for c in range(DC):
                            nc.tensor.matmul(out, gw[:, c, a, :], qT[j][:, c, :], start=c == 0, stop=False)
                        for c in range(DC):
                            last = nc.tensor.matmul(out, gc[:, c, a, :], cT[j][:, c, :], start=False, stop=c == DC - 1)
                last.then_inc(pre_raw, 1)

        @block.scalar
        def _(act):
            with act.Fori(0, GROUPS) as g:
                for j in LANES:
                    act.wait_ge(zT_raw, lane_count(g, j))
                    nc.scalar.activation(qT[j][:], halves(T(j)), ACT.Copy).then_inc(qT_ready, 1)


def mlstm_decays(nc, t, d, s):
    ctx = ExitStack()
    with ctx:
        sem = signals(nc, ctx, "m_")
        sb = lambda n, shape, dt=FP: ctx.enter_context(nc.sbuf_tensor("m_" + n, shape, dt))
        bias, rows_ = sb("bias", [P, 2]), s["rows"]
        keep, penalty = sb("keep", [P, GROUPS, S]), sb("penalty", [P, GROUPS, S])
        cum = sb("cum", [P, GROUPS, S])
        pre, g, top, m = s["pre"], s["g"], s["top"], s["m"]
        flat = lambda a: a.rearrange("p g s -> p (g s)")
        c_in, steps, tanh_done, exp_done, ln_done = (sem(n) for n in ("c_in", "steps", "tanh", "exp", "ln"))
        block = ctx.enter_context(nc.Block())

        @block.sync
        def _(sp):
            sp.dma_start(bias[:], d["gbias"]).then_inc(c_in, 16)
            sp.dma_start(rows_[:], d["grows"]).then_inc(c_in, 16)

        @block.scalar
        def _(act):
            act.wait_ge(steps, 1)
            for a in range(2):
                nc.scalar.activation(flat(pre[:, a]), flat(pre[:, a]), ACT.Tanh, bias=bias[:, a:a + 1], scale=1.0 / CAP).then_inc(tanh_done, 1)
            act.wait_ge(tanh_done, 2)
            nc.scalar.preload_act_table_set("natural_log_exp_and_others")
            nc.scalar.activation(flat(pre[:, 1]), flat(pre[:, 1]), ACT.Exp, scale=-CAP).then_inc(exp_done, 1)
            act.wait_ge(exp_done, 1)
            nc.scalar.activation(flat(pre[:, 1]), flat(pre[:, 1]), ACT.Ln, bias=1.0).then_inc(ln_done, 1)

        @block.vector
        def _(dve):
            ch = Chain(dve, steps, 11)
            dve.wait_ge(c_in, 32)
            ch.did(nc.vector.tensor_scalar(bias[:], bias[:], 1.0 / CAP, None, ALU.mult)).see()
            ch.did(nc.vector.memset(keep[:], 1.0))
            ch.did(nc.vector.memset(penalty[:], 0.0)).see()
            ch.did(nc.vector.memset(keep[:, :, 0:1], 0.0))
            ch.did(nc.vector.memset(penalty[:, :, 0:1], -1e30)).see()
            dve.wait_ge(ln_done, 1)
            ch.did(nc.vector.tensor_tensor_scan(flat(cum[:]), flat(keep[:]), flat(pre[:, 1]), 0.0, ALU.mult, ALU.subtract)).see()
            ch.did(nc.vector.scalar_tensor_tensor(flat(top[:]), flat(pre[:, 0]), CAP, flat(cum[:]), ALU.mult, ALU.subtract)).see()
            ch.did(nc.vector.tensor_scalar(flat(g[:]), flat(top[:]), rows_[:, 0:1], rows_[:, 1:2], ALU.mult, ALU.add))
            ch.did(nc.vector.tensor_tensor_scan(flat(m[:]), flat(penalty[:]), flat(top[:]), 0.0, ALU.add, ALU.max)).see()
            ch.did(nc.vector.tensor_copy(flat(top[:]), flat(m[:]))).see()
            ch.did(nc.vector.tensor_tensor(flat(m[:]), flat(m[:]), flat(cum[:]), ALU.add)).see()
            ch.end()


def layer0_mlstm(nc, t, d, bank):
    ctx = ExitStack()
    with ctx:
        sb = lambda n, shape, dt=FP: ctx.enter_context(nc.sbuf_tensor("b_" + n, shape, dt))
        s = {"g": sb("g", [P, GROUPS, S]), "top": sb("top", [P, GROUPS, S]), "m": sb("m", [P, GROUPS, S]),
             "rows": sb("rows", [P, 2 + 2 * HEADS])}
        with nc.sbuf_tensor("b_pre", [P, 2, GROUPS, S], FP) as pre:
            s["pre"] = pre
            mlstm_gates(nc, t, d, bank, s)
            mlstm_decays(nc, t, d, s)
        mlstm_heads(nc, t, d, bank, s)


def mlstm_heads(nc, t, d, bank, s):
    ctx = ExitStack()
    with ctx:
        sem = signals(nc, ctx, "b_")
        sb = lambda n, shape, dt=FP: ctx.enter_context(nc.sbuf_tensor("b_" + n, shape, dt))
        LANES, JOBS, LAG, RING = range(LANES4), LANES4 * HEADS, 2, 4
        VW = HD + 1
        COLS = 3 * P
        gain = sb("gain", [P, D])
        gm, lg, right = sb("gm", [P, S]), sb("lg", [P, S]), sb("right", [P, HEADS, S])
        em = sb("em", [P, TB, LANES4, HEADS])
        tiny = sb("tiny", [P, 1])
        z = [sb(f"z{k}", [P, TB, D]) for k in range(2)]
        qT = [sb(f"qT{k}", [P, DC, S]) for k in range(2)]
        cT = [sb(f"cT{k}", [P, DC, S]) for k in range(2)]
        cn = [sb(f"cn{k}", [P, TB, D]) for k in range(2)]
        v = [sb(f"v{k}", [P, TB, HEADS, VW]) for k in range(2)]
        decay = [sb(f"decay{k}", [P, COLS]) for k in range(RING)]
        sm = [sb(f"sm{k}", [P, COLS]) for k in range(RING)]
        o = [sb(f"o{k}", [P, TB, HEADS, VW]) for k in range(2)]
        sq, y = sb("sq", [P, TB, HEADS, HD]), sb("y", [P, TB, HEADS, HD])
        small = [sb(f"small{k}", [P, TB, HEADS]) for k in range(6)]
        ss, den, rden, rden2, rms, scale = small
        names = ("w_in", "setup", "group", "mT_raw", "em", "z", "zT_raw", "qT", "v", "pv", "o_read", "o", "sq", "q_in", "rms_ln", "rms",
                 "scale", "y0", "y", "x_done", "took_wait", "steps", "sc", "dd", "decay", "sm", "c_used", "took_pool_wait")
        (w_in, setup, group, mT_raw, em_ready, z_ready, zT_raw, qT_ready, v_ready, pv_done, o_read, o_ready, sq_ready, q_in, rms_ln, rms_ready,
         scale_ready, y0_ready, y_ready, x_done, took_wait, steps, sc_raw, dd_raw, decay_ready, sm_ready, c_used, took_pool_wait) = (sem(n) for n in names)
        c_in = [sem(f"c_in{k}") for k in range(2)]
        SC, DD, O, T, MT = (bank[0], bank[1]), (bank[2], bank[3]), (bank[4], bank[5]), bank[6], bank[7]
        halves = lambda b: b[:].rearrange("p (c s) -> p c s", c=DC)
        SETUP, GROUP_OPS = 4, 2 + HEADS
        PER = 6 * LANES4
        block = ctx.enter_context(nc.Block())

        @block.sync
        def _(sp):
            sp.dma_start(gain[:], d["outnorm"]).then_inc(w_in, 16)
            with sp.Fori(0, GROUPS) as g:
                for j in LANES:
                    k = j % 2
                    sp.wait_ge(c_used, lane_count(g, j))
                    b = bass.ds(g * LANES4 + j, 1)
                    sp.dma_start(cT[k][:], d["ctxT"][b].rearrange("o p c s -> p (o c) s")).then_inc(c_in[k], 16)
                    sp.dma_start(cn[k][:], d["ctx"][b].rearrange("o p n d -> p (o n) d")).then_inc(c_in[k], 16)

        def arrived(g, j):
            return g * 64 + (j // 2 + 1) * 32

        @block.gpsimd
        def _(pool):
            for k in range(2):
                nc.gpsimd.memset(v[k][:], 1.0).then_inc(setup, 1)
            nc.gpsimd.memset(tiny[:], 1e-6).then_inc(setup, 1)
            pool.wait_ge(setup, 3)
            pool.wait_ge(w_in, 16)
            nc.gpsimd.tensor_scalar(gain[:], gain[:], 1.0, None, ALU.add).then_inc(setup, 1)
            pool.wait_ge(setup, SETUP)

            def values(g, j):
                pool.wait_ge(c_in[j % 2], arrived(g, j))
                nc.gpsimd.sem_inc(took_pool_wait, 1)
                nc.gpsimd.tensor_copy(v[j % 2][:, :, :, 0:HD], cn[j % 2][:].rearrange("p n (h e) -> p n h e", h=HEADS)).then_inc(v_ready, 1)

            def norm(g, j):
                pool.wait_ge(o_ready, lane_count(g, j) + 1)
                ov = o[j % 2][:, :, :, 0:HD]
                nc.gpsimd.tensor_tensor(sq[:], ov, ov, ALU.mult).then_inc(sq_ready, 1)
                pool.wait_ge(scale_ready, lane_count(g, j))
                nc.gpsimd.tensor_tensor(y[:], ov, scale[:, :, :, None].to_broadcast([P, TB, HEADS, HD]), ALU.mult).then_inc(y0_ready, 1)
                pool.wait_ge(y0_ready, lane_count(g, j))
                nc.gpsimd.tensor_tensor(y[:].rearrange("p n h e -> p n (h e)"), y[:].rearrange("p n h e -> p n (h e)"),
                                        gain[:, None, :].to_broadcast([P, TB, D]), ALU.mult).then_inc(y_ready, 1)

            with pool.Fori(0, GROUPS) as g:
                for n in range(JOBS + LAG):
                    if n % HEADS == 0 and n < JOBS:
                        values(g, n // HEADS)
                    if n % HEADS == LAG and n > HEADS:
                        norm(g, n // HEADS - 1)
                norm(g, LANES4 - 1) if (JOBS + LAG - 1) % HEADS < LAG else None

        @block.scalar
        def _(act):
            act.wait_ge(setup, 3)
            act.preload_act_table_set("natural_log_exp_and_others")
            act.sem_inc(o_ready, 1)

            def queries(g, j):
                act.wait_ge(zT_raw, lane_count(g, j))
                nc.scalar.activation(qT[j % 2][:], halves(T), ACT.Copy).then_inc(qT_ready, 1)

            def rms_root(g, j):
                act.wait_ge(q_in, lane_count(g, j))
                nc.scalar.activation(rms[:], rms[:], ACT.Ln, scale=1.0 / HD, bias=tiny[:]).then_inc(rms_ln, 1)
                act.wait_ge(rms_ln, lane_count(g, j))
                nc.scalar.activation(rms[:], rms[:], ACT.Exp, scale=-0.5).then_inc(rms_ready, 1)

            with act.Fori(0, GROUPS) as g:
                act.wait_ge(mT_raw, g + 1)
                nc.scalar.activation(em[:], MT[:, 0:TB * P].rearrange("p (n j r) -> p n j r", n=TB, j=LANES4)[:, :, :, 0:HEADS],
                                     ACT.Exp, scale=-1.0).then_inc(em_ready, 1)
                queries(g, 0)
                for n in range(JOBS + LAG):
                    if n < JOBS:
                        act.wait_ge(dd_raw, g * JOBS + (n + 1))
                        if n >= RING:
                            act.wait_ge(sm_ready, g * JOBS + (n - RING + 1))
                        nc.scalar.activation(decay[n % RING][:], DD[n % 2][:, 0:COLS], ACT.Exp).then_inc(decay_ready, 1)
                    if n % HEADS == 4 and n // HEADS + 1 < LANES4:
                        queries(g, n // HEADS + 1)
                    if n % HEADS == LAG - 1 and n >= HEADS:
                        j = n // HEADS - 1
                        act.wait_ge(pv_done, lane_count(g, j))
                        for b in range(TB):
                            last = nc.scalar.activation(o[j % 2][:, b].rearrange("p h e -> p (h e)"), O[b][:, 0:HEADS * VW], ACT.Copy)
                        last.then_inc(o_ready, 1)
                    if n % HEADS == 5 and n > HEADS:
                        rms_root(g, n // HEADS - 1)
                rms_root(g, LANES4 - 1)

        @block.tensor
        def _(pe):
            def transpose_z(g, j):
                pe.wait_ge(z_ready, lane_count(g, j) * TB)
                if j:
                    pe.wait_ge(qT_ready, lane_count(g, j) - 1)
                for c in range(DC):
                    for n in range(TB):
                        last = nc.tensor.transpose(T[:, c * S + n * P:c * S + (n + 1) * P],
                                                   z[j % 2][:, n, c * P:(c + 1) * P], t["ident"][:])
                last.then_inc(zT_raw, 1)

            with pe.Fori(0, GROUPS) as g:
                pe.wait_ge(group, (g + 1) * GROUP_OPS)
                for n in range(TB):
                    last = nc.tensor.transpose(MT[:, n * P:(n + 1) * P], gm[:, n * P:(n + 1) * P], t["ident"][:])
                last.then_inc(mT_raw, 1)
                transpose_z(g, 0)
                for n in range(JOBS + LAG):
                    if n < JOBS:
                        j, h = n // HEADS, n % HEADS
                        k, c, r = j % 2, h // 4, 32 * (h % 4)
                        if h == 0:
                            pe.wait_ge(c_in[k], arrived(g, j))
                            pe.wait_ge(qT_ready, lane_count(g, j))
                        if n >= 2:
                            pe.wait_ge(sm_ready, g * JOBS + (n - 1))
                        rows_ = slice(r, r + 32)
                        out = SC[n % 2]
                        nc.tensor.matmul(out[:, 0:S], cT[k][rows_, c, 0:P], qT[k][rows_, c, :], start=True, stop=True)
                        nc.tensor.matmul(out[:, S:COLS], cT[k][rows_, c, P:S], qT[k][rows_, c, P:S], start=True, stop=True).then_inc(sc_raw, 1)
                        if n >= 2:
                            pe.wait_ge(decay_ready, g * JOBS + (n - 1))
                        out, lane = DD[n % 2], slice(32 * j, 32 * j + 32)
                        nc.tensor.matmul(out[:, 0:COLS], t["identb"][:], t["maskneg"][:], start=True, stop=False)
                        nc.tensor.matmul(out[:, 0:S], lg[lane, 0:P], right[lane, h, :], start=False, stop=False)
                        nc.tensor.matmul(out[:, S:COLS], lg[lane, P:S], right[lane, h, P:S], start=False, stop=True).then_inc(dd_raw, 1)
                        if n % HEADS == 3 and j + 1 < LANES4:
                            transpose_z(g, j + 1)
                    if n >= LAG:
                        q = n - LAG
                        j, h = q // HEADS, q % HEADS
                        k = j % 2
                        if h == 0:
                            pe.wait_ge(v_ready, lane_count(g, j))
                            pe.wait_ge(o_ready, lane_count(g, j))
                        pe.wait_ge(sm_ready, g * JOBS + (q + 1))
                        m, w = sm[q % RING], slice(h * VW, (h + 1) * VW)
                        nc.tensor.matmul(O[0][:, w], m[:, 0:P], v[k][:, 0, h, :], start=True, stop=True)
                        nc.tensor.matmul(O[1][:, w], m[:, P:S], v[k][:, 0, h, :], start=True, stop=False)
                        last = nc.tensor.matmul(O[1][:, w], m[:, S:COLS], v[k][:, 1, h, :], start=False, stop=True)
                        if h == HEADS - 1:
                            last.then_inc(pv_done, 1)

        @block.vector
        def _(dve):
            nc.vector.sem_inc(c_used, 2)
            dve.wait_ge(w_in, 16)

            def queries(g, j):
                tile = (g * LANES4 + j) * TB
                for c in range(TB):
                    nc.vector.tensor_scalar(z[j % 2][:, c, :], t["X"][:, bass.ds(tile + c, 1), :].rearrange("p o d -> p (o d)"),
                                            t["mean"][:, bass.ds(tile + c, 1)], t["rstd"][:, bass.ds(tile + c, 1)],
                                            ALU.subtract, ALU.mult).then_inc(z_ready, 1)

            def norm(g, j, ch):
                dve.wait_ge(o_ready, lane_count(g, j) + 1)
                nc.vector.sem_inc(c_used, 1)
                ch.did(nc.vector.tensor_tensor(den[:], o[j % 2][:, :, :, HD], em[:, :, j, :], ALU.max)).see()
                ch.did(nc.vector.scalar_tensor_tensor(den[:], o[j % 2][:, :, :, HD], -1.0, den[:], ALU.mult, ALU.max)).see()
                ch.did(nc.vector.tensor_scalar(den[:], den[:], 5e-5, None, ALU.add)).see()
                ch.did(nc.vector.reciprocal(rden[:], den[:])).see()
                dve.wait_ge(sq_ready, lane_count(g, j))
                ch.did(nc.vector.tensor_reduce(ss[:], sq[:], AX.X, ALU.add))
                ch.did(nc.vector.tensor_tensor(rden2[:], rden[:], rden[:], ALU.mult)).see()
                nc.vector.tensor_tensor(rms[:], ss[:], rden2[:], ALU.mult).then_inc(q_in, 1)

            def finish(g, j):
                dve.wait_ge(rms_ready, lane_count(g, j))
                nc.vector.tensor_tensor(scale[:], rms[:], rden[:], ALU.mult).then_inc(scale_ready, 1)

            def add(g, j):
                tile = (g * LANES4 + j) * TB
                x = t["X"][:, bass.ds(tile, TB), :]
                dve.wait_ge(y_ready, lane_count(g, j))
                nc.vector.tensor_tensor(x, y[:].rearrange("p n h e -> p n (h e)"), x, ALU.add).then_inc(x_done, 1)
                dve.wait_ge(x_done, lane_count(g, j))
                update_stats(nc, t, tile, took_wait)

            with dve.Fori(0, GROUPS) as g:
                ch = Chain(dve, steps, PER, g)
                col = lambda name: s[name][:, bass.ds(g, 1), :].rearrange("p o s -> p (o s)")
                nc.vector.tensor_copy(gm[:], col("m")).then_inc(group, 1)
                nc.vector.tensor_copy(lg[:], col("g")).then_inc(group, 1)
                for h in range(HEADS):
                    nc.vector.tensor_scalar(right[:, h, :], col("top"), s["rows"][:, 2 + h:3 + h], s["rows"][:, 2 + HEADS + h:3 + HEADS + h],
                                            ALU.mult, ALU.add).then_inc(group, 1)
                queries(g, 0)
                for n in range(JOBS + LAG):
                    if n < JOBS:
                        dve.wait_ge(sc_raw, g * JOBS + (n + 1))
                        dve.wait_ge(decay_ready, g * JOBS + (n + 1))
                        nc.vector.scalar_tensor_tensor(sm[n % RING][:], SC[n % 2][:, 0:COLS], float(HD) ** -0.5, decay[n % RING][:],
                                                       ALU.mult, ALU.mult).then_inc(sm_ready, 1)
                    if n % HEADS == 2 and n // HEADS + 1 < LANES4 and n < JOBS:
                        queries(g, n // HEADS + 1)
                    j = n // HEADS - 1
                    if n >= HEADS and n < JOBS and n % HEADS == 3:
                        norm(g, j, ch)
                    if n >= HEADS and n < JOBS and n % HEADS == 5:
                        finish(g, j)
                    if n >= HEADS and n < JOBS and n % HEADS == 7:
                        add(g, j)
                norm(g, LANES4 - 1, ch)
                finish(g, LANES4 - 1)
                add(g, LANES4 - 1)
                ch.end()


EX, EF = 8, 512
EFC = EF // P


def layer0_experts(nc, t, d, bank):
    ctx = ExitStack()
    with ctx:
        sem = signals(nc, ctx, "c_")
        sb = lambda n, shape, dt=FP: ctx.enter_context(nc.sbuf_tensor("c_" + n, shape, dt))
        LANES = range(PAIR)
        TT, WIDE = PAIR * TB, PAIR * S
        w1, w2 = sb("w1", [P, EX, DC, EF]), sb("w2", [P, EX, EFC, D])
        b1, b2, router = sb("b1", [P, EX, EFC]), sb("b2", [EX, D]), sb("router", [P, DC, EX])
        z, zT = sb("z", [P, TT, D]), sb("zT", [P, DC, WIDE])
        lg, best = sb("lg", [P, TT, EX]), sb("best", [P, TT, EX])
        place = sb("place", [P, TT, EX], mybir.dt.uint32)
        placef, gap, prob = sb("placef", [P, TT, 2]), sb("gap", [P, TT]), sb("prob", [P, TT, 2])
        number = sb("number", [P, EX])
        mine, comb = sb("mine", [P, TT, EX]), sb("comb", [P, TT, EX])
        combT = sb("combT", [EX, WIDE])
        h = [sb(f"h{k}", [P, EFC, WIDE]) for k in range(2)]
        acc = sb("acc", [P, TT, D])
        names = ("w_in", "z", "zT_raw", "zT", "lg_raw", "steps", "gap", "prob", "comb", "cT_raw", "cT", "h_raw", "h_read", "h", "y_raw", "y_read", "acc", "x_done", "took_wait", "b2_raw", "asteps")
        (w_in, z_ready, zT_raw, zT_ready, lg_raw, steps, gap_ready, prob_ready, comb_ready, cT_raw, cT_ready, h_raw, h_read, h_ready, y_raw, y_read, acc_done,
         x_done, took_wait, b2_raw, asteps) = (sem(n) for n in names)
        H = bank[0:4]
        Y = (bank[4:6], bank[6:8])
        block = ctx.enter_context(nc.Block())
        W_LOADS, PER = 6, 5 + 4 * TT + EX * (TT - 1)
        LOADS = ((w1, "cw1"), (w2, "cw2"), (b1, "cb1"), (b2, "cb2"), (router, "crouter"), (number, "cnumber"))

        @block.sync
        def _(sp):
            for dst, src in LOADS:
                sp.dma_start(dst[:], d[src]).then_inc(w_in, 16)

        @block.scalar
        def _(act):
            act.wait_ge(w_in, 16 * W_LOADS)
            with act.Fori(0, TRIPS) as i:
                for c in range(DC):
                    act.wait_ge(zT_raw, i * DC + (c + 1))
                    nc.scalar.activation(zT[:, c, :], H[c][:], ACT.Copy).then_inc(zT_ready, 1)
                act.wait_ge(gap_ready, i + 1)
                nc.scalar.activation(prob[:, :, 0], gap[:], ACT.Exp).then_inc(prob_ready, 1)
                for e in range(EX):
                    act.wait_ge(y_raw, i * (EX * 2) + (2 * max(0, e - 1) + 1))
                    for f in range(EFC):
                        act.wait_ge(h_raw, i * (EX * EFC) + (e * EFC + f + 1))
                        nc.scalar.activation(h[e % 2][:, f, :], H[f][:], ACT.Gelu, bias=b1[:, e, f:f + 1]).then_inc(h_ready, 1)

        @block.tensor
        def _(pe):
            pe.wait_ge(w_in, 16 * W_LOADS)
            nc.tensor.sem_inc(y_raw, 1)
            with pe.Fori(0, TRIPS) as i:
                pe.wait_ge(z_ready, (i + 1) * TT)
                for c in range(DC):
                    for n in range(TT):
                        last = nc.tensor.transpose(H[c][:, n * P:(n + 1) * P], z[:, n, c * P:(c + 1) * P], t["ident"][:])
                    last.then_inc(zT_raw, 1)
                pe.wait_ge(zT_ready, (i + 1) * DC)
                for n in range(TT):
                    for c in range(DC):
                        last = nc.tensor.matmul(H[2][:, n * EX:(n + 1) * EX], zT[:, c, n * P:(n + 1) * P], router[:, c, :], start=c == 0, stop=c == DC - 1)
                last.then_inc(lg_raw, 1)
                pe.wait_ge(comb_ready, i + 1)
                for n in range(TT):
                    last = nc.tensor.transpose(H[3][0:EX, n * P:(n + 1) * P], comb[:, n, :], t["ident"][:])
                last.then_inc(cT_raw, 1)
                pe.wait_ge(cT_ready, i + 1)
                for n in range(TT):
                    last = nc.tensor.matmul(Y[1][n // 2][:, (n % 2) * D:(n % 2 + 1) * D], combT[:, n * P:(n + 1) * P], b2[:], start=True, stop=True)
                last.then_inc(b2_raw, 1)

                def up(e):
                    for f in range(EFC):
                        pe.wait_ge(h_ready, i * (EX * EFC) + max(0, (e - 1) * EFC + f + 1)) if e else None
                        for c in range(DC):
                            last = nc.tensor.matmul(H[f][:], w1[:, e, c, f * P:(f + 1) * P], zT[:, c, :], start=c == 0, stop=c == DC - 1)
                        last.then_inc(h_raw, 1)

                def down(e):
                    pe.wait_ge(h_ready, i * (EX * EFC) + (e + 1) * EFC)
                    pe.wait_ge(y_read, i * (EX + 1) + (max(0, e) + 1))
                    for n in range(TT):
                        for f in range(EFC):
                            last = nc.tensor.matmul(Y[e % 2][n // 2][:, (n % 2) * D:(n % 2 + 1) * D], h[e % 2][:, f, n * P:(n + 1) * P], w2[:, e, f, :],
                                                    start=f == 0, stop=f == EFC - 1)
                        if n % 2:
                            last.then_inc(y_raw, 1)

                up(0)
                for e in range(1, EX):
                    up(e)
                    down(e - 1)
                down(EX - 1)

        @block.vector
        def _(dve):
            dve.wait_ge(w_in, 16 * W_LOADS)
            nc.vector.sem_inc(y_read, 1)
            with dve.Fori(0, TRIPS) as i:
                ch = Chain(dve, steps, PER, i)
                for n in range(TT):
                    tile = i * TT + n
                    nc.vector.tensor_scalar(z[:, n, :], t["X"][:, bass.ds(tile, 1), :].rearrange("p o d -> p (o d)"),
                                            t["mean"][:, bass.ds(tile, 1)], t["rstd"][:, bass.ds(tile, 1)],
                                            ALU.subtract, ALU.mult).then_inc(z_ready, 1)
                dve.wait_ge(lg_raw, i + 1)
                ch.did(nc.vector.tensor_copy(lg[:], H[2][:, 0:TT * EX].rearrange("p (n e) -> p n e", n=TT))).see()
                nc.vector.sem_inc(took_wait, 1)
                for n in range(TT):
                    ch.did(nc.vector.max(best[:, n, :], lg[:, n, :]))
                ch.see()
                nc.vector.sem_inc(took_wait, 1)
                for n in range(TT):
                    ch.did(nc.vector.max_index(place[:, n, :], best[:, n, :], lg[:, n, :]))
                nc.vector.tensor_tensor(gap[:], best[:, :, 1], best[:, :, 0], ALU.subtract).then_inc(gap_ready, 1)
                ch.see()
                ch.did(nc.vector.tensor_copy(placef[:], place[:, :, 0:2]))
                dve.wait_ge(prob_ready, i + 1)
                ch.did(nc.vector.tensor_scalar(prob[:, :, 1], prob[:, :, 0], 1.0, None, ALU.add)).see()
                ch.did(nc.vector.reciprocal(prob[:, :, 1], prob[:, :, 1])).see()
                ch.did(nc.vector.tensor_tensor(prob[:, :, 0], prob[:, :, 0], prob[:, :, 1], ALU.mult)).see()
                for n in range(TT):
                    ch.did(nc.vector.tensor_scalar(mine[:, n, :], number[:], placef[:, n, 0:1], prob[:, n, 1:2], ALU.is_equal, ALU.mult))
                    ch.did(nc.vector.tensor_scalar(comb[:, n, :], number[:], placef[:, n, 1:2], prob[:, n, 0:1], ALU.is_equal, ALU.mult))
                ch.see()
                nc.vector.tensor_tensor(comb[:], comb[:], mine[:], ALU.add).then_inc(comb_ready, 1)
                dve.wait_ge(cT_raw, i + 1)
                nc.vector.tensor_copy(combT[:], H[3][0:EX, :]).then_inc(cT_ready, 1)
                dve.wait_ge(b2_raw, i + 1)
                for n in range(TT):
                    last = nc.vector.tensor_copy(acc[:, n, :], Y[1][n // 2][:, (n % 2) * D:(n % 2 + 1) * D])
                last.then_inc(y_read, 1)
                dve.wait_ge(y_read, i * (EX + 1) + 2)
                for e in range(EX):
                    for n in range(TT):
                        if n % 2 == 0:
                            dve.wait_ge(y_raw, i * (2 * EX) + (2 * e + n // 2 + 2))
                        last = nc.vector.scalar_tensor_tensor(acc[:, n, :], Y[e % 2][n // 2][:, (n % 2) * D:(n % 2 + 1) * D], comb[:, n, e:e + 1], acc[:, n, :], ALU.mult, ALU.add)
                        if n < TT - 1:
                            ch.did(last)
                    last.then_inc(y_read, 1)
                    dve.wait_ge(y_read, i * (EX + 1) + (e + 3))
                for p in LANES:
                    tile = (i * PAIR + p) * TB
                    x = t["X"][:, bass.ds(tile, TB), :]
                    nc.vector.tensor_tensor(x, acc[:, p * TB:(p + 1) * TB, :], x, ALU.add).then_inc(x_done, 1)
                dve.wait_ge(x_done, (i + 1) * PAIR)
                for p in LANES:
                    update_stats(nc, t, (i * PAIR + p) * TB, took_wait)
                ch.end()


def layer1_rwkv(nc, t, d, bank):
    ctx = ExitStack()
    with ctx:
        sem = signals(nc, ctx, "d_")
        sb = lambda n, shape, dt=FP: ctx.enter_context(nc.sbuf_tensor("d_" + n, shape, dt))
        LANES = range(PAIR)
        w = [sb(f"w{m}", [P, DC, D]) for m in "kvr"]
        wo = sb("wo", [P, DC, D])
        cols = sb("cols", [P, 5, DC])
        decay = sb("decay", [P, DC, S])
        wcol = sb("wcol", [P, DC])
        z = [sb(f"z{p}", [P, TB, D]) for p in LANES]
        zT = [sb(f"zT{p}", [P, DC, S + 1]) for p in LANES]
        diff = [sb(f"diff{p}", [P, DC, S]) for p in LANES]
        mixed = [[sb(f"x{m}{p}", [P, DC, S]) for m in "kvr"] for p in LANES]
        pp = [sb(f"pp{p}", [P, DC, S + 1]) for p in LANES]
        aa = [sb(f"aa{p}", [P, DC, S + 1]) for p in LANES]
        bb = [sb(f"bb{p}", [P, DC, S + 1]) for p in LANES]
        top = [sb(f"top{p}", [P, DC, S]) for p in LANES]
        ex = [sb(f"ex{p}", [P, 4, DC, S]) for p in LANES]
        ev = [sb(f"ev{p}", [P, 2, DC, S]) for p in LANES]
        num = [sb(f"num{p}", [P, DC, S]) for p in LANES]
        den = [sb(f"den{p}", [P, DC, S]) for p in LANES]
        rr = [sb(f"rr{p}", [P, 2, DC, S]) for p in LANES]
        gate = [sb(f"gate{p}", [P, DC, S]) for p in LANES]
        w_in, wexp, setup, took_wait, steps, psteps, asteps = (sem(n) for n in ("w_in", "wexp", "setup", "took_wait", "steps", "psteps", "asteps"))
        z_ready, zT_raw, zT_ready, diff_ready, mixed_ready = (sem(n) for n in ("z", "zT_raw", "zT", "diff", "mixed"))
        kvr_ready, decays_in, decays, firsts_in, firsts = (sem(n) for n in ("kvr", "decays_in", "decays", "firsts_in", "firsts"))
        den_ready, num_ready, soft_ready, lnden_ready, gate_in, gate_ready = (sem(n) for n in ("den", "num", "soft", "lnden", "gate_in", "gate"))
        pool_prev, y_ready, o_raw, x_done = (sem(n) for n in ("pool_prev", "y", "o_raw", "x_done"))
        ev_ready, decay_set = sem("ev"), sem("decay_set")
        K, V, R, O = ((lambda p, j=j: bank[4 * p + j]) for j in range(4))
        halves = lambda b: b[:].rearrange("p (c s) -> p c s", c=DC)
        block = ctx.enter_context(nc.Block())
        ONCE, PER = 1, 8 * PAIR
        PER_POOL = 4 * PAIR
        INIT = 4 * PAIR

        @block.sync
        def _(sp):
            for dst, src in zip(w + [wo, cols], ("dwk", "dwv", "dwr", "dwo", "dcols")):
                sp.dma_start(dst[:], d[src]).then_inc(w_in, 16)

        @block.gpsimd
        def _(pool):
            for p in LANES:
                nc.gpsimd.memset(zT[p][:, :, 0:1], 0.0).then_inc(setup, 1)
                nc.gpsimd.memset(pp[p][:, :, 0:1], -1e30).then_inc(setup, 1)
                nc.gpsimd.memset(aa[p][:, :, 0:1], 0.0).then_inc(setup, 1)
                nc.gpsimd.memset(bb[p][:, :, 0:1], 0.0).then_inc(setup, 1)
            pool.wait_ge(setup, INIT)
            with pool.Fori(0, TRIPS) as i:
                ch = Chain(pool, psteps, PER_POOL, i)
                for p in LANES:
                    pool.wait_ge(zT_ready, batch_of(i, p))
                    nc.gpsimd.tensor_tensor(diff[p][:], zT[p][:, :, 1:S + 1], zT[p][:, :, 0:S], ALU.subtract).then_inc(diff_ready, 1)
                for p in LANES:
                    pool.wait_ge(firsts, batch_of(i, p))
                    pool.wait_ge(ev_ready, batch_of(i, p))
                    ch.did(nc.gpsimd.tensor_tensor(den[p][:], ex[p][:, 2], bb[p][:, :, 0:S], ALU.mult)).see()
                    nc.gpsimd.tensor_tensor(den[p][:], den[p][:], ex[p][:, 3], ALU.add).then_inc(den_ready, 1)
                    ch.did(nc.gpsimd.tensor_tensor(num[p][:], ex[p][:, 2], aa[p][:, :, 0:S], ALU.mult)).see()
                    ch.did(nc.gpsimd.tensor_tensor(num[p][:], num[p][:], ev[p][:, 1], ALU.add))
                    pool.wait_ge(lnden_ready, batch_of(i, p))
                    pool.wait_ge(gate_in, batch_of(i, p))
                    ch.did(nc.gpsimd.tensor_tensor(gate[p][:], gate[p][:], rr[p][:, 1], ALU.subtract)).see()
                    nc.gpsimd.sem_inc(pool_prev, 1)
                ch.end()

        @block.scalar
        def _(act):
            nc.scalar.preload_act_table_set("natural_log_exp_and_others")
            act.wait_ge(w_in, 80)
            nc.scalar.activation(wcol[:], cols[:, 3, :], ACT.Exp).then_inc(wexp, 1)
            with act.Fori(0, TRIPS) as i:
                ch = Chain(act, asteps, 2 * PAIR, i)
                for p in LANES:
                    act.wait_ge(zT_raw, batch_of(i, p))
                    nc.scalar.activation(zT[p][:, :, 1:S + 1], halves(K(p)), ACT.Copy).then_inc(zT_ready, 1)
                for p in LANES:
                    act.wait_ge(kvr_ready, batch_of(i, p))
                    ch.did(nc.scalar.activation(rr[p][:, 0], halves(R(p)), ACT.Abs)).see()
                    ch.did(nc.scalar.activation(rr[p][:, 0], rr[p][:, 0], ACT.Exp, scale=-1.0)).see()
                    nc.scalar.activation(rr[p][:, 0], rr[p][:, 0], ACT.Ln, bias=1.0).then_inc(soft_ready, 1)
                for p in LANES:
                    act.wait_ge(decays_in, batch_of(i, p))
                    nc.scalar.activation(ex[p][:, 0:2], ex[p][:, 0:2], ACT.Exp).then_inc(decays, 1)
                    act.wait_ge(firsts_in, batch_of(i, p))
                    nc.scalar.activation(ex[p][:, 2:4], ex[p][:, 2:4], ACT.Exp).then_inc(firsts, 1)
                for p in LANES:
                    act.wait_ge(den_ready, batch_of(i, p))
                    nc.scalar.activation(rr[p][:, 1], den[p][:], ACT.Ln).then_inc(lnden_ready, 1)
                for p in LANES:
                    act.wait_ge(pool_prev, batch_of(i, p))
                    nc.scalar.activation(gate[p][:], gate[p][:], ACT.Exp).then_inc(gate_ready, 1)
                ch.end()

        @block.tensor
        def _(pe):
            pe.wait_ge(w_in, 80)
            with pe.Fori(0, TRIPS) as i:
                for p in LANES:
                    pe.wait_ge(z_ready, batch_of(i, p) * TB)
                    for c in range(DC):
                        for n in range(TB):
                            last = nc.tensor.transpose(K(p)[:, c * S + n * P:c * S + (n + 1) * P],
                                                       z[p][:, n, c * P:(c + 1) * P], t["ident"][:])
                    last.then_inc(zT_raw, 1)
                for p in LANES:
                    pe.wait_ge(mixed_ready, batch_of(i, p))
                    for m, out in enumerate((K(p), V(p), R(p))):
                        for e in range(DC):
                            for c in range(DC):
                                last = nc.tensor.matmul(out[:, e * S:(e + 1) * S], w[m][:, c, e * P:(e + 1) * P], mixed[p][m][:, c, :],
                                                        start=c == 0, stop=c == DC - 1)
                    last.then_inc(kvr_ready, 1)
                for p in LANES:
                    pe.wait_ge(y_ready, batch_of(i, p))
                    for n in range(TB):
                        for c in range(DC):
                            last = nc.tensor.matmul(O(p)[:, n * D:(n + 1) * D], num[p][:, c, n * P:(n + 1) * P], wo[:, c, :],
                                                    start=c == 0, stop=c == DC - 1)
                    last.then_inc(o_raw, 1)

        @block.vector
        def _(dve):
            dve.wait_ge(wexp, 1)
            nc.vector.memset(decay[:], -1.0).then_inc(steps, 1)
            dve.wait_ge(steps, 1)
            for c in range(DC):
                nc.vector.tensor_scalar(decay[:, c, :], decay[:, c, :], wcol[:, c:c + 1], None, ALU.mult).then_inc(decay_set, 1)
            dve.wait_ge(decay_set, DC)
            dve.wait_ge(setup, INIT)
            dve.wait_ge(w_in, 80)
            with dve.Fori(0, TRIPS) as i:
                ch = Chain(dve, steps, PER, i, ONCE)
                for p in LANES:
                    tile = (i * PAIR + p) * TB
                    for c in range(TB):
                        nc.vector.tensor_scalar(z[p][:, c, :], t["X"][:, bass.ds(tile + c, 1), :].rearrange("p o d -> p (o d)"),
                                                t["mean"][:, bass.ds(tile + c, 1)], t["rstd"][:, bass.ds(tile + c, 1)],
                                                ALU.subtract, ALU.mult).then_inc(z_ready, 1)
                for p in LANES:
                    dve.wait_ge(diff_ready, batch_of(i, p))
                    for m in range(3):
                        for c in range(DC):
                            last = nc.vector.scalar_tensor_tensor(mixed[p][m][:, c, :], diff[p][:, c, :], cols[:, m, c:c + 1],
                                                                  zT[p][:, c, 0:S], ALU.mult, ALU.add)
                    last.then_inc(mixed_ready, 1)
                for p in LANES:
                    k, v, r = halves(K(p)), halves(V(p)), halves(R(p))
                    dve.wait_ge(kvr_ready, batch_of(i, p))
                    for c in range(DC):
                        ch.did(nc.vector.tensor_tensor_scan(pp[p][:, c, 1:S + 1], decay[:, c, :], k[:, c, :], -1e30, ALU.add, ALU.max))
                    ch.see()
                    for c in range(DC):
                        ch.did(nc.vector.scalar_tensor_tensor(top[p][:, c, :], k[:, c, :], cols[:, 4, c:c + 1], pp[p][:, c, 0:S], ALU.add, ALU.max))
                    ch.did(nc.vector.tensor_tensor(ex[p][:, 0], pp[p][:, :, 0:S], decay[:], ALU.add)).see()
                    nc.vector.tensor_tensor(ex[p][:, 1], k, pp[p][:, :, 1:S + 1], ALU.subtract)
                    nc.vector.tensor_tensor(ex[p][:, 0], ex[p][:, 0], pp[p][:, :, 1:S + 1], ALU.subtract).then_inc(decays_in, 1)
                    nc.vector.tensor_tensor(ex[p][:, 2], pp[p][:, :, 0:S], top[p][:], ALU.subtract)
                    for c in range(DC):
                        last = nc.vector.scalar_tensor_tensor(ex[p][:, 3, c, :], k[:, c, :], cols[:, 4, c:c + 1], top[p][:, c, :], ALU.add, ALU.subtract)
                    last.then_inc(firsts_in, 1)
                    dve.wait_ge(soft_ready, batch_of(i, p))
                    nc.vector.scalar_tensor_tensor(gate[p][:], r, 0.0, rr[p][:, 0], ALU.min, ALU.subtract).then_inc(gate_in, 1)
                for p in LANES:
                    v = halves(V(p))
                    dve.wait_ge(decays, batch_of(i, p))
                    ch.did(nc.vector.tensor_tensor(ev[p][:, 0], ex[p][:, 1], v, ALU.mult))
                    for c in range(DC):
                        last = nc.vector.tensor_tensor_scan(bb[p][:, c, 1:S + 1], ex[p][:, 0, c, :], ex[p][:, 1, c, :], 0.0, ALU.mult, ALU.add)
                    ch.see()
                    for c in range(DC):
                        ch.did(nc.vector.tensor_tensor_scan(aa[p][:, c, 1:S + 1], ex[p][:, 0, c, :], ev[p][:, 0, c, :], 0.0, ALU.mult, ALU.add))
                    dve.wait_ge(firsts, batch_of(i, p))
                    nc.vector.tensor_tensor(ev[p][:, 1], ex[p][:, 3], v, ALU.mult).then_inc(ev_ready, 1)
                for p in LANES:
                    dve.wait_ge(gate_ready, batch_of(i, p))
                    nc.vector.tensor_tensor(num[p][:], num[p][:], gate[p][:], ALU.mult).then_inc(y_ready, 1)
                for p in LANES:
                    tile = (i * PAIR + p) * TB
                    x = t["X"][:, bass.ds(tile, TB), :]
                    dve.wait_ge(o_raw, batch_of(i, p))
                    nc.vector.tensor_tensor(x, O(p)[:].rearrange("p (c k) -> p c k", c=TB), x, ALU.add).then_inc(x_done, 1)
                    dve.wait_ge(x_done, batch_of(i, p))
                    update_stats(nc, t, tile, took_wait)
                ch.end()


def layer1_stablemax(nc, t, d, bank):
    ctx = ExitStack()
    with ctx:
        sem = signals(nc, ctx, "e_")
        sb = lambda n, shape, dt=FP: ctx.enter_context(nc.sbuf_tensor("e_" + n, shape, dt))
        XH, QUADS, SLOTS, RING = 16, 4, 6, 4
        XD = D // XH
        SIDES = range(3)
        wq, wk, wv, wo = (sb("w" + m, [P, DC, D]) for m in "qkvo")
        cols = sb("cols", [P, 3, DC])
        mask = sb("mask", [P, 2])
        bo = sb("bo", [P, D])
        bq4, bkm = sb("bq4", [P, DC]), sb("bkm", [P, 2, DC])
        z, zT = sb("z", [P, TB, D]), sb("zT", [P, DC, S])
        cT = [sb(f"cT{k}", [P, DC, S]) for k in SIDES]
        qT = [sb(f"qT{k}", [P, DC, S]) for k in SIDES]
        kT = [sb(f"kT{k}", [P, 2, DC, S]) for k in SIDES]
        vx = [sb(f"vx{k}", [P, TB, XH, 32]) for k in SIDES]
        low = [sb(f"low{k}", [P, TB, S]) for k in range(RING)]
        st = [sb(f"st{k}", [P, QUADS, TB, S]) for k in range(2)]
        u = sb("u", [P, QUADS, S])
        rec = sb("rec", [P, 2, XH])
        cn = sb("cn", [P, TB, D])
        oT = sb("oT", [P, DC, S])
        names = ("w_in", "setup", "z", "zT", "q", "k", "v", "neg", "ln", "low", "st", "u", "rec", "cn", "oT", "bo", "x_done", "took_wait", "took_pool_wait", "consts")
        (w_in, setup, z_ready, zT_ready, q_ready, k_ready, v_ready, neg_ready, ln_ready, low_ready, st_ready, u_ready, rec_ready,
         cn_ready, oT_ready, bo_added, x_done, took_wait, took_pool_wait, consts) = (sem(n) for n in names)
        c_in = [sem(f"c_in{k}") for k in SIDES]
        full = [sem(f"full{k}") for k in range(8)]
        free = [sem(f"free{k}") for k in range(8)]
        halves = lambda b: b[:].rearrange("p (c s) -> p c s", c=DC)
        block = ctx.enter_context(nc.Block())
        W_LOADS, SETUP, CONSTS = 7, 2 * len(SIDES), 3

        EXTRA = {0: (("start_z", 6),), 2: (("pv_before", 7), ("start_q", 6)), 4: (("end_u0", 7), ("end_u1", 6)),
                 6: (("start_k", 7), ("pv0", 6)), 8: (("end_T", 7),), 10: (("end_o", 6), ("pv1", 7)), 12: (("start_v", 6),), 14: (("pv2", 7),)}
        PROLOGUE = (("start_z", 6), ("start_q", 6), ("start_k", 7), ("start_v", 6))
        EPILOGUE = (("pv_before", 7), ("end_u0", 7), ("end_u1", 6), ("end_T", 7), ("end_o", 6))

        class Batch:

            def __init__(self, trip, side):
                self.trip, self.side, self.n = trip, side, trip * 3 + side

            def next(self):
                return Batch(self.trip, self.side + 1) if self.side < 2 else Batch(self.trip + 1, 0)

            def last(self):
                return Batch(self.trip, self.side - 1) if self.side else Batch(self.trip - 1, 2)

            def head(self, k):
                n = XH * self.side + k
                return n % SLOTS, self.trip * (3 * XH // SLOTS) + n // SLOTS

        def steps(before, after):
            uses = {6: 0, 7: 0}
            for k in range(0, XH, 2):
                yield "heads", k, None, None
                for what, b in EXTRA[k]:
                    if what.startswith("start") and not after or (what.startswith("end") or what == "pv_before") and not before:
                        continue
                    yield what, k, b, uses[b]
                    uses[b] += 1

        def whole(engine, body):
            uses = {6: 0, 7: 0}

            def run(batch, list_, base=None):
                for what, k, b, n in list_:
                    body(what, k, batch, b, None if b is None else base[b] + n)

            def alone(batch, list_):
                list_ = list(list_)
                run(batch, list_, dict(uses))
                for _, _, b, n in list_:
                    if b is not None:
                        uses[b] += 1

            def beside(list_):
                seen = {6: 0, 7: 0}
                for what, b in list_:
                    yield what, 0, b, seen[b]
                    seen[b] += 1

            alone(Batch(-1, 2), beside(PROLOGUE))
            alone(Batch(0, 0), steps(False, True))
            with engine.Fori(0, B // 3) as i:
                for h in range(3):
                    run(Batch(i, h + 1) if h < 2 else Batch(i + 1, 0), steps(True, True), {b: uses[b] + (i * 18 + 6 * h) for b in uses})
            for b in uses:
                uses[b] += B // 3 * 18
            last = Batch(B // 3, 1)
            alone(last, steps(True, False))
            alone(last.next(), beside(EPILOGUE))

        @block.sync
        def _(sp):
            for dst, src in ((wq, "ewq"), (wk, "ewk"), (wv, "ewv"), (wo, "ewo"), (cols, "ecols"), (mask, "emask"), (bo, "ebo")):
                sp.dma_start(dst[:], d[src]).then_inc(w_in, 16)
            for k in SIDES:
                sp.dma_start(cT[k][:], d["ctxT"][k]).then_inc(c_in[k], 16)
            with sp.Fori(1, B // 3) as i:
                for k in SIDES:
                    sp.wait_ge(v_ready, 3 * i + (k - 2))
                    sp.dma_start(cT[k][:], d["ctxT"][bass.ds(3 * i + k, 1)].rearrange("o p c s -> p (o c) s")).then_inc(c_in[k], 16)
            for n in range(B // 3 * 3, B):
                sp.wait_ge(v_ready, n - 2)
                sp.dma_start(cT[n % 3][:], d["ctxT"][n]).then_inc(c_in[n % 3], 16)

        @block.gpsimd
        def _(pool):
            for k in SIDES:
                nc.gpsimd.memset(vx[k][:, :, :, XD:32], 0.0).then_inc(setup, 1)
            pool.wait_ge(setup, len(SIDES))
            for k in SIDES:
                nc.gpsimd.memset(vx[k][:, :, :, XD:XD + 1], 1.0).then_inc(setup, 1)
            pool.wait_ge(w_in, 16 * W_LOADS)
            nc.gpsimd.tensor_scalar(bq4[:], cols[:, 0, :], 0.25, None, ALU.mult).then_inc(consts, 1)
            for h in range(2):
                nc.gpsimd.tensor_scalar(bkm[:, h, :], cols[:, 1, :], mask[:, h:h + 1], None, ALU.mult).then_inc(consts, 1)
            with pool.Fori(0, B) as b:
                pool.wait_ge(z_ready, (b + 1) * TB)
                nc.gpsimd.sem_inc(took_pool_wait, 1)
                x = t["X"][:, bass.ds(b * TB, TB), :]
                nc.gpsimd.tensor_tensor(x, x, bo[:, None, :].to_broadcast([P, TB, D]), ALU.add).then_inc(bo_added, 1)

        @block.scalar
        def _(act):
            nc.scalar.preload_act_table_set("natural_log_exp_and_others")
            act.wait_ge(w_in, 16 * W_LOADS)
            act.wait_ge(setup, SETUP)
            act.wait_ge(consts, CONSTS)

            def body(what, k, batch, slot, before):
                b, after, other = batch.n, batch.n + 1, batch.next().side
                here = None if slot is None else bank[slot]
                if what == "heads":
                    for k in (k, k + 1):
                        n = XH * b + (k + 1)
                        act.wait_ge(neg_ready, n)
                        nc.scalar.activation(low[k % RING][:], low[k % RING][:], ACT.Ln, bias=1.0).then_inc(ln_ready, 1)
                        act.wait_ge(ln_ready, n)
                        nc.scalar.activation(low[k % RING][:], low[k % RING][:], ACT.Exp, scale=-1.0).then_inc(low_ready, 1)
                if what != "heads" and what not in ("end_u0", "end_u1", "end_o"):
                    act.wait_ge(full[slot], before + 1)
                if what == "start_z":
                    nc.scalar.activation(zT[:], halves(here), ACT.Copy).then_inc(zT_ready, 1)
                    act.wait_ge(zT_ready, after + 1)
                    act.sem_inc(free[slot], 1)
                if what == "start_q":
                    for c in range(DC):
                        nc.scalar.activation(qT[other][:, c, :], here[:, c * S:(c + 1) * S], ACT.Identity,
                                             bias=bq4[:, c:c + 1], scale=0.25).then_inc(q_ready, 1)
                    act.wait_ge(q_ready, (after + 1) * DC)
                    act.sem_inc(free[slot], 1)
                if what == "start_k":
                    for h in range(2):
                        for c in range(DC):
                            nc.scalar.activation(kT[other][:, h, c, :], here[:, c * S:(c + 1) * S], ACT.Identity,
                                                 bias=bkm[:, h, c:c + 1], scale=mask[:, h:h + 1]).then_inc(k_ready, 1)
                    act.wait_ge(k_ready, (after + 1) * 2 * DC)
                    act.sem_inc(free[slot], 1)
                if what == "start_v":
                    nc.scalar.activation(vx[other][:, :, :, 0:XD], here[:].rearrange("p (n h e) -> p n h e", n=TB, h=XH), ACT.Copy).then_inc(v_ready, 1)
                    act.wait_ge(v_ready, after + 1)
                    act.sem_inc(free[slot], 1)
                if what.startswith("pv"):
                    quad, of = (QUADS - 1, b - 1) if what == "pv_before" else (int(what[2]), b)
                    nc.scalar.activation(u[:, quad, :], here[:, 0:S], ACT.Copy).then_inc(u_ready, 1)
                    act.wait_ge(u_ready, QUADS * of + (quad + 1))
                    act.sem_inc(free[slot], 1)
                if what == "end_T":
                    for c in range(DC):
                        nc.scalar.activation(oT[:, c, :], here[:, c * S:(c + 1) * S], ACT.Identity, bias=cols[:, 2, c:c + 1]).then_inc(oT_ready, 1)
                    act.wait_ge(oT_ready, b * DC)
                    act.sem_inc(free[slot], 1)

            whole(act, body)

        @block.tensor
        def _(pe):
            pe.wait_ge(w_in, 16 * W_LOADS)

            def body(what, k, batch, slot, before):
                b, side, after, other = batch.n, batch.side, batch.n + 1, batch.next().side
                here = None if slot is None else bank[slot]
                if what == "heads":
                    if k == 0:
                        pe.wait_ge(q_ready, (b + 1) * DC)
                        pe.wait_ge(k_ready, (b + 1) * 2 * DC)
                    slots = [batch.head(k + j) for j in range(2)]
                    for s_, n in slots:
                        pe.wait_ge(free[s_], n)
                    for c2 in range(TB):
                        for j in range(2):
                            quad, r = (k + j) // 4, (k + j) % 4
                            c, e, rows_ = quad // 2, quad % 2, slice(32 * r, 32 * r + 32)
                            last = nc.tensor.matmul(bank[slots[j][0]][:, c2 * S:(c2 + 1) * S], kT[side][rows_, e, c, c2 * P:(c2 + 1) * P],
                                                    qT[side][rows_, c, :], start=True, stop=True)
                            if c2 == TB - 1:
                                last.then_inc(full[slots[j][0]], 1)
                if what != "heads":
                    pe.wait_ge(free[slot], before)
                if what == "start_z":
                    pe.wait_ge(z_ready, (after + 1) * TB)
                    for c in range(DC):
                        for n in range(TB):
                            last = nc.tensor.transpose(here[:, c * S + n * P:c * S + (n + 1) * P], z[:, n, c * P:(c + 1) * P], t["ident"][:])
                if what in ("start_q", "start_k"):
                    if what == "start_q":
                        pe.wait_ge(zT_ready, after + 1)
                    else:
                        pe.wait_ge(c_in[other], (batch.next().trip + 1) * 16)
                    w, x = (wq, zT) if what == "start_q" else (wk, cT[other])
                    for e in range(DC):
                        for c in range(DC):
                            last = nc.tensor.matmul(here[:, e * S:(e + 1) * S], w[:, c, e * P:(e + 1) * P], x[:, c, :], start=c == 0, stop=c == DC - 1)
                if what == "start_v":
                    for n in range(TB):
                        for c in range(DC):
                            last = nc.tensor.matmul(here[:, n * D:(n + 1) * D], cT[other][:, c, n * P:(n + 1) * P], wv[:, c, :], start=c == 0, stop=c == DC - 1)
                if what.startswith("pv"):
                    quad, of, s_ = (QUADS - 1, b - 1, batch.last().side) if what == "pv_before" else (int(what[2]), b, side)
                    pe.wait_ge(st_ready, XH * of + 4 * (quad + 1))
                    if quad == 0:
                        pe.wait_ge(v_ready, of + 1)
                    for c2 in range(TB):
                        for r in range(4):
                            last = nc.tensor.matmul(here[32 * r:32 * r + 32, 0:S], vx[s_][:, c2, 4 * quad + r, :],
                                                    st[quad % 2][:, r, c2, :], start=c2 == 0, stop=c2 == TB - 1)
                    last.then_inc(full[slot], 1)
                if what in ("end_u0", "end_u1"):
                    n = int(what[5])
                    pe.wait_ge(u_ready, b * QUADS)
                    for quad in range(QUADS):
                        last = nc.tensor.transpose(here[:, quad * P:(quad + 1) * P], u[:, quad, n * P:(n + 1) * P], t["ident"][:])
                if what == "end_T":
                    pe.wait_ge(cn_ready, b * TB)
                    for c in range(DC):
                        for n in range(TB):
                            last = nc.tensor.transpose(here[:, c * S + n * P:c * S + (n + 1) * P], cn[:, n, c * P:(c + 1) * P], t["ident"][:])
                if what == "end_o":
                    pe.wait_ge(oT_ready, b * DC)
                    for n in range(TB):
                        for c in range(DC):
                            last = nc.tensor.matmul(here[:, n * D:(n + 1) * D], oT[:, c, n * P:(n + 1) * P], wo[:, c, :], start=c == 0, stop=c == DC - 1)
                if what != "heads" and not what.startswith("pv"):
                    last.then_inc(full[slot], 1)

            whole(pe, body)

        @block.vector
        def _(dve):
            row = lambda n: t["X"][:, bass.ds(n, 1), :].rearrange("p o d -> p (o d)")
            stat = lambda name, n: t[name][:, bass.ds(n, 1)]

            def weigh(k, batch):
                slot, _ = batch.head(k)
                n = XH * batch.n + (k + 1)
                dve.wait_ge(low_ready, n)
                if not (isinstance(batch.n, int) and batch.n == 0 and k < 8):
                    dve.wait_ge(u_ready, QUADS * batch.n + (k // 4 - 1))
                nc.vector.scalar_tensor_tensor(st[(k // 4) % 2][:, k % 4].rearrange("p n s -> p (n s)"), bank[slot][:], 0.0,
                                               low[k % RING][:].rearrange("p n s -> p (n s)"), ALU.max, ALU.add).then_inc(st_ready, 1)
                dve.wait_ge(st_ready, n)
                dve.sem_inc(free[slot], 1)

            def body(what, k, batch, slot, before):
                b = batch.n
                here = None if slot is None else bank[slot]
                if what == "heads":
                    for j in range(2):
                        s_, n = batch.head(k + j)
                        dve.wait_ge(full[s_], n + 1)
                        nc.vector.tensor_scalar(low[(k + j) % RING][:].rearrange("p n s -> p (n s)"), bank[s_][:], -1.0, 0.0, ALU.mult, ALU.max).then_inc(neg_ready, 1)
                    for j in range(2):
                        if k:
                            weigh(k - 2 + j, batch)
                        elif not (isinstance(b, int) and b == 0):
                            weigh(XH - 2 + j, batch.last())
                if what == "pv_before" and isinstance(b, int) and b == B:
                    for j in range(2):
                        weigh(XH - 2 + j, batch.last())
                if what == "start_z":
                    tile = (b + 1) * TB
                    for c in range(TB):
                        nc.vector.tensor_scalar(z[:, c, :], row(tile + c), stat("mean", tile + c), stat("rstd", tile + c),
                                                ALU.subtract, ALU.mult).then_inc(z_ready, 1)
                if what in ("end_u0", "end_u1"):
                    n = int(what[5])
                    by_head = here[:].rearrange("p (h e) -> p h e", h=XH)
                    dve.wait_ge(full[slot], before + 1)
                    nc.vector.reciprocal(rec[:, n, :], by_head[:, :, XD]).then_inc(rec_ready, 1)
                    dve.wait_ge(rec_ready, (b - 1) * TB + (n + 1))
                    nc.vector.tensor_tensor(cn[:, n, :].rearrange("p (h e) -> p h e", h=XH), by_head[:, :, 0:XD],
                                            rec[:, n, :, None].to_broadcast([P, XH, XD]), ALU.mult).then_inc(cn_ready, 1)
                    dve.wait_ge(cn_ready, (b - 1) * TB + (n + 1))
                    dve.sem_inc(free[slot], 1)
                if what == "end_o":
                    tile = (b - 1) * TB
                    x = t["X"][:, bass.ds(tile, TB), :]
                    dve.wait_ge(full[slot], before + 1)
                    dve.wait_ge(bo_added, b)
                    nc.vector.tensor_tensor(x, halves(here), x, ALU.add).then_inc(x_done, 1)
                    dve.wait_ge(x_done, b)
                    nc.vector.sem_inc(free[slot], 1)
                    update_stats(nc, t, tile, took_wait)

            whole(dve, body)


FF = 1024
FC = FF // P
MAGIC = 1.5 * 2.0 ** 23
ALL_MAX = bass.bass_isa.ReduceOp.max


def layer1_ffn(nc, t, d, bank):
    ctx = ExitStack()
    with ctx:
        sb = lambda n, shape, dt=FP: ctx.enter_context(nc.sbuf_tensor("f_" + n, shape, dt))
        s = {"win": sb("win", [P, DC, FF]), "wout": sb("wout", [P, FC, D]), "cols": sb("cols", [P, 3, FC]),
             "bo": sb("bo", [P, D]), "scale": sb("scale", [P, 8]), "top": sb("top", [P, 1])}
        hidden = nc.dram_tensor("hidden", (B, P, FC, S), FP).ap()
        ffn_weights(nc, t, d, bank, s)
        ffn_up(nc, t, d, bank, s, hidden)
        ffn_down(nc, t, d, bank, s, hidden)


def ffn_weights(nc, t, d, bank, s):
    ctx = ExitStack()
    with ctx:
        sem = signals(nc, ctx, "fw_")
        sb = lambda n, shape, dt=FP: ctx.enter_context(nc.sbuf_tensor("fw_" + n, shape, dt))
        w = [sb("wi", [P, FC, D]), s["wout"]]
        hi, lo, amax, inv = (sb(n, [P, 2, FC]) for n in ("hi", "lo", "amax", "inv"))
        xhi, xlo = sb("xhi", [P, NT]), sb("xlo", [P, NT])
        top, topall = sb("top", [P, 1]), sb("topall", [P, 1])
        w_in, steps, wi_ready, wT_raw, wT_ready, top_ready, all_ready = (sem(n) for n in ("w_in", "steps", "wi", "wT_raw", "wT", "top", "all"))
        block = ctx.enter_context(nc.Block())
        QUARTERS = 4

        @block.sync
        def _(sp):
            for dst, src in ((w[0], "fwi"), (w[1], "fwo"), (s["bo"], "fbo")):
                sp.dma_start(dst[:], d[src]).then_inc(w_in, 16)
            sp.dma_start(s["cols"][:, 0, :], d["fbi"]).then_inc(w_in, 16)

        @block.tensor
        def _(pe):
            pe.wait_ge(wi_ready, 1)
            for c in range(DC):
                for f in range(FC):
                    last = nc.tensor.transpose(bank[2 * c + f // 4][:, (f % 4) * P:(f % 4 + 1) * P], w[0][:, f, c * P:(c + 1) * P], t["ident"][:])
            last.then_inc(wT_raw, 1)

        @block.scalar
        def _(act):
            act.wait_ge(wT_raw, 1)
            for k in range(2 * DC):
                c, part = k // 2, slice((k % 2) * 512, (k % 2 + 1) * 512)
                last = nc.scalar.activation(s["win"][:, c, part], bank[k][:], ACT.Copy)
            last.then_inc(wT_ready, 1)

        @block.gpsimd
        def _(pool):
            pool.wait_ge(top_ready, 1)
            nc.gpsimd.partition_all_reduce(topall[:], top[:], P, ALL_MAX).then_inc(all_ready, 1)

        @block.vector
        def _(dve):
            ch = Chain(dve, steps, 29)
            dve.wait_ge(w_in, 64)
            for k in range(2):
                ch.did(nc.vector.tensor_reduce(hi[:, k, :], w[k][:], AX.X, ALU.max))
                ch.did(nc.vector.tensor_reduce(lo[:, k, :], w[k][:], AX.X, ALU.min))
            ch.see()
            ch.did(nc.vector.scalar_tensor_tensor(amax[:], lo[:], -1.0, hi[:], ALU.mult, ALU.max)).see()
            ch.did(nc.vector.tensor_scalar(amax[:], amax[:], 1e-8, None, ALU.max)).see()
            ch.did(nc.vector.reciprocal(inv[:], amax[:])).see()
            ch.did(nc.vector.tensor_scalar(inv[:], inv[:], 127.0, None, ALU.mult))
            ch.did(nc.vector.tensor_scalar(amax[:], amax[:], 1.0 / 127.0, None, ALU.mult)).see()
            for k in range(2):
                by = lambda a: a[:, k, :, None].to_broadcast([P, FC, D])
                ch.did(nc.vector.tensor_tensor(w[k][:], w[k][:], by(inv), ALU.mult)).see()
                last = nc.vector.tensor_scalar(w[k][:], w[k][:], MAGIC, MAGIC, ALU.add, ALU.subtract)
                if k == 0:
                    last.then_inc(wi_ready, 1)
                else:
                    ch.did(last).see()
                    ch.did(nc.vector.tensor_tensor(w[k][:], w[k][:], by(amax), ALU.mult))
            for q in range(QUARTERS):
                part = slice(q * NT // QUARTERS, (q + 1) * NT // QUARTERS)
                ch.did(nc.vector.tensor_reduce(xhi[:, part], t["X"][:, part, :], AX.X, ALU.max))
                ch.did(nc.vector.tensor_reduce(xlo[:, part], t["X"][:, part, :], AX.X, ALU.min))
            ch.see()
            nc.vector.tensor_tensor(xhi[:], xhi[:], t["mean"][:], ALU.subtract)
            ch.did(nc.vector.tensor_tensor(xlo[:], t["mean"][:], xlo[:], ALU.subtract)).see()
            ch.did(nc.vector.tensor_tensor(xhi[:], xhi[:], xlo[:], ALU.max)).see()
            ch.did(nc.vector.tensor_tensor(xhi[:], xhi[:], t["rstd"][:], ALU.mult)).see()
            nc.vector.tensor_reduce(top[:], xhi[:], AX.X, ALU.max).then_inc(top_ready, 1)
            dve.wait_ge(all_ready, 1)
            sx, isx = s["scale"][:, 0:1], s["scale"][:, 1:2]
            quantiser(nc, ch, topall, sx, isx)
            ch.did(nc.vector.tensor_scalar(s["cols"][:, 1, :], amax[:, 0, :], isx, None, ALU.mult)).see()
            dve.wait_ge(wT_ready, 1)
            ch.end()


def quantiser(nc, ch, top, scale, inverse):
    ch.did(nc.vector.tensor_scalar(top[:], top[:], 1e-8, None, ALU.max)).see()
    ch.did(nc.vector.reciprocal(scale, top[:]))
    ch.did(nc.vector.tensor_scalar(inverse, top[:], 1.0 / 32767.0, None, ALU.mult)).see()
    ch.did(nc.vector.tensor_scalar(scale, scale, 32767.0, None, ALU.mult)).see()


def ffn_up(nc, t, d, bank, s, hidden):
    ctx = ExitStack()
    with ctx:
        sem = signals(nc, ctx, "fu_")
        sb = lambda n, shape, dt=FP: ctx.enter_context(nc.sbuf_tensor("fu_" + n, shape, dt))
        LANES = range(PAIR)
        z = [sb(f"z{p}", [P, TB, D]) for p in LANES]
        zT = [sb(f"zT{p}", [P, DC, S]) for p in LANES]
        h = [sb(f"h{p}", [P, FC, S]) for p in LANES]
        square = sb("square", [P, FC, S])
        unmagic, one = sb("unmagic", [P, 1]), sb("one", [P, PAIR])
        one_ready, took_wait = sem("one"), sem("took_wait")
        z0, z_ready, zT_raw, zT_ready, h_raw, h_ready, top_ready, setup = (sem(n) for n in ("z0", "z", "zT_raw", "zT", "h_raw", "h", "top", "setup"))
        stored = [sem(f"stored{p}") for p in LANES]
        T = lambda p: bank[4 * p]
        halves = lambda b: b[:].rearrange("p (c s) -> p c s", c=DC)
        block = ctx.enter_context(nc.Block())

        @block.sync
        def _(sp):
            for p in LANES:
                sp.sem_inc(stored[p], 16)
            with sp.Fori(0, TRIPS) as i:
                for p in LANES:
                    sp.wait_ge(h_ready, batch_of(i, p) * FC + 1)
                    sp.dma_start(hidden[bass.ds(i * PAIR + p, 1)].rearrange("o p c s -> p (o c) s"), h[p][:]).then_inc(stored[p], 16)
            for p in LANES:
                sp.wait_ge(stored[p], 16 * (TRIPS + 1))

        @block.scalar
        def _(act):
            nc.scalar.preload_act_table(ACT.Gelu)
            act.sem_inc(h_ready, 1)
            act.wait_ge(setup, 2)
            with act.Fori(0, TRIPS) as i:
                for p in LANES:
                    act.wait_ge(zT_raw, batch_of(i, p))
                    nc.scalar.activation(zT[p][:], halves(T(p)), ACT.Identity, bias=unmagic[:]).then_inc(zT_ready, 1)
                for p in LANES:
                    act.wait_ge(h_raw, batch_of(i, p))
                    act.wait_ge(stored[p], (i + 1) * 16)
                    act.wait_ge(top_ready, batch_of(i, p))
                    for f in range(FC):
                        nc.scalar.activation(h[p][:, f, :], bank[4 * p + f // 2][:, (f % 2) * S:(f % 2 + 1) * S], ACT.Gelu,
                                             bias=s["cols"][:, 0, f:f + 1], scale=s["cols"][:, 1, f:f + 1]).then_inc(h_ready, 1)

        @block.tensor
        def _(pe):
            with pe.Fori(0, TRIPS) as i:
                for p in LANES:
                    pe.wait_ge(z_ready, batch_of(i, p) * TB)
                    pe.wait_ge(h_ready, i * (PAIR * FC) + 1)
                    for c in range(DC):
                        for n in range(TB):
                            last = nc.tensor.transpose(T(p)[:, c * S + n * P:c * S + (n + 1) * P],
                                                       z[p][:, n, c * P:(c + 1) * P], t["ident"][:])
                    last.then_inc(zT_raw, 1)
                for p in LANES:
                    pe.wait_ge(zT_ready, batch_of(i, p))
                    for f in range(FC):
                        for c in range(DC):
                            last = nc.tensor.matmul(bank[4 * p + f // 2][:, (f % 2) * S:(f % 2 + 1) * S], s["win"][:, c, f * P:(f + 1) * P],
                                                    zT[p][:, c, :], start=c == 0, stop=c == DC - 1)
                    last.then_inc(h_raw, 1)

        @block.vector
        def _(dve):
            nc.vector.memset(unmagic[:], -MAGIC).then_inc(setup, 1)
            nc.vector.memset(s["top"][:], 0.0).then_inc(setup, 1)
            nc.vector.sem_inc(top_ready, 1)
            dve.wait_ge(setup, 2)
            with dve.Fori(0, TRIPS) as i:
                for p in LANES:
                    tile = (i * PAIR + p) * TB
                    for c in range(TB):
                        nc.vector.tensor_scalar(z[p][:, c, :], t["X"][:, bass.ds(tile + c, 1), :].rearrange("p o d -> p (o d)"),
                                                t["mean"][:, bass.ds(tile + c, 1)], t["rstd"][:, bass.ds(tile + c, 1)],
                                                ALU.subtract, ALU.mult).then_inc(z0, 1)
                    dve.wait_ge(z0, batch_of(i, p) * TB)
                    for c in range(TB):
                        nc.vector.tensor_scalar(z[p][:, c, :], z[p][:, c, :], s["scale"][:, 0:1], MAGIC, ALU.mult, ALU.add).then_inc(z_ready, 1)
                for p in LANES:
                    dve.wait_ge(h_ready, batch_of(i, p) * FC + 1)
                    flat = h[p][:].rearrange("p c s -> p (c s)")
                    dve.wait_ge(top_ready, batch_of(i, p))
                    nc.vector.sem_inc(took_wait, 1)
                    nc.vector.tensor_tensor_reduce(out=square[:].rearrange("p c s -> p (c s)"), in0=flat, in1=flat, scale=1.0, scalar=0.0,
                                                   op0=ALU.mult, op1=ALU.max, accum_out=one[:, p:p + 1]).then_inc(one_ready, 1)
                    dve.wait_ge(one_ready, batch_of(i, p))
                    nc.vector.tensor_tensor(s["top"][:], s["top"][:], one[:, p:p + 1], ALU.max).then_inc(top_ready, 1)


def ffn_down(nc, t, d, bank, s, hidden):
    ctx = ExitStack()
    with ctx:
        sem = signals(nc, ctx, "fd_")
        sb = lambda n, shape, dt=FP: ctx.enter_context(nc.sbuf_tensor("fd_" + n, shape, dt))
        LANES = range(PAIR)
        h = [sb(f"h{p}", [P, FC, S]) for p in LANES]
        q = [sb(f"q{p}", [P, FC, S]) for p in LANES]
        top, topall = sb("top", [P, 1]), sb("topall", [P, 1])
        steps, all_ready, root, q0, q_ready, o_raw, x_done, bo_added, took_pool_wait = (
            sem(n) for n in ("steps", "all", "root", "q0", "q", "o_raw", "x_done", "bo", "took_pool_wait"))
        h_in = [sem(f"h_in{p}") for p in LANES]
        O = lambda p: bank[p]
        block = ctx.enter_context(nc.Block())

        @block.sync
        def _(sp):
            with sp.Fori(0, TRIPS) as i:
                for p in LANES:
                    sp.wait_ge(q0, i * PAIR + 1)
                    sp.dma_start(h[p][:], hidden[bass.ds(i * PAIR + p, 1)].rearrange("o p c s -> p (o c) s")).then_inc(h_in[p], 16)

        @block.gpsimd
        def _(pool):
            nc.gpsimd.partition_all_reduce(topall[:], s["top"][:], P, ALL_MAX).then_inc(all_ready, 1)
            with pool.Fori(0, B) as b:
                x = t["X"][:, bass.ds(b * TB, TB), :]
                nc.gpsimd.tensor_tensor(x, x, s["bo"][:, None, :].to_broadcast([P, TB, D]), ALU.add).then_inc(bo_added, 1)

        @block.scalar
        def _(act):
            act.wait_ge(all_ready, 1)
            nc.scalar.activation(top[:], topall[:], ACT.Sqrt).then_inc(root, 1)

        @block.tensor
        def _(pe):
            nc.tensor.sem_inc(o_raw, 1)
            with pe.Fori(0, TRIPS) as i:
                for p in LANES:
                    pe.wait_ge(q_ready, batch_of(i, p))
                    pe.wait_ge(x_done, i * PAIR + 1)
                    for n in range(TB):
                        for f in range(FC):
                            last = nc.tensor.matmul(O(p)[:, n * D:(n + 1) * D], q[p][:, f, n * P:(n + 1) * P], s["wout"][:, f, :],
                                                    start=f == 0, stop=f == FC - 1)
                    last.then_inc(o_raw, 1)

        @block.vector
        def _(dve):
            dve.wait_ge(root, 1)
            ch = Chain(dve, steps, 4)
            sh, ish = s["scale"][:, 2:3], s["scale"][:, 3:4]
            quantiser(nc, ch, top, sh, ish)
            ch.end()
            nc.vector.sem_inc(q0, 1)
            nc.vector.sem_inc(x_done, 1)
            with dve.Fori(0, TRIPS) as i:
                for p in LANES:
                    dve.wait_ge(h_in[p], (i + 1) * 16)
                    dve.wait_ge(o_raw, i * PAIR + 1)
                    nc.vector.tensor_scalar(q[p][:], h[p][:], sh, MAGIC, ALU.mult, ALU.add).then_inc(q0, 1)
                    dve.wait_ge(q0, batch_of(i, p) + 1)
                    nc.vector.tensor_scalar(q[p][:], q[p][:], MAGIC, None, ALU.subtract).then_inc(q_ready, 1)
                for p in LANES:
                    x = t["X"][:, bass.ds((i * PAIR + p) * TB, TB), :]
                    dve.wait_ge(o_raw, batch_of(i, p) + 1)
                    dve.wait_ge(bo_added, batch_of(i, p))
                    nc.vector.scalar_tensor_tensor(x, O(p)[:].rearrange("p (c k) -> p c k", c=TB), ish, x, ALU.mult, ALU.add).then_inc(x_done, 1)
            dve.wait_ge(x_done, B + 1)


def store_everything(nc, t, out):
    ctx = ExitStack()
    with ctx:
        x_out = signals(nc, ctx, "st_")("x_out")
        block = ctx.enter_context(nc.Block())
        view = out.rearrange("(n p) d -> p n d", p=P)
        PARTS = 4

        @block.sync
        def _(sp):
            for q in range(PARTS):
                n0 = q * NT // PARTS
                sp.dma_start(view[:, n0:n0 + NT // PARTS, :], t["X"][:, n0:n0 + NT // PARTS, :]).then_inc(x_out, 16)
            sp.wait_ge(x_out, 16 * PARTS)


def build(nc, d, out):
    ctx = ExitStack()
    with ctx:
        sb = lambda n, shape, dt=FP: ctx.enter_context(nc.sbuf_tensor(n, shape, dt))
        t = {"X": sb("X", [P, NT, D]), "mean": sb("mean", [P, NT]), "var": sb("var", [P, NT]), "rstd": sb("rstd", [P, NT]),
             "bn": sb("bn", [P, NT, 6]), "eps": sb("eps", [P, 1]), "ident": sb("ident", [P, P]),
             "identb": sb("identb", [P, P], BF), "maskneg": sb("maskneg", [P, 3 * P], BF)}
        bank = [ctx.enter_context(nc.psum_tensor(f"bank{k}", [P, 512], FP)) for k in range(8)]
        load_everything(nc, t, d)
        LAYERS = [layer0_attention, layer0_mlstm, layer0_experts, layer1_rwkv, layer1_stablemax, layer1_ffn]
        for n, layer in enumerate(LAYERS):
            row_stats(nc, t, f"ln{n}")
            layer(nc, t, d, bank)
        store_everything(nc, t, out)


def kernel(**inputs):
    import numpy as np
    import ml_dtypes
    import concourse.bacc as bacc
    from concourse.bass_utils import run_bass_kernel_spmd

    a = {k: np.asarray(v) for k, v in inputs.items()}

    def by_rows(w):
        return w.reshape(w.shape[0] // P, P, -1).transpose(1, 0, 2)

    def column(v):
        return v.reshape(-1, P).T

    def rows(v):
        return np.broadcast_to(v.reshape(1, -1), (P, v.size))

    qkv, qkv_b = a["L0_attn_qkv_w"], a["L0_attn_qkv_b"]
    key, token = np.arange(P)[:, None], np.arange(P)[None, :]
    causal = np.where(key > token, -1e30, 0.0)
    mask = np.concatenate([causal, np.zeros((P, P)), causal], 1)

    def gate_weights(w):
        g = np.zeros((P, 3 * DC, 2, 32), np.float32)
        by = w.reshape(2, HEADS, 3 * DC, P).transpose(3, 2, 0, 1)
        g[..., 0:HEADS] = by
        g[..., HEADS:2 * HEADS] = by
        return g

    gate_bias = np.zeros((LANES4, 32, 2), np.float32)
    gate_bias[:, 0:HEADS] = gate_bias[:, HEADS:2 * HEADS] = a["L0_xattn_ifgate_b"].reshape(2, HEADS).T
    gate_bias = gate_bias.reshape(P, 2)
    r, h = np.arange(P)[:, None] % 32, np.arange(HEADS)[None, :]
    gate_rows = np.concatenate([r < HEADS, -1.0 * ((r >= HEADS) & (r < 2 * HEADS)), r == HEADS + h, r == h], 1).astype(np.float32)
    quad_order = np.arange(D).reshape(2, 4, 2, 16).transpose(0, 2, 1, 3).reshape(-1)
    data = {
        "x": a["x"].reshape(B * S, D),
        "ident": np.eye(P, dtype=np.float32),
        "identb": np.eye(P).astype(ml_dtypes.bfloat16),
        "maskneg": mask.astype(ml_dtypes.bfloat16),
        "wqk": by_rows(qkv[:2 * D].T), "wv": by_rows(qkv[2 * D:].T), "wproj": by_rows(a["L0_attn_proj_w"].T),
        "acols": np.stack([column(a["L0_attn_norm_w"]), column(a["L0_attn_norm_b"]), column(qkv_b[2 * D:])], 1),
        "bqk": rows(qkv_b[:2 * D]), "bproj": rows(a["L0_attn_proj_b"]),
        "dwk": by_rows(a["L1_attn_Wk"].T), "dwv": by_rows(a["L1_attn_Wv"].T), "dwr": by_rows(a["L1_attn_Wr"].T),
        "dwo": by_rows(a["L1_attn_Wo"].T),
        "dcols": np.stack([column(a["L1_attn_" + n]) for n in ("time_mix_k", "time_mix_v", "time_mix_r", "time_decay", "time_first")], 1),
        "gw": gate_weights(a["L0_xattn_ifgate_w"]), "gbias": gate_bias, "grows": gate_rows,
        "outnorm": rows(a["L0_xattn_outnorm_w"]),
        "ctx": a["ctx_1024"].reshape(B, TB, P, D).transpose(0, 2, 1, 3),
        "ctxT": a["ctx_1024"].transpose(0, 2, 1).reshape(B, DC, P, S).transpose(0, 2, 1, 3),
        "ewq": by_rows(a["L1_xattn_Wq"].T), "ewk": by_rows(a["L1_xattn_Wk"].T),
        "ewv": by_rows(a["L1_xattn_Wv"].T[:, quad_order]), "ewo": by_rows(a["L1_xattn_Wo"].T[quad_order]),
        "ecols": np.stack([column(a["L1_xattn_bq"]), column(a["L1_xattn_bk"]), column(a["L1_xattn_bv"][quad_order])], 1),
        "emask": np.concatenate([r < 16, r >= 16], 1).astype(np.float32), "ebo": rows(a["L1_xattn_bo"]),
        "fwi": by_rows(a["L1_ffn_W_in"].T), "fwo": by_rows(a["L1_ffn_W_out"]), "fbi": column(a["L1_ffn_b_in"]),
        "fbo": rows(a["L1_ffn_b_out"]),
        "cw1": a["L0_ffn_w1"].transpose(2, 0, 1).reshape(DC, P, EX, EF).transpose(1, 2, 0, 3),
        "cw2": a["L0_ffn_w2"].transpose(2, 0, 1).reshape(EFC, P, EX, D).transpose(1, 2, 0, 3),
        "cb1": a["L0_ffn_b1"].reshape(EX, EFC, P).transpose(2, 0, 1), "cb2": a["L0_ffn_b2"],
        "crouter": by_rows(a["L0_ffn_router_w"].T), "cnumber": rows(np.arange(EX, dtype=np.float32)),
    }
    nc = bacc.Bacc("TRN2", target_bir_lowering=False, num_devices=1)
    arrays, d = {}, {}
    for name, v in data.items():
        arrays[name + "_dram"] = v = np.ascontiguousarray(v)
        d[name] = nc.dram_tensor(name + "_dram", v.shape, mybir.dt.from_np(v.dtype), kind="ExternalInput").ap()
    out = nc.dram_tensor("out_dram", (B * S, D), FP, kind="ExternalOutput").ap()
    build(nc, d, out)
    r = run_bass_kernel_spmd(nc, [arrays], core_ids=[0])
    return r.results[0]["out_dram"].reshape(B, S, D)
```

```python
import concourse.bass as bass
from concourse import mybir
from contextlib import ExitStack

FP = mybir.dt.float32
BF = mybir.dt.bfloat16
ALU = mybir.AluOpType
ACT = mybir.ActivationFunctionType
AX = mybir.AxisListType

B, S, D = 32, 256, 256
P = 128
NT = B * S // P
TB = S // P
DC = D // P
PAIR = 2
TRIPS = B // PAIR
EPS = 1e-5


def batch_of(i, p):
    return i * PAIR + (p + 1)


class Chain:

    def __init__(self, eng, sem, per=0, trip=0, before=0):
        self.eng, self.sem, self.base, self.per, self.n = eng, sem, trip * per + before, per, 0

    def did(self, ins):
        self.n += 1
        ins.then_inc(self.sem, 1)
        return self

    def see(self):
        self.eng.wait_ge(self.sem, self.base + self.n)

    def end(self):
        assert self.n == self.per, (self.sem, self.n, self.per)


def signals(nc, ctx, prefix):
    held = []

    def give_back():
        nc.clear_and_free_semaphores(held)
        nc.all_engine_barrier()

    def sem(name):
        held.append(nc.alloc_semaphore(prefix + name))
        return held[-1]

    ctx.callback(give_back)
    return sem


def load_everything(nc, t, d):
    ctx = ExitStack()
    with ctx:
        sem = signals(nc, ctx, "ld_")
        QUARTERS, STEP = 4, 8
        x_in, const_in, stats_done = [sem(f"x_in{q}") for q in range(QUARTERS)], sem("const_in"), sem("ld_stats")
        block = ctx.enter_context(nc.Block())

        @block.sync
        def _(sp):
            for name, dram in (("ident", d["ident"]), ("maskneg", d["maskneg"]), ("identb", d["identb"])):
                sp.dma_start(t[name][:], dram).then_inc(const_in, 16)
            view = d["x"].rearrange("(n p) d -> p n d", p=P)
            for q in range(QUARTERS):
                n0 = q * NT // QUARTERS
                sp.dma_start(t["X"][:, n0:n0 + NT // QUARTERS, :], view[:, n0:n0 + NT // QUARTERS, :]).then_inc(x_in[q], 16)
            sp.wait_ge(const_in, 48)

        @block.vector
        def _(dve):
            nc.vector.memset(t["eps"][:], EPS)
            for q in range(QUARTERS):
                dve.wait_ge(x_in[q], 16)
                with dve.Fori(q * NT // QUARTERS // STEP, (q + 1) * NT // QUARTERS // STEP) as i:
                    for k in range(STEP):
                        n = bass.ds(i * STEP + k, 1)
                        nc.vector.bn_stats(t["bn"][:, n, :].rearrange("p o s -> p (o s)"),
                                           t["X"][:, n, :].rearrange("p o d -> p (o d)")).then_inc(stats_done, 1)
            dve.wait_ge(stats_done, NT)


def row_stats(nc, t, tag):
    ctx = ExitStack()
    with ctx:
        sem = signals(nc, ctx, tag)
        root, done = sem("_root"), sem("_steps")
        block = ctx.enter_context(nc.Block())
        VAR_STEPS = 6

        @block.scalar
        def _(act):
            act.wait_ge(done, VAR_STEPS)
            nc.scalar.activation(t["rstd"][:], t["var"][:], ACT.Sqrt, bias=t["eps"][:]).then_inc(root, 1)

        @block.vector
        def _(dve):
            even, odd = (t["bn"][:, :, 3 * h + 1] for h in range(2))
            spread, mean, var = t["rstd"], t["mean"], t["var"]
            ch = Chain(dve, done, VAR_STEPS + 1)
            ch.did(nc.vector.tensor_tensor(mean[:], even, odd, ALU.add))
            ch.did(nc.vector.tensor_tensor(spread[:], even, odd, ALU.subtract))
            ch.did(nc.vector.tensor_tensor(var[:], t["bn"][:, :, 2], t["bn"][:, :, 5], ALU.add)).see()
            nc.vector.tensor_scalar(mean[:], mean[:], 0.5, None, ALU.mult)
            ch.did(nc.vector.tensor_tensor(spread[:], spread[:], spread[:], ALU.mult))
            ch.did(nc.vector.tensor_scalar(var[:], var[:], 1.0 / D, None, ALU.mult)).see()
            ch.did(nc.vector.scalar_tensor_tensor(var[:], spread[:], 0.25, var[:], ALU.mult, ALU.add))
            dve.wait_ge(root, 1)
            ch.did(nc.vector.reciprocal(t["rstd"][:], t["rstd"][:])).see()
            ch.end()


def update_stats(nc, t, tile, took_wait):
    nc.vector.sem_inc(took_wait, 1)
    for c in range(TB):
        nc.vector.bn_stats(t["bn"][:, bass.ds(tile + c, 1), :].rearrange("p o s -> p (o s)"),
                           t["X"][:, bass.ds(tile + c, 1), :].rearrange("p o d -> p (o d)"))


def layer0_attention(nc, t, d, bank):
    ctx = ExitStack()
    with ctx:
        sem = signals(nc, ctx, "a_")
        sb = lambda n, shape, dt=FP: ctx.enter_context(nc.sbuf_tensor("a_" + n, shape, dt))
        wqk, wv, wproj = sb("wqk", [P, DC, 2 * D]), sb("wv", [P, DC, D]), sb("wproj", [P, DC, D])
        bqk, bproj = sb("bqk", [P, 2 * D]), sb("bproj", [P, D])
        cols = sb("cols", [P, 3, DC])
        var2, r2 = sb("var2", [P, NT]), sb("r2", [P, NT])
        r12, gain, shift = sb("r12", [P, NT]), sb("gain", [P, NT]), sb("shift", [P, NT])
        z = [sb(f"z{p}", [P, TB, D]) for p in range(PAIR)]
        hT = [sb(f"hT{p}", [P, DC, S]) for p in range(PAIR)]
        qk = [sb(f"qk{p}", [P, TB, 2 * D]) for p in range(PAIR)]
        vT = [sb(f"vT{p}", [P, DC, S]) for p in range(PAIR)]
        top = sb("top", [P, PAIR, DC])
        ntop = sb("ntop", [P, PAIR, DC])
        e = [sb(f"e{p}", [P, DC, D]) for p in range(PAIR)]
        esum, rsum = sb("esum", [P, PAIR, DC]), sb("rsum", [P, PAIR, DC])
        eT = [sb(f"eT{p}", [P, DC, D]) for p in range(PAIR)]
        aT = [sb(f"aT{p}", [P, DC, S]) for p in range(PAIR)]
        res = [sb(f"res{p}", [P, TB, D]) for p in range(PAIR)]
        w_in, root = sem("w_in"), sem("root")
        z_ready, zT_ready, hT_ready = sem("z"), sem("zT"), sem("hT")
        qk_raw, qk_ready, v_raw, v_ready = sem("qk_raw"), sem("qk"), sem("v_raw"), sem("v")
        sc_raw, ntop_ready, e_ready = sem("sc_raw"), sem("ntop"), sem("e")
        eT_raw, eT_ready, rsum_ready = sem("eT_raw"), sem("eT"), sem("rsum")
        a_raw, a_ready, o_raw, x_done = sem("a_raw"), sem("a"), sem("o_raw"), sem("x_done")
        res_scaled, res_ready, v_steps = sem("res_scaled"), sem("res"), sem("v_steps")
        took_wait = sem("took_wait")
        zB, qB, vB = (lambda p: bank[4 * p]), (lambda p: (bank[4 * p + 1], bank[4 * p + 2])), (lambda p: bank[4 * p + 3])
        ONCE, PER = 7, 2
        block = ctx.enter_context(nc.Block())

        @block.sync
        def _(sp):
            for dst, src in ((wqk, "wqk"), (wv, "wv"), (wproj, "wproj"), (cols, "acols"), (bqk, "bqk"), (bproj, "bproj")):
                sp.dma_start(dst[:], d[src]).then_inc(w_in, 16)

        @block.gpsimd
        def _(pool):
            pool.wait_ge(w_in, 96)
            with pool.Fori(0, TRIPS) as i:
                for p in range(PAIR):
                    pool.wait_ge(res_scaled, batch_of(i, p) * TB)
                    nc.gpsimd.tensor_tensor(res[p][:], res[p][:], bproj[:, None, :].to_broadcast([P, TB, D]), ALU.add).then_inc(res_ready, 1)

        @block.scalar
        def _(act):
            act.wait_ge(v_steps, 2)
            nc.scalar.activation(r2[:], var2[:], ACT.Sqrt, bias=t["eps"][:]).then_inc(root, 1)
            nc.scalar.preload_act_table(ACT.Exp)
            act.wait_ge(w_in, 96)
            def turned(i):
                for p in range(PAIR):
                    act.wait_ge(zT_ready, batch_of(i, p))
                    for c in range(DC):
                        nc.scalar.activation(hT[p][:, c, :], zB(p)[:, c * S:(c + 1) * S], ACT.Identity,
                                             bias=cols[:, 1, c:c + 1], scale=cols[:, 0, c:c + 1]).then_inc(hT_ready, 1)

            def middle(i):
                for p in range(PAIR):
                    act.wait_ge(v_raw, batch_of(i, p))
                    for c in range(DC):
                        nc.scalar.activation(vT[p][:, c, :], vB(p)[:, c * S:(c + 1) * S], ACT.Identity,
                                             bias=cols[:, 2, c:c + 1]).then_inc(v_ready, 1)
                for p in range(PAIR):
                    act.wait_ge(ntop_ready, batch_of(i, p))
                    for c in range(DC):
                        nc.scalar.activation(e[p][:, c, :], zB(p)[:, c * D:(c + 1) * D], ACT.Exp,
                                             bias=ntop[:, p, c:c + 1], scale=1.0 / 16,
                                             accum_out=esum[:, p, c:c + 1]).then_inc(e_ready, 1)
                for p in range(PAIR):
                    act.wait_ge(a_raw, batch_of(i, p))
                    act.wait_ge(rsum_ready, batch_of(i, p))
                    for c in range(DC):
                        nc.scalar.activation(aT[p][:, c, :], qB(p)[1][:, c * S:(c + 1) * S], ACT.Identity,
                                             scale=rsum[:, p, c:c + 1]).then_inc(a_ready, 1)

            turned(0)
            with act.Fori(0, TRIPS - 1) as i:
                middle(i)
                turned(i + 1)
            middle(TRIPS - 1)

        @block.tensor
        def _(pe):
            pe.wait_ge(w_in, 96)
            def turn(i):
                for p in range(PAIR):
                    pe.wait_ge(z_ready, batch_of(i, p) * TB)
                    for c in range(DC):
                        for n in range(TB):
                            last = nc.tensor.transpose(zB(p)[:, c * S + n * P:c * S + (n + 1) * P],
                                                       z[p][:, n, c * P:(c + 1) * P], t["ident"][:])
                    last.then_inc(zT_ready, 1)

            def middle(i):
                for p in range(PAIR):
                    pe.wait_ge(hT_ready, batch_of(i, p) * DC)
                    for n in range(TB):
                        for c in range(DC):
                            last = nc.tensor.matmul(qB(p)[n][:], hT[p][:, c, n * P:(n + 1) * P], wqk[:, c, :],
                                                    start=c == 0, stop=c == DC - 1)
                    last.then_inc(qk_raw, 1)
                    pe.wait_ge(x_done, batch_of(i, p))
                    for k in range(DC):
                        for c in range(DC):
                            last = nc.tensor.matmul(vB(p)[:, k * S:(k + 1) * S], wv[:, c, k * P:(k + 1) * P], hT[p][:, c, :],
                                                    start=c == 0, stop=c == DC - 1)
                    last.then_inc(v_raw, 1)
                for p in range(PAIR):
                    pe.wait_ge(qk_ready, batch_of(i, p))
                    for q in range(DC):
                        for n in range(TB):
                            last = nc.tensor.matmul(zB(p)[:, q * D:(q + 1) * D], qk[p][:, n, q * P:(q + 1) * P], qk[p][:, n, D:2 * D],
                                                    start=n == 0, stop=n == TB - 1)
                    last.then_inc(sc_raw, 1)
                for p in range(PAIR):
                    pe.wait_ge(e_ready, batch_of(i, p) * DC)
                    for k in range(DC):
                        for q in range(DC):
                            last = nc.tensor.transpose(qB(p)[0][:, k * D + q * P:k * D + (q + 1) * P],
                                                       e[p][:, q, k * P:(k + 1) * P], t["ident"][:])
                    last.then_inc(eT_raw, 1)
                for p in range(PAIR):
                    pe.wait_ge(eT_ready, batch_of(i, p))
                    pe.wait_ge(v_ready, batch_of(i, p) * DC)
                    for q in range(DC):
                        for k in range(DC):
                            last = nc.tensor.matmul(qB(p)[1][:, q * S:(q + 1) * S], eT[p][:, k, q * P:(q + 1) * P], vT[p][:, k, :],
                                                    start=k == 0, stop=k == DC - 1)
                    last.then_inc(a_raw, 1)

            def project(i):
                for p in range(PAIR):
                    pe.wait_ge(a_ready, batch_of(i, p) * DC)
                    for n in range(TB):
                        for q in range(DC):
                            last = nc.tensor.matmul(vB(p)[:, n * D:(n + 1) * D], aT[p][:, q, n * P:(n + 1) * P], wproj[:, q, :],
                                                    start=q == 0, stop=q == DC - 1)
                    last.then_inc(o_raw, 1)

            turn(0)
            with pe.Fori(0, TRIPS - 1) as i:
                middle(i)
                turn(i + 1)
                project(i)
            middle(TRIPS - 1)
            project(TRIPS - 1)

        @block.vector
        def _(dve):
            one = Chain(dve, v_steps, ONCE)
            one.did(nc.vector.tensor_tensor(var2[:], t["var"][:], t["rstd"][:], ALU.mult)); one.see()
            one.did(nc.vector.tensor_tensor(var2[:], var2[:], t["rstd"][:], ALU.mult))
            dve.wait_ge(root, 1)
            one.did(nc.vector.reciprocal(r2[:], r2[:])); one.see()
            one.did(nc.vector.tensor_tensor(r12[:], r2[:], t["rstd"][:], ALU.mult))
            one.did(nc.vector.tensor_scalar(gain[:], t["rstd"][:], 1.0, None, ALU.add))
            one.did(nc.vector.tensor_tensor(shift[:], t["mean"][:], t["rstd"][:], ALU.mult)); one.see()
            one.did(nc.vector.tensor_scalar(shift[:], shift[:], -1.0, None, ALU.mult)); one.see()
            one.end()
            nc.vector.sem_inc(x_done, PAIR)
            dve.wait_ge(w_in, 96)
            def normalise(i):
                for p in range(PAIR):
                    tile = (i * PAIR + p) * TB
                    for c in range(TB):
                        nc.vector.tensor_scalar(z[p][:, c, :], t["X"][:, bass.ds(tile + c, 1), :].rearrange("p o d -> p (o d)"),
                                                t["mean"][:, bass.ds(tile + c, 1)], r12[:, bass.ds(tile + c, 1)],
                                                ALU.subtract, ALU.mult).then_inc(z_ready, 1)

            def residual(i):
                for p in range(PAIR):
                    tile = (i * PAIR + p) * TB
                    for c in range(TB):
                        nc.vector.tensor_scalar(res[p][:, c, :], t["X"][:, bass.ds(tile + c, 1), :].rearrange("p o d -> p (o d)"),
                                                gain[:, bass.ds(tile + c, 1)], shift[:, bass.ds(tile + c, 1)],
                                                ALU.mult, ALU.add).then_inc(res_scaled, 1)

            def middle(i):
                ch = Chain(dve, v_steps, PER, i, ONCE)
                for p in range(PAIR):
                    dve.wait_ge(qk_raw, batch_of(i, p))
                    for n in range(TB):
                        last = nc.vector.tensor_tensor(qk[p][:, n, :], qB(p)[n][:], bqk[:], ALU.add)
                    last.then_inc(qk_ready, 1)
                for p in range(PAIR):
                    dve.wait_ge(sc_raw, batch_of(i, p))
                    ch.did(nc.vector.tensor_reduce(top[:, p, :], zB(p)[:].rearrange("p (c k) -> p c k", c=DC), AX.X, ALU.max)); ch.see()
                    nc.vector.tensor_scalar(ntop[:, p, :], top[:, p, :], -1.0 / 16, None, ALU.mult).then_inc(ntop_ready, 1)
                for p in range(PAIR):
                    dve.wait_ge(e_ready, batch_of(i, p) * DC)
                    nc.vector.reciprocal(rsum[:, p, :], esum[:, p, :]).then_inc(rsum_ready, 1)
                    dve.wait_ge(eT_raw, batch_of(i, p))
                    nc.vector.tensor_copy(eT[p][:], qB(p)[0][:].rearrange("p (c k) -> p c k", c=DC)).then_inc(eT_ready, 1)
                ch.end()

            def add(i):
                for p in range(PAIR):
                    tile = (i * PAIR + p) * TB
                    dve.wait_ge(o_raw, batch_of(i, p))
                    dve.wait_ge(res_ready, batch_of(i, p))
                    nc.vector.tensor_tensor(t["X"][:, bass.ds(tile, TB), :], vB(p)[:].rearrange("p (c k) -> p c k", c=TB),
                                            res[p][:], ALU.add).then_inc(x_done, 1)
                    dve.wait_ge(x_done, batch_of(i, p) + PAIR)
                    update_stats(nc, t, tile, took_wait)

            normalise(0)
            residual(0)
            with dve.Fori(0, TRIPS - 1) as i:
                middle(i)
                normalise(i + 1)
                add(i)
                residual(i + 1)
            middle(TRIPS - 1)
            add(TRIPS - 1)


LANES4 = 4
GROUPS = B // LANES4
HEADS = 8
HD = D // HEADS
CAP = 15.0


def lane_count(g, j):
    return g * LANES4 + (j + 1)


def mlstm_gates(nc, t, d, bank, s):
    ctx = ExitStack()
    with ctx:
        sem = signals(nc, ctx, "g_")
        sb = lambda n, shape, dt=FP: ctx.enter_context(nc.sbuf_tensor("g_" + n, shape, dt))
        LANES = range(LANES4)
        gw = sb("gw", [P, 6, 2, 32])
        gc = sb("gc", [P, DC, 2, 32])
        z = [sb(f"z{j}", [P, TB, D]) for j in LANES]
        qT = [sb(f"qT{j}", [P, DC, S]) for j in LANES]
        cT = [sb(f"cT{j}", [P, DC, S]) for j in LANES]
        w_in, gc_ready, z_ready, zT_raw, qT_ready, pre_raw, pre_ready = (sem(n) for n in ("w_in", "gc", "z", "zT", "qT", "pre_raw", "pre"))
        c_in = [sem(f"c_in{j}") for j in LANES]
        T, G = (lambda j: bank[4 + j]), bank[0]
        halves = lambda b: b[:].rearrange("p (c s) -> p c s", c=DC)
        block = ctx.enter_context(nc.Block())

        @block.sync
        def _(sp):
            sp.dma_start(gw[:], d["gw"]).then_inc(w_in, 16)
            with sp.Fori(0, GROUPS) as g:
                for j in LANES:
                    sp.wait_ge(pre_raw, g + 1)
                    sp.dma_start(cT[j][:], d["ctxT"][bass.ds(g * LANES4 + j, 1)].rearrange("o p c s -> p (o c) s")).then_inc(c_in[j], 16)

        @block.vector
        def _(dve):
            dve.wait_ge(w_in, 16)
            nc.vector.tensor_tensor(gc[:], gw[:, 2:4], gw[:, 4:6], ALU.add).then_inc(gc_ready, 1)
            nc.vector.sem_inc(pre_ready, 1)
            with dve.Fori(0, GROUPS) as g:
                for j in LANES:
                    tile = (g * LANES4 + j) * TB
                    for c in range(TB):
                        nc.vector.tensor_scalar(z[j][:, c, :], t["X"][:, bass.ds(tile + c, 1), :].rearrange("p o d -> p (o d)"),
                                                t["mean"][:, bass.ds(tile + c, 1)], t["rstd"][:, bass.ds(tile + c, 1)],
                                                ALU.subtract, ALU.mult).then_inc(z_ready, 1)
                dve.wait_ge(pre_raw, g + 2)
                nc.vector.tensor_copy(s["pre"][:, :, bass.ds(g, 1), :].rearrange("p a o s -> p a (o s)"),
                                      G[:].rearrange("p (a s) -> p a s", a=2)).then_inc(pre_ready, 1)

        @block.tensor
        def _(pe):
            pe.wait_ge(gc_ready, 1)
            nc.tensor.sem_inc(pre_raw, 1)
            with pe.Fori(0, GROUPS) as g:
                for j in LANES:
                    pe.wait_ge(z_ready, lane_count(g, j) * TB)
                    for c in range(DC):
                        for n in range(TB):
                            last = nc.tensor.transpose(T(j)[:, c * S + n * P:c * S + (n + 1) * P],
                                                       z[j][:, n, c * P:(c + 1) * P], t["ident"][:])
                    last.then_inc(zT_raw, 1)
                pe.wait_ge(pre_ready, g + 1)
                for j in LANES:
                    pe.wait_ge(qT_ready, lane_count(g, j))
                    pe.wait_ge(c_in[j], (g + 1) * 16)
                    for a in range(2):
                        out = G[32 * j:32 * j + 32, a * S:(a + 1) * S]
                        for c in range(DC):
                            nc.tensor.matmul(out, gw[:, c, a, :], qT[j][:, c, :], start=c == 0, stop=False)
                        for c in range(DC):
                            last = nc.tensor.matmul(out, gc[:, c, a, :], cT[j][:, c, :], start=False, stop=c == DC - 1)
                last.then_inc(pre_raw, 1)

        @block.scalar
        def _(act):
            with act.Fori(0, GROUPS) as g:
                for j in LANES:
                    act.wait_ge(zT_raw, lane_count(g, j))
                    nc.scalar.activation(qT[j][:], halves(T(j)), ACT.Copy).then_inc(qT_ready, 1)


def mlstm_decays(nc, t, d, s):
    ctx = ExitStack()
    with ctx:
        sem = signals(nc, ctx, "m_")
        sb = lambda n, shape, dt=FP: ctx.enter_context(nc.sbuf_tensor("m_" + n, shape, dt))
        bias, rows_ = sb("bias", [P, 2]), s["rows"]
        keep, penalty = sb("keep", [P, GROUPS, S]), sb("penalty", [P, GROUPS, S])
        cum = sb("cum", [P, GROUPS, S])
        pre, g, top, m = s["pre"], s["g"], s["top"], s["m"]
        flat = lambda a: a.rearrange("p g s -> p (g s)")
        c_in, steps, tanh_done, exp_done, ln_done = (sem(n) for n in ("c_in", "steps", "tanh", "exp", "ln"))
        block = ctx.enter_context(nc.Block())

        @block.sync
        def _(sp):
            sp.dma_start(bias[:], d["gbias"]).then_inc(c_in, 16)
            sp.dma_start(rows_[:], d["grows"]).then_inc(c_in, 16)

        @block.scalar
        def _(act):
            act.wait_ge(steps, 1)
            for a in range(2):
                nc.scalar.activation(flat(pre[:, a]), flat(pre[:, a]), ACT.Tanh, bias=bias[:, a:a + 1], scale=1.0 / CAP).then_inc(tanh_done, 1)
            act.wait_ge(tanh_done, 2)
            nc.scalar.preload_act_table_set("natural_log_exp_and_others")
            nc.scalar.activation(flat(pre[:, 1]), flat(pre[:, 1]), ACT.Exp, scale=-CAP).then_inc(exp_done, 1)
            act.wait_ge(exp_done, 1)
            nc.scalar.activation(flat(pre[:, 1]), flat(pre[:, 1]), ACT.Ln, bias=1.0).then_inc(ln_done, 1)

        @block.vector
        def _(dve):
            ch = Chain(dve, steps, 11)
            dve.wait_ge(c_in, 32)
            ch.did(nc.vector.tensor_scalar(bias[:], bias[:], 1.0 / CAP, None, ALU.mult)).see()
            ch.did(nc.vector.memset(keep[:], 1.0))
            ch.did(nc.vector.memset(penalty[:], 0.0)).see()
            ch.did(nc.vector.memset(keep[:, :, 0:1], 0.0))
            ch.did(nc.vector.memset(penalty[:, :, 0:1], -1e30)).see()
            dve.wait_ge(ln_done, 1)
            ch.did(nc.vector.tensor_tensor_scan(flat(cum[:]), flat(keep[:]), flat(pre[:, 1]), 0.0, ALU.mult, ALU.subtract)).see()
            ch.did(nc.vector.scalar_tensor_tensor(flat(top[:]), flat(pre[:, 0]), CAP, flat(cum[:]), ALU.mult, ALU.subtract)).see()
            ch.did(nc.vector.tensor_scalar(flat(g[:]), flat(top[:]), rows_[:, 0:1], rows_[:, 1:2], ALU.mult, ALU.add))
            ch.did(nc.vector.tensor_tensor_scan(flat(m[:]), flat(penalty[:]), flat(top[:]), 0.0, ALU.add, ALU.max)).see()
            ch.did(nc.vector.tensor_copy(flat(top[:]), flat(m[:]))).see()
            ch.did(nc.vector.tensor_tensor(flat(m[:]), flat(m[:]), flat(cum[:]), ALU.add)).see()
            ch.end()


def layer0_mlstm(nc, t, d, bank):
    ctx = ExitStack()
    with ctx:
        sb = lambda n, shape, dt=FP: ctx.enter_context(nc.sbuf_tensor("b_" + n, shape, dt))
        s = {"g": sb("g", [P, GROUPS, S]), "top": sb("top", [P, GROUPS, S]), "m": sb("m", [P, GROUPS, S]),
             "rows": sb("rows", [P, 2 + 2 * HEADS])}
        with nc.sbuf_tensor("b_pre", [P, 2, GROUPS, S], FP) as pre:
            s["pre"] = pre
            mlstm_gates(nc, t, d, bank, s)
            mlstm_decays(nc, t, d, s)
        mlstm_heads(nc, t, d, bank, s)


def mlstm_heads(nc, t, d, bank, s):
    ctx = ExitStack()
    with ctx:
        sem = signals(nc, ctx, "b_")
        sb = lambda n, shape, dt=FP: ctx.enter_context(nc.sbuf_tensor("b_" + n, shape, dt))
        LANES, JOBS, LAG, RING = range(LANES4), LANES4 * HEADS, 2, 4
        VW = HD + 1
        COLS = 3 * P
        gain = sb("gain", [P, D])
        gm, right = sb("gm", [P, S]), sb("right", [P, HEADS, S])
        lg = sb("lg", [P, LANES4, S])
        em = sb("em", [P, TB, LANES4, HEADS])
        tiny = sb("tiny", [P, 1])
        z = [sb(f"z{k}", [P, TB, D]) for k in range(2)]
        qT = [sb(f"qT{k}", [P, HEADS, S]) for k in range(2)]
        head_rows = sb("head_rows", [P, P // HD])
        cT = [sb(f"cT{k}", [P, DC, S]) for k in range(2)]
        cn = [sb(f"cn{k}", [P, TB, D]) for k in range(2)]
        v = [sb(f"v{k}", [P, TB, HEADS, VW]) for k in range(2)]
        decay = [sb(f"decay{k}", [P, COLS]) for k in range(RING)]
        sm = [sb(f"sm{k}", [P, COLS]) for k in range(RING)]
        o = [sb(f"o{k}", [P, TB, HEADS, VW]) for k in range(2)]
        sq, y = sb("sq", [P, TB, HEADS, HD]), sb("y", [P, TB, HEADS, HD])
        small = [sb(f"small{k}", [P, TB, HEADS]) for k in range(6)]
        ss, den, rden, rden2, rms, scale = small
        names = ("w_in", "setup", "group", "mT_raw", "em", "z", "zT_raw", "qT", "v", "pv", "o_read", "o", "sq", "q_in", "rms_ln", "rms",
                 "scale", "y0", "y", "x_done", "took_wait", "steps", "sc", "dd", "decay", "sm", "c_used", "took_pool_wait", "em_used")
        (w_in, setup, group, mT_raw, em_ready, z_ready, zT_raw, qT_ready, v_ready, pv_done, o_read, o_ready, sq_ready, q_in, rms_ln, rms_ready,
         scale_ready, y0_ready, y_ready, x_done, took_wait, steps, sc_raw, dd_raw, decay_ready, sm_ready, c_used, took_pool_wait, em_used) = (sem(n) for n in names)
        c_in = [sem(f"c_in{k}") for k in range(2)]
        SC, DD, O, T, MT = (bank[0], bank[1]), (bank[2], bank[3]), (bank[4], bank[5]), bank[6], bank[7]
        halves = lambda b: b[:].rearrange("p (c s) -> p c s", c=DC)
        SETUP, GROUP_OPS = 4, 1 + LANES4 + HEADS
        PER = 6 * LANES4
        block = ctx.enter_context(nc.Block())

        def following(g, j):
            return (g, j + 1) if j + 1 < LANES4 else None if isinstance(g, int) else (g + 1, 0)

        def groups(eng, body):
            with eng.Fori(0, GROUPS - 1) as g:
                body(g)
            body(GROUPS - 1)

        @block.sync
        def _(sp):
            sp.dma_start(gain[:], d["outnorm"]).then_inc(w_in, 16)
            sp.dma_start(head_rows[:], d["bheads"]).then_inc(w_in, 16)
            with sp.Fori(0, GROUPS) as g:
                for j in LANES:
                    k = j % 2
                    sp.wait_ge(c_used, lane_count(g, j))
                    b = bass.ds(g * LANES4 + j, 1)
                    sp.dma_start(cT[k][:], d["ctxT"][b].rearrange("o p c s -> p (o c) s")).then_inc(c_in[k], 16)
                    sp.dma_start(cn[k][:], d["ctx"][b].rearrange("o p n d -> p (o n) d")).then_inc(c_in[k], 16)

        def arrived(g, j):
            return g * 64 + (j // 2 + 1) * 32

        @block.gpsimd
        def _(pool):
            for k in range(2):
                nc.gpsimd.memset(v[k][:], 1.0).then_inc(setup, 1)
            nc.gpsimd.memset(tiny[:], 1e-6).then_inc(setup, 1)
            pool.wait_ge(setup, 3)
            pool.wait_ge(w_in, 32)
            nc.gpsimd.tensor_scalar(gain[:], gain[:], 1.0, None, ALU.add).then_inc(setup, 1)
            pool.wait_ge(setup, SETUP)

            def values(g, j):
                pool.wait_ge(c_in[j % 2], arrived(g, j))
                nc.gpsimd.sem_inc(took_pool_wait, 1)
                nc.gpsimd.tensor_copy(v[j % 2][:, :, :, 0:HD], cn[j % 2][:].rearrange("p n (h e) -> p n h e", h=HEADS)).then_inc(v_ready, 1)

            def norm(g, j):
                pool.wait_ge(o_ready, lane_count(g, j) + 1)
                ov = o[j % 2][:, :, :, 0:HD]
                nc.gpsimd.tensor_tensor(sq[:], ov, ov, ALU.mult).then_inc(sq_ready, 1)
                pool.wait_ge(scale_ready, lane_count(g, j))
                nc.gpsimd.tensor_tensor(y[:], ov, scale[:, :, :, None].to_broadcast([P, TB, HEADS, HD]), ALU.mult).then_inc(y0_ready, 1)
                pool.wait_ge(y0_ready, lane_count(g, j))
                nc.gpsimd.tensor_tensor(y[:].rearrange("p n h e -> p n (h e)"), y[:].rearrange("p n h e -> p n (h e)"),
                                        gain[:, None, :].to_broadcast([P, TB, D]), ALU.mult).then_inc(y_ready, 1)

            with pool.Fori(0, GROUPS) as g:
                for n in range(JOBS + LAG):
                    if n % HEADS == 0 and n < JOBS:
                        values(g, n // HEADS)
                    if n % HEADS == LAG and n > HEADS:
                        norm(g, n // HEADS - 1)
                norm(g, LANES4 - 1) if (JOBS + LAG - 1) % HEADS < LAG else None

        @block.scalar
        def _(act):
            act.wait_ge(setup, 3)
            act.wait_ge(w_in, 32)
            act.preload_act_table_set("natural_log_exp_and_others")
            act.sem_inc(o_ready, 1)

            def queries(g, j):
                act.wait_ge(zT_raw, lane_count(g, j))
                for h in range(HEADS):
                    last = nc.scalar.activation(qT[j % 2][:, h, :], T[:, (h // 4) * S:(h // 4 + 1) * S], ACT.Copy, scale=head_rows[:, h % 4:h % 4 + 1])
                last.then_inc(qT_ready, 1)

            def rms_root(g, j):
                act.wait_ge(q_in, lane_count(g, j))
                nc.scalar.activation(rms[:], rms[:], ACT.Ln, scale=1.0 / HD, bias=tiny[:]).then_inc(rms_ln, 1)
                act.wait_ge(rms_ln, lane_count(g, j))
                nc.scalar.activation(rms[:], rms[:], ACT.Exp, scale=-0.5).then_inc(rms_ready, 1)

            def body(g):
                for n in range(JOBS + LAG):
                    if n < JOBS:
                        act.wait_ge(dd_raw, g * JOBS + (n + 1))
                        if n >= RING:
                            act.wait_ge(sm_ready, g * JOBS + (n - RING + 1))
                        nc.scalar.activation(decay[n % RING][:], DD[n % 2][:, 0:COLS], ACT.Exp).then_inc(decay_ready, 1)
                    if n % HEADS == 4 and n < JOBS and following(g, n // HEADS):
                        queries(*following(g, n // HEADS))
                    if n == HEADS - 2:
                        act.wait_ge(mT_raw, g + 1)
                        act.wait_ge(em_used, g + 1)
                        nc.scalar.activation(em[:], MT[:, 0:TB * P].rearrange("p (n j r) -> p n j r", n=TB, j=LANES4)[:, :, :, 0:HEADS],
                                             ACT.Exp, scale=-1.0).then_inc(em_ready, 1)
                    if n % HEADS == LAG - 1 and n >= HEADS:
                        j = n // HEADS - 1
                        act.wait_ge(pv_done, lane_count(g, j))
                        for b in range(TB):
                            last = nc.scalar.activation(o[j % 2][:, b].rearrange("p h e -> p (h e)"), O[b][:, 0:HEADS * VW], ACT.Copy)
                        last.then_inc(o_ready, 1)
                    if n % HEADS == 5 and n > HEADS:
                        rms_root(g, n // HEADS - 1)
                rms_root(g, LANES4 - 1)

            queries(0, 0)
            groups(act, body)

        @block.tensor
        def _(pe):
            def transpose_z(g, j):
                pe.wait_ge(z_ready, lane_count(g, j) * TB)
                if j or not isinstance(g, int):
                    pe.wait_ge(qT_ready, lane_count(g, j) - 1)
                for c in range(DC):
                    for n in range(TB):
                        last = nc.tensor.transpose(T[:, c * S + n * P:c * S + (n + 1) * P],
                                                   z[j % 2][:, n, c * P:(c + 1) * P], t["ident"][:])
                last.then_inc(zT_raw, 1)

            def body(g):
                pe.wait_ge(group, (g + 1) * GROUP_OPS)
                for n in range(JOBS + LAG):
                    if n < JOBS:
                        j, h = n // HEADS, n % HEADS
                        k, c = j % 2, h // 4
                        if h == 0:
                            pe.wait_ge(c_in[k], arrived(g, j))
                            pe.wait_ge(qT_ready, lane_count(g, j))
                        if n >= 2:
                            pe.wait_ge(sm_ready, g * JOBS + (n - 1))
                        out = SC[n % 2]
                        nc.tensor.matmul(out[:, 0:S], cT[k][:, c, 0:P], qT[k][:, h, :], start=True, stop=True)
                        nc.tensor.matmul(out[:, S:COLS], cT[k][:, c, P:S], qT[k][:, h, P:S], start=True, stop=True).then_inc(sc_raw, 1)
                        if n >= 2:
                            pe.wait_ge(decay_ready, g * JOBS + (n - 1))
                        out = DD[n % 2]
                        nc.tensor.matmul(out[:, 0:COLS], t["identb"][:], t["maskneg"][:], start=True, stop=False)
                        nc.tensor.matmul(out[:, 0:S], lg[:, j, 0:P], right[:, h, :], start=False, stop=False)
                        nc.tensor.matmul(out[:, S:COLS], lg[:, j, P:S], right[:, h, P:S], start=False, stop=True).then_inc(dd_raw, 1)
                        if n % HEADS == 3 and following(g, j):
                            transpose_z(*following(g, j))
                        if n == 2:
                            for c in range(TB):
                                last = nc.tensor.transpose(MT[:, c * P:(c + 1) * P], gm[:, c * P:(c + 1) * P], t["ident"][:])
                            last.then_inc(mT_raw, 1)
                    if n >= LAG:
                        q = n - LAG
                        j, h = q // HEADS, q % HEADS
                        k = j % 2
                        if h == 0:
                            pe.wait_ge(v_ready, lane_count(g, j))
                            pe.wait_ge(o_ready, lane_count(g, j))
                        pe.wait_ge(sm_ready, g * JOBS + (q + 1))
                        m, w = sm[q % RING], slice(h * VW, (h + 1) * VW)
                        nc.tensor.matmul(O[0][:, w], m[:, 0:P], v[k][:, 0, h, :], start=True, stop=True)
                        nc.tensor.matmul(O[1][:, w], m[:, P:S], v[k][:, 0, h, :], start=True, stop=False)
                        last = nc.tensor.matmul(O[1][:, w], m[:, S:COLS], v[k][:, 1, h, :], start=False, stop=True)
                        if h == HEADS - 1:
                            last.then_inc(pv_done, 1)

            transpose_z(0, 0)
            groups(pe, body)

        @block.vector
        def _(dve):
            nc.vector.sem_inc(em_used, 1)
            nc.vector.sem_inc(c_used, 2)
            dve.wait_ge(w_in, 32)

            def queries(g, j):
                tile = (g * LANES4 + j) * TB
                for c in range(TB):
                    nc.vector.tensor_scalar(z[j % 2][:, c, :], t["X"][:, bass.ds(tile + c, 1), :].rearrange("p o d -> p (o d)"),
                                            t["mean"][:, bass.ds(tile + c, 1)], t["rstd"][:, bass.ds(tile + c, 1)],
                                            ALU.subtract, ALU.mult).then_inc(z_ready, 1)

            def norm(g, j, ch):
                dve.wait_ge(o_ready, lane_count(g, j) + 1)
                nc.vector.sem_inc(c_used, 1)
                ch.did(nc.vector.tensor_tensor(den[:], o[j % 2][:, :, :, HD], em[:, :, j, :], ALU.max)).see()
                if j == LANES4 - 1:
                    nc.vector.sem_inc(em_used, 1)
                ch.did(nc.vector.scalar_tensor_tensor(den[:], o[j % 2][:, :, :, HD], -1.0, den[:], ALU.mult, ALU.max)).see()
                ch.did(nc.vector.tensor_scalar(den[:], den[:], 5e-5, None, ALU.add)).see()
                ch.did(nc.vector.reciprocal(rden[:], den[:])).see()
                dve.wait_ge(sq_ready, lane_count(g, j))
                ch.did(nc.vector.tensor_reduce(ss[:], sq[:], AX.X, ALU.add))
                ch.did(nc.vector.tensor_tensor(rden2[:], rden[:], rden[:], ALU.mult)).see()
                nc.vector.tensor_tensor(rms[:], ss[:], rden2[:], ALU.mult).then_inc(q_in, 1)

            def finish(g, j):
                dve.wait_ge(rms_ready, lane_count(g, j))
                nc.vector.tensor_tensor(scale[:], rms[:], rden[:], ALU.mult).then_inc(scale_ready, 1)

            def add(g, j):
                tile = (g * LANES4 + j) * TB
                x = t["X"][:, bass.ds(tile, TB), :]
                dve.wait_ge(y_ready, lane_count(g, j))
                nc.vector.tensor_tensor(x, y[:].rearrange("p n h e -> p n (h e)"), x, ALU.add).then_inc(x_done, 1)
                dve.wait_ge(x_done, lane_count(g, j))
                update_stats(nc, t, tile, took_wait)

            def prepare(g):
                col = lambda name: s[name][:, bass.ds(g, 1), :].rearrange("p o s -> p (o s)")
                nc.vector.tensor_copy(gm[:], col("m")).then_inc(group, 1)
                for j in LANES:
                    nc.vector.tensor_scalar(lg[:, j, :], col("g"), head_rows[:, j:j + 1], None, ALU.mult).then_inc(group, 1)
                for h in range(HEADS):
                    nc.vector.tensor_scalar(right[:, h, :], col("top"), s["rows"][:, 2 + h:3 + h], s["rows"][:, 2 + HEADS + h:3 + HEADS + h],
                                            ALU.mult, ALU.add).then_inc(group, 1)

            def body(g):
                ch = Chain(dve, steps, PER, g)
                for n in range(JOBS + LAG):
                    if n < JOBS:
                        dve.wait_ge(sc_raw, g * JOBS + (n + 1))
                        dve.wait_ge(decay_ready, g * JOBS + (n + 1))
                        nc.vector.scalar_tensor_tensor(sm[n % RING][:], SC[n % 2][:, 0:COLS], float(HD) ** -0.5, decay[n % RING][:],
                                                       ALU.mult, ALU.mult).then_inc(sm_ready, 1)
                    if n % HEADS == 2 and n < JOBS and following(g, n // HEADS):
                        queries(*following(g, n // HEADS))
                    if n == JOBS - 1 and not isinstance(g, int):
                        prepare(g + 1)
                    j = n // HEADS - 1
                    if n >= HEADS and n < JOBS and n % HEADS == 3:
                        norm(g, j, ch)
                    if n >= HEADS and n < JOBS and n % HEADS == 5:
                        finish(g, j)
                    if n >= HEADS and n < JOBS and n % HEADS == 7:
                        add(g, j)
                norm(g, LANES4 - 1, ch)
                finish(g, LANES4 - 1)
                add(g, LANES4 - 1)
                ch.end()

            prepare(0)
            queries(0, 0)
            groups(dve, body)


EX, EF = 8, 512
EFC = EF // P
GROUP_ROWS = 2 * P
GROUP_TILES = GROUP_ROWS // P
MAX_GROUPS = B * S // GROUP_ROWS
SLOT_GROUPS = 2 * B * S // GROUP_ROWS + EX
FULL_GROUPS = 2 * B * S // GROUP_ROWS
CHOSEN = 2


def layer0_experts(nc, t, d, bank):
    ctx = ExitStack()
    with ctx:
        sb = lambda n, shape, dt=FP: ctx.enter_context(nc.sbuf_tensor("c_" + n, shape, dt))
        s = {"place": sb("place", [P, NT, CHOSEN]), "prob": sb("prob", [P, NT, CHOSEN]), "slot": sb("slot", [P, CHOSEN, NT], mybir.dt.uint32),
             "expert": sb("expert", [P, SLOT_GROUPS], mybir.dt.int32), "last": sb("last", [P, EX], mybir.dt.int32),
             "rows": nc.dram_tensor("slot_rows", (SLOT_GROUPS * GROUP_ROWS, D), FP).ap(), "y": nc.dram_tensor("slot_y", (SLOT_GROUPS * GROUP_ROWS, D), FP).ap()}
        choose_experts(nc, t, d, bank, s)
        place_slots(nc, t, d, bank, s)
        fill_slots(nc, t, d, s)
        run_experts(nc, t, d, bank, s)
        collect_slots(nc, t, s)


def choose_experts(nc, t, d, bank, s):
    ctx = ExitStack()
    with ctx:
        sem = signals(nc, ctx, "cr_")
        sb = lambda n, shape, dt=FP: ctx.enter_context(nc.sbuf_tensor("cr_" + n, shape, dt))
        TT, WIDE = 4, 4 * P
        N = NT // TT
        router = sb("router", [P, DC, EX])
        z, zT = sb("z", [P, TT, D]), sb("zT", [P, DC, WIDE])
        lg, best, place = sb("lg", [P, TT, EX]), sb("best", [P, TT, EX]), sb("place", [P, TT, EX], mybir.dt.uint32)
        w_in, z_ready, zT_raw, zT_ready, lg_raw, lg_read, steps, chosen, took_wait = (
            sem(n) for n in ("w_in", "z", "zT_raw", "zT", "lg_raw", "lg_read", "steps", "chosen", "took_wait"))
        H, L = bank[0:DC], bank[DC]
        PER = 1 + 2 * TT
        block = ctx.enter_context(nc.Block())

        @block.sync
        def _(sp):
            sp.dma_start(router[:], d["crouter"]).then_inc(w_in, 16)

        @block.tensor
        def _(pe):
            pe.wait_ge(w_in, 16)
            nc.tensor.sem_inc(lg_read, 1)
            with pe.Fori(0, N) as i:
                pe.wait_ge(z_ready, (i + 1) * TT)
                for c in range(DC):
                    for n in range(TT):
                        last = nc.tensor.transpose(H[c][:, n * P:(n + 1) * P], z[:, n, c * P:(c + 1) * P], t["ident"][:])
                    last.then_inc(zT_raw, 1)
                pe.wait_ge(zT_ready, (i + 1) * DC)
                pe.wait_ge(lg_read, i + 1)
                for n in range(TT):
                    for c in range(DC):
                        last = nc.tensor.matmul(L[:, n * EX:(n + 1) * EX], zT[:, c, n * P:(n + 1) * P], router[:, c, :], start=c == 0, stop=c == DC - 1)
                last.then_inc(lg_raw, 1)

        @block.scalar
        def _(act):
            with act.Fori(0, N) as i:
                for c in range(DC):
                    act.wait_ge(zT_raw, i * DC + (c + 1))
                    nc.scalar.activation(zT[:, c, :], H[c][:], ACT.Copy).then_inc(zT_ready, 1)

        @block.vector
        def _(dve):
            def normalise(i):
                for n in range(TT):
                    nc.vector.tensor_scalar(z[:, n, :], t["X"][:, bass.ds(i * TT + n, 1), :].rearrange("p o d -> p (o d)"),
                                            t["mean"][:, bass.ds(i * TT + n, 1)], t["rstd"][:, bass.ds(i * TT + n, 1)],
                                            ALU.subtract, ALU.mult).then_inc(z_ready, 1)

            def choose(i):
                ch = Chain(dve, steps, PER, i)
                dve.wait_ge(lg_raw, i + 1)
                ch.did(nc.vector.tensor_copy(lg[:], L[:, 0:TT * EX].rearrange("p (n e) -> p n e", n=TT))).see()
                nc.vector.sem_inc(lg_read, 1)
                for n in range(TT):
                    ch.did(nc.vector.max(best[:, n, :], lg[:, n, :]))
                ch.see()
                nc.vector.sem_inc(took_wait, 1)
                for n in range(TT):
                    ch.did(nc.vector.max_index(place[:, n, :], best[:, n, :], lg[:, n, :]))
                nc.vector.tensor_tensor(s["prob"][:, bass.ds(i * TT, TT), 0], best[:, :, 1], best[:, :, 0], ALU.subtract)
                ch.see()
                nc.vector.tensor_copy(s["place"][:, bass.ds(i * TT, TT), :], place[:, :, 0:CHOSEN]).then_inc(chosen, 1)
                dve.wait_ge(chosen, i + 1)
                ch.end()

            normalise(0)
            with dve.Fori(0, N - 1) as i:
                dve.wait_ge(zT_raw, (i + 1) * DC)
                normalise(i + 1)
                choose(i)
            choose(N - 1)


def place_slots(nc, t, d, bank, s):
    ctx = ExitStack()
    with ctx:
        sem = signals(nc, ctx, "cp_")
        sb = lambda n, shape, dt=FP: ctx.enter_context(nc.sbuf_tensor("cp_" + n, shape, dt))
        earlier, ones = sb("earlier", [P, P]), sb("ones", [P, P])
        number, group_number, group_start = sb("number", [P, EX]), sb("group_number", [P, SLOT_GROUPS]), sb("group_start", [P, MAX_GROUPS])
        took = [sb(f"took{k}", [P, NT, EX]) for k in range(CHOSEN)]
        both, scan = sb("both", [P, NT, EX]), [sb(f"scan{k}", [P, NT, EX]) for k in range(2)]
        above = sb("above", [P, EX, MAX_GROUPS])
        groups, end, base, lastf = sb("groups", [P, EX]), sb("end", [P, EX]), sb("base", [P, EX]), sb("lastf", [P, EX])
        past, expertf, slotf = sb("past", [P, SLOT_GROUPS, EX]), sb("expertf", [P, SLOT_GROUPS]), sb("slotf", [P, CHOSEN, NT])
        prob = s["prob"]
        zero = sb("zero", [P, GROUP_TILES, D])
        w_in, both_ready, ranked, steps, exp_ready, last_ready, zero_ready, tail_done, end_done = (
            sem(n) for n in ("w_in", "both", "ranked", "steps", "exp", "last", "zero", "tail_done", "end_done"))
        RANK, TOTAL = bank[0], bank[1]
        flat = lambda a: a[:].rearrange("p n e -> p (n e)")
        LOADS = ((earlier, "cearlier"), (ones, "cones"), (number, "cnumber"), (group_number, "cgroup"), (group_start, "cstart"))
        block = ctx.enter_context(nc.Block())
        tile_view = s["rows"].rearrange("(g n p) d -> g p n d", p=P, n=GROUP_TILES)

        @block.sync
        def _(sp):
            for dst, src in LOADS:
                sp.dma_start(dst[:], d[src]).then_inc(w_in, 16)
            sp.wait_ge(zero_ready, 1)
            for g in range(FULL_GROUPS, SLOT_GROUPS):
                sp.dma_start(tile_view[g], zero[:]).then_inc(tail_done, 16)
            sp.wait_ge(tail_done, 16 * (SLOT_GROUPS - FULL_GROUPS))
            sp.wait_ge(last_ready, 1)
            for e in range(EX):
                g = sp.value_load(s["last"][0:1, e:e + 1], min_val=0, max_val=SLOT_GROUPS - 1)
                sp.dma_start(tile_view[bass.ds(g, 1)].rearrange("o p n d -> (o p) n d"), zero[:]).then_inc(end_done, 16)
                sp.wait_ge(end_done, 16 * (e + 1))

        @block.gpsimd
        def _(pool):
            nc.gpsimd.memset(zero[:], 0.0).then_inc(zero_ready, 1)

        @block.tensor
        def _(pe):
            pe.wait_ge(both_ready, 1)
            nc.tensor.matmul(RANK[:], earlier[:], flat(both), start=True, stop=True)
            nc.tensor.matmul(TOTAL[:], ones[:], flat(both), start=True, stop=True).then_inc(ranked, 1)

        @block.scalar
        def _(act):
            nc.scalar.activation(prob[:, :, 1], prob[:, :, 0], ACT.Exp).then_inc(exp_ready, 1)

        @block.vector
        def _(dve):
            ch = Chain(dve, steps)
            dve.wait_ge(w_in, 16 * len(LOADS))
            by_tile = lambda a: a[:, None, :].to_broadcast([P, NT, EX])
            for k in range(CHOSEN):
                ch.did(nc.vector.tensor_tensor(took[k][:], s["place"][:, :, k:k + 1].to_broadcast([P, NT, EX]), by_tile(number), ALU.is_equal))
            ch.see()
            nc.vector.tensor_tensor(both[:], took[0][:], took[1][:], ALU.add).then_inc(both_ready, 1)
            dve.wait_ge(exp_ready, 1)
            ch.did(nc.vector.tensor_scalar(prob[:, :, 0], prob[:, :, 1], 1.0, None, ALU.add)).see()
            ch.did(nc.vector.reciprocal(prob[:, :, 0], prob[:, :, 0])).see()
            ch.did(nc.vector.tensor_tensor(prob[:, :, 1], prob[:, :, 0], prob[:, :, 1], ALU.mult))
            dve.wait_ge(ranked, 1)
            ch.did(nc.vector.tensor_copy(flat(scan[0]), TOTAL[:])).see()
            src, step = 0, 1
            while step < NT:
                a, b = scan[src], scan[1 - src]
                ch.did(nc.vector.tensor_copy(b[:, 0:step, :], a[:, 0:step, :]))
                ch.did(nc.vector.tensor_tensor(b[:, step:, :], a[:, step:, :], a[:, :NT - step, :], ALU.add)).see()
                src, step = 1 - src, 2 * step
            total, spare = scan[src], scan[1 - src]
            ch.did(nc.vector.tensor_tensor(above[:], total[:, NT - 1, :, None].to_broadcast([P, EX, MAX_GROUPS]),
                                           group_start[:, None, :].to_broadcast([P, EX, MAX_GROUPS]), ALU.is_gt)).see()
            ch.did(nc.vector.tensor_reduce(groups[:], above[:], AX.X, ALU.add)).see()
            ch.did(nc.vector.tensor_copy(end[:], groups[:])).see()
            for e in range(1, EX):
                ch.did(nc.vector.tensor_tensor(end[:, e:e + 1], end[:, e - 1:e], groups[:, e:e + 1], ALU.add)).see()
            ch.did(nc.vector.tensor_scalar(lastf[:], end[:], -1.0, 0.0, ALU.add, ALU.max))
            ch.did(nc.vector.tensor_tensor(base[:], end[:], groups[:], ALU.subtract)).see()
            nc.vector.tensor_copy(s["last"][:], lastf[:]).then_inc(last_ready, 1)
            ch.did(nc.vector.tensor_scalar(base[:], base[:], float(GROUP_ROWS), None, ALU.mult))
            ch.did(nc.vector.tensor_tensor(flat(spare), flat(total), TOTAL[:], ALU.subtract)).see()
            ch.did(nc.vector.tensor_tensor(flat(spare), flat(spare), RANK[:], ALU.add)).see()
            ch.did(nc.vector.tensor_tensor(spare[:], spare[:], by_tile(base), ALU.add)).see()
            for k in range(CHOSEN):
                ch.did(nc.vector.tensor_tensor(took[k][:], took[k][:], spare[:], ALU.mult)).see()
                ch.did(nc.vector.tensor_reduce(slotf[:, k, :], took[k][:], AX.X, ALU.add)).see()
            ch.did(nc.vector.tensor_copy(s["slot"][:], slotf[:]))
            ch.did(nc.vector.tensor_tensor(past[:], group_number[:, :, None].to_broadcast([P, SLOT_GROUPS, EX]),
                                           end[:, None, :].to_broadcast([P, SLOT_GROUPS, EX]), ALU.is_ge)).see()
            ch.did(nc.vector.tensor_reduce(expertf[:], past[:], AX.X, ALU.add)).see()
            ch.did(nc.vector.tensor_scalar(expertf[:], expertf[:], float(EX - 1), None, ALU.min)).see()
            ch.did(nc.vector.tensor_copy(s["expert"][:], expertf[:])).see()


def fill_slots(nc, t, d, s):
    ctx = ExitStack()
    with ctx:
        sem = signals(nc, ctx, "cf_")
        sb = lambda n, shape, dt=FP: ctx.enter_context(nc.sbuf_tensor("cf_" + n, shape, dt))
        Q = 4
        z, slot = [sb(f"z{q}", [P, D]) for q in range(Q)], [sb(f"slot{q}", [P, CHOSEN], mybir.dt.uint32) for q in range(Q)]
        z_ready, took_wait, sent = sem("z"), sem("took_wait"), [sem(f"sent{q}") for q in range(Q)]
        block = ctx.enter_context(nc.Block())

        @block.gpsimd
        def _(pool):
            with pool.Fori(0, NT // Q) as i:
                for q in range(Q):
                    pool.wait_ge(z_ready, i * Q + (q + 1))
                    nc.gpsimd.sem_inc(took_wait, 1)
                    for k in range(CHOSEN):
                        pool.indirect_dma_start(s["rows"], bass.IndirectOffsetOnAxis(ap=slot[q][:, k:k + 1], axis=0), z[q][:], None).then_inc(sent[q], 16)
            for q in range(Q):
                pool.wait_ge(sent[q], 16 * CHOSEN * (NT // Q))

        @block.vector
        def _(dve):
            def normalise(i, q, first=False):
                n = i * Q + q
                if not first:
                    dve.wait_ge(sent[q], i * (16 * CHOSEN))
                nc.vector.tensor_copy(slot[q][:], s["slot"][:, :, bass.ds(n, 1)].rearrange("p k o -> p (k o)"))
                nc.vector.tensor_scalar(z[q][:], t["X"][:, bass.ds(n, 1), :].rearrange("p o d -> p (o d)"),
                                        t["mean"][:, bass.ds(n, 1)], t["rstd"][:, bass.ds(n, 1)],
                                        ALU.subtract, ALU.mult).then_inc(z_ready, 1)

            for q in range(Q):
                normalise(0, q, True)
            with dve.Fori(1, NT // Q) as i:
                for q in range(Q):
                    normalise(i, q)


def run_experts(nc, t, d, bank, s):
    ctx = ExitStack()
    with ctx:
        sem = signals(nc, ctx, "cx_")
        sb = lambda n, shape, dt=FP: ctx.enter_context(nc.sbuf_tensor("cx_" + n, shape, dt))
        w2, b1, b2 = sb("w2", [P, EX, EFC, D]), sb("b1", [P, EX, EFC]), sb("b2", [P, EX, D])
        w1 = [sb(f"w1_{k}", [P, DC, EF]) for k in range(2)]
        rows = [sb(f"rows{k}", [P, GROUP_TILES, D]) for k in range(2)]
        zT = [sb(f"zT{k}", [P, DC, GROUP_ROWS]) for k in range(2)]
        h = [sb(f"h{k}", [P, EFC, GROUP_ROWS]) for k in range(2)]
        y = [sb(f"y{k}", [P, GROUP_TILES, D]) for k in range(2)]
        w_in, rows_in, w1_in, y_out = sem("w_in"), *[[sem(f"{n}{k}") for k in range(2)] for n in ("rows_in", "w1_in", "y_out")]
        zT_raw, zT_ready, h_raw, h_ready, y_raw, y_ready = (sem(n) for n in ("zT_raw", "zT", "h_raw", "h", "y_raw", "y"))
        T, H, Y = bank[0], (bank[1:3], bank[3:5]), bank[5:7]
        view = lambda name, g: s[name].rearrange("(g n p) d -> g p n d", p=P, n=GROUP_TILES)[bass.ds(g, 1)].rearrange("o p n d -> (o p) n d")
        number = lambda eng, g: eng.value_load(s["expert"][0:1, bass.ds(g, 1)], min_val=0, max_val=EX - 1)
        LOADS = ((w2, "cw2"), (b1, "cb1"), (b2, "cb2"))
        HALF = SLOT_GROUPS // 2
        block = ctx.enter_context(nc.Block())

        @block.sync
        def _(sp):
            for dst, src in LOADS:
                sp.dma_start(dst[:], d[src]).then_inc(w_in, 16)
            with sp.Fori(0, HALF) as i:
                for k in range(2):
                    g = i * 2 + k
                    sp.wait_ge(zT_raw, i * 2 + (k + 1))
                    sp.dma_start(rows[k][:], view("rows", g)).then_inc(rows_in[k], 16)
                    e = number(sp, g)
                    sp.wait_ge(h_raw, i * 4 + (2 * k + 2))
                    sp.dma_start(w1[k][:], d["cw1"][bass.ds(e, 1)].rearrange("o p c f -> (o p) c f")).then_inc(w1_in[k], 16)

        @block.gpsimd
        def _(pool):
            with pool.Fori(0, HALF) as i:
                for k in range(2):
                    pool.wait_ge(y_ready, i * 2 + (k + 1))
                    pool.dma_start(view("y", i * 2 + k), y[k][:]).then_inc(y_out[k], 16)
            for k in range(2):
                pool.wait_ge(y_out[k], 16 * HALF)

        @block.tensor
        def _(pe):
            nc.tensor.sem_inc(zT_raw, 2)
            nc.tensor.sem_inc(h_raw, 4)
            pe.wait_ge(w_in, 16 * len(LOADS))

            def turn(j, k, i):
                pe.wait_ge(rows_in[k], (i + 1) * 16)
                pe.wait_ge(zT_ready, j) if not isinstance(j, int) or j > 0 else None
                for c in range(DC):
                    for n in range(GROUP_TILES):
                        last = nc.tensor.transpose(T[:, (c * GROUP_TILES + n) * P:(c * GROUP_TILES + n + 1) * P], rows[k][:, n, c * P:(c + 1) * P], t["ident"][:])
                last.then_inc(zT_raw, 1)

            def up(j, k, i):
                pe.wait_ge(w1_in[k], (i + 1) * 16)
                pe.wait_ge(zT_ready, j + 1)
                for f in range(EFC):
                    for c in range(DC):
                        last = nc.tensor.matmul(H[k][f // 2][:, (f % 2) * GROUP_ROWS:(f % 2 + 1) * GROUP_ROWS], w1[k][:, c, f * P:(f + 1) * P], zT[k][:, c, :],
                                                start=c == 0, stop=c == DC - 1)
                    if f % 2:
                        last.then_inc(h_raw, 1)

            def down(j, k, i):
                e = number(pe, j)
                pe.wait_ge(h_ready, (j + 1) * EFC)
                pe.wait_ge(y_ready, j - 1) if not isinstance(j, int) or j > 1 else None
                for n in range(GROUP_TILES):
                    for f in range(EFC):
                        last = nc.tensor.matmul(Y[k][:, n * D:(n + 1) * D], h[k][:, f, n * P:(n + 1) * P],
                                                w2[:, bass.ds(e, 1), f, :].rearrange("p o d -> p (o d)"), start=f == 0, stop=f == EFC - 1)
                last.then_inc(y_raw, 1)

            turn(0, 0, 0)
            up(0, 0, 0)
            turn(1, 1, 0)
            up(1, 1, 0)
            turn(2, 0, 1)
            down(0, 0, 0)
            up(2, 0, 1)
            turn(3, 1, 1)
            down(1, 1, 0)
            with pe.Fori(1, HALF - 1) as i:
                up(i * 2 + 1, 1, i)
                turn(i * 2 + 2, 0, i + 1)
                down(i * 2, 0, i)
                up(i * 2 + 2, 0, i + 1)
                turn(i * 2 + 3, 1, i + 1)
                down(i * 2 + 1, 1, i)
            up(SLOT_GROUPS - 1, 1, HALF - 1)
            down(SLOT_GROUPS - 2, 0, HALF - 1)
            down(SLOT_GROUPS - 1, 1, HALF - 1)

        @block.scalar
        def _(act):
            act.wait_ge(w_in, 16 * len(LOADS))
            nc.scalar.preload_act_table(ACT.Gelu)
            with act.Fori(0, HALF) as i:
                for k in range(2):
                    e = number(act, i * 2 + k)
                    for f in range(EFC):
                        if f % 2 == 0:
                            act.wait_ge(h_raw, i * 4 + (2 * k + f // 2 + 5))
                        nc.scalar.activation(h[k][:, f, :], H[k][f // 2][:, (f % 2) * GROUP_ROWS:(f % 2 + 1) * GROUP_ROWS], ACT.Gelu,
                                             bias=b1[:, bass.ds(e, 1), f:f + 1].rearrange("p o f -> p (o f)")).then_inc(h_ready, 1)

        @block.vector
        def _(dve):
            dve.wait_ge(w_in, 16 * len(LOADS))

            def turned(j, k):
                dve.wait_ge(zT_raw, j + 3)
                nc.vector.tensor_copy(zT[k][:], T[:].rearrange("p (c r) -> p c r", c=DC)).then_inc(zT_ready, 1)

            def output(j, k, i, first=False):
                e = number(dve, j)
                dve.wait_ge(y_raw, j + 1)
                if not first:
                    dve.wait_ge(y_out[k], i * 16)
                nc.vector.tensor_tensor(y[k][:], Y[k][:].rearrange("p (n d) -> p n d", n=GROUP_TILES),
                                        b2[:, bass.ds(e, 1), :].to_broadcast([P, GROUP_TILES, D]), ALU.add).then_inc(y_ready, 1)

            turned(0, 0)
            turned(1, 1)
            turned(2, 0)
            output(0, 0, 0, True)
            turned(3, 1)
            output(1, 1, 0, True)
            with dve.Fori(1, HALF - 1) as i:
                turned(i * 2 + 2, 0)
                output(i * 2, 0, i)
                turned(i * 2 + 3, 1)
                output(i * 2 + 1, 1, i)
            output(SLOT_GROUPS - 2, 0, HALF - 1)
            output(SLOT_GROUPS - 1, 1, HALF - 1)


def collect_slots(nc, t, s):
    ctx = ExitStack()
    with ctx:
        sem = signals(nc, ctx, "cc_")
        sb = lambda n, shape, dt=FP: ctx.enter_context(nc.sbuf_tensor("cc_" + n, shape, dt))
        Q = 4
        y = [[sb(f"y{q}_{k}", [P, D]) for k in range(CHOSEN)] for q in range(Q)]
        slot = [sb(f"slot{q}", [P, CHOSEN], mybir.dt.uint32) for q in range(Q)]
        added, done, slot_ready, took_wait = (sem(n) for n in ("added", "done", "slot", "took_wait"))
        y_in = [sem(f"y_in{q}") for q in range(Q)]
        block = ctx.enter_context(nc.Block())

        @block.gpsimd
        def _(pool):
            with pool.Fori(0, NT // Q) as i:
                for q in range(Q):
                    pool.wait_ge(slot_ready, i * Q + (q + 1))
                    nc.gpsimd.sem_inc(took_wait, 1)
                    for k in range(CHOSEN):
                        pool.indirect_dma_start(y[q][k][:], None, s["y"], bass.IndirectOffsetOnAxis(ap=slot[q][:, k:k + 1], axis=0)).then_inc(y_in[q], 16)

        @block.vector
        def _(dve):
            def ask(i, q):
                nc.vector.tensor_copy(slot[q][:], s["slot"][:, :, bass.ds(i * Q + q, 1)].rearrange("p k o -> p (k o)")).then_inc(slot_ready, 1)

            def add(i, ask_next):
                x = lambda q: t["X"][:, bass.ds(i * Q + q, 1), :].rearrange("p o d -> p (o d)")
                weight = lambda q, k: s["prob"][:, bass.ds(i * Q + q, 1), k:k + 1].rearrange("p o k -> p (o k)")
                for q in range(Q):
                    dve.wait_ge(y_in[q], (i + 1) * (16 * CHOSEN))
                    nc.vector.scalar_tensor_tensor(x(q), y[q][0][:], weight(q, 0), x(q), ALU.mult, ALU.add).then_inc(added, 1)
                    dve.wait_ge(added, i * Q + (q + 1))
                    nc.vector.scalar_tensor_tensor(x(q), y[q][1][:], weight(q, 1), x(q), ALU.mult, ALU.add).then_inc(done, 1)
                    dve.wait_ge(done, i * Q + (q + 1))
                    if ask_next:
                        ask(i + 1, q)
                    if q % TB == TB - 1:
                        update_stats(nc, t, i * Q + q - (TB - 1), took_wait)

            for q in range(Q):
                ask(0, q)
            with dve.Fori(0, NT // Q - 1) as i:
                add(i, True)
            add(NT // Q - 1, False)


def layer1_rwkv(nc, t, d, bank):
    ctx = ExitStack()
    with ctx:
        sem = signals(nc, ctx, "d_")
        sb = lambda n, shape, dt=FP: ctx.enter_context(nc.sbuf_tensor("d_" + n, shape, dt))
        LANES = range(PAIR)
        w = [sb(f"w{m}", [P, DC, D]) for m in "kvr"]
        wo = sb("wo", [P, DC, D])
        cols = sb("cols", [P, 5, DC])
        decay = sb("decay", [P, DC, S])
        wcol = sb("wcol", [P, DC])
        z = [sb(f"z{p}", [P, TB, D]) for p in LANES]
        zT = [sb(f"zT{p}", [P, DC, S + 1]) for p in LANES]
        diff = [sb(f"diff{p}", [P, DC, S]) for p in LANES]
        mixed = [[sb(f"x{m}{p}", [P, DC, S]) for m in "kvr"] for p in LANES]
        pp = [sb(f"pp{p}", [P, DC, S + 1]) for p in LANES]
        aa = [sb(f"aa{p}", [P, DC, S + 1]) for p in LANES]
        bb = [sb(f"bb{p}", [P, DC, S + 1]) for p in LANES]
        top = [sb(f"top{p}", [P, DC, S]) for p in LANES]
        ex = [sb(f"ex{p}", [P, 4, DC, S]) for p in LANES]
        ev = [sb(f"ev{p}", [P, 2, DC, S]) for p in LANES]
        num = [sb(f"num{p}", [P, DC, S]) for p in LANES]
        den = [sb(f"den{p}", [P, DC, S]) for p in LANES]
        rr = [sb(f"rr{p}", [P, 2, DC, S]) for p in LANES]
        gate = [sb(f"gate{p}", [P, DC, S]) for p in LANES]
        w_in, wexp, setup, took_wait, steps, psteps, asteps = (sem(n) for n in ("w_in", "wexp", "setup", "took_wait", "steps", "psteps", "asteps"))
        z_ready, zT_raw, zT_ready, diff_ready, mixed_ready = (sem(n) for n in ("z", "zT_raw", "zT", "diff", "mixed"))
        kvr_ready, decays_in, decays, firsts_in, firsts = (sem(n) for n in ("kvr", "decays_in", "decays", "firsts_in", "firsts"))
        den_ready, num_ready, soft_ready, lnden_ready, gate_in, gate_ready = (sem(n) for n in ("den", "num", "soft", "lnden", "gate_in", "gate"))
        pool_prev, y_ready, o_raw, x_done = (sem(n) for n in ("pool_prev", "y", "o_raw", "x_done"))
        ev_ready, decay_set = sem("ev"), sem("decay_set")
        K, V, R, O = ((lambda p, j=j: bank[4 * p + j]) for j in range(4))
        halves = lambda b: b[:].rearrange("p (c s) -> p c s", c=DC)
        block = ctx.enter_context(nc.Block())
        ONCE, PER = 1, 8 * PAIR
        PER_POOL = 4
        INIT = 4 * PAIR

        @block.sync
        def _(sp):
            for dst, src in zip(w + [wo, cols], ("dwk", "dwv", "dwr", "dwo", "dcols")):
                sp.dma_start(dst[:], d[src]).then_inc(w_in, 16)

        @block.gpsimd
        def _(pool):
            for p in LANES:
                nc.gpsimd.memset(zT[p][:, :, 0:1], 0.0).then_inc(setup, 1)
                nc.gpsimd.memset(pp[p][:, :, 0:1], -1e30).then_inc(setup, 1)
                nc.gpsimd.memset(aa[p][:, :, 0:1], 0.0).then_inc(setup, 1)
                nc.gpsimd.memset(bb[p][:, :, 0:1], 0.0).then_inc(setup, 1)
            pool.wait_ge(setup, INIT)

            def change(i, p):
                pool.wait_ge(zT_ready, batch_of(i, p))
                nc.gpsimd.tensor_tensor(diff[p][:], zT[p][:, :, 1:S + 1], zT[p][:, :, 0:S], ALU.subtract).then_inc(diff_ready, 1)

            def output(i, p):
                ch = Chain(pool, psteps, PER_POOL, batch_of(i, p) - 1)
                pool.wait_ge(firsts, batch_of(i, p))
                pool.wait_ge(ev_ready, batch_of(i, p))
                ch.did(nc.gpsimd.tensor_tensor(den[p][:], ex[p][:, 2], bb[p][:, :, 0:S], ALU.mult)).see()
                nc.gpsimd.tensor_tensor(den[p][:], den[p][:], ex[p][:, 3], ALU.add).then_inc(den_ready, 1)
                if not isinstance(i, int) or i > 0:
                    pool.wait_ge(o_raw, batch_of(i - 1, p))
                ch.did(nc.gpsimd.tensor_tensor(num[p][:], ex[p][:, 2], aa[p][:, :, 0:S], ALU.mult)).see()
                ch.did(nc.gpsimd.tensor_tensor(num[p][:], num[p][:], ev[p][:, 1], ALU.add))
                pool.wait_ge(lnden_ready, batch_of(i, p))
                pool.wait_ge(gate_in, batch_of(i, p))
                ch.did(nc.gpsimd.tensor_tensor(gate[p][:], gate[p][:], rr[p][:, 1], ALU.subtract)).see()
                nc.gpsimd.sem_inc(pool_prev, 1)
                ch.end()

            def trip(i, more=True):
                output(i, 0)
                if more:
                    for p in LANES:
                        change(i + 1, p)
                output(i, 1)

            for p in LANES:
                change(0, p)
            trip(0)
            with pool.Fori(1, TRIPS - 1) as i:
                trip(i)
            trip(TRIPS - 1, False)

        @block.scalar
        def _(act):
            nc.scalar.preload_act_table_set("natural_log_exp_and_others")
            act.wait_ge(w_in, 80)
            nc.scalar.activation(wcol[:], cols[:, 3, :], ACT.Exp).then_inc(wexp, 1)

            def turned(i, p):
                act.wait_ge(zT_raw, batch_of(i, p))
                nc.scalar.activation(zT[p][:, :, 1:S + 1], halves(K(p)), ACT.Copy).then_inc(zT_ready, 1)

            def scan_inputs(i):
                ch = Chain(act, asteps, 2 * PAIR, i)
                for p in LANES:
                    act.wait_ge(kvr_ready, batch_of(i, p))
                    ch.did(nc.scalar.activation(rr[p][:, 0], halves(R(p)), ACT.Abs)).see()
                    ch.did(nc.scalar.activation(rr[p][:, 0], rr[p][:, 0], ACT.Exp, scale=-1.0)).see()
                    nc.scalar.activation(rr[p][:, 0], rr[p][:, 0], ACT.Ln, bias=1.0).then_inc(soft_ready, 1)
                for p in LANES:
                    act.wait_ge(decays_in, batch_of(i, p))
                    nc.scalar.activation(ex[p][:, 0:2], ex[p][:, 0:2], ACT.Exp).then_inc(decays, 1)
                    act.wait_ge(firsts_in, batch_of(i, p))
                    nc.scalar.activation(ex[p][:, 2:4], ex[p][:, 2:4], ACT.Exp).then_inc(firsts, 1)
                ch.end()

            def ln_den(i, p):
                act.wait_ge(den_ready, batch_of(i, p))
                nc.scalar.activation(rr[p][:, 1], den[p][:], ACT.Ln).then_inc(lnden_ready, 1)

            def gates(i, p):
                act.wait_ge(pool_prev, batch_of(i, p))
                nc.scalar.activation(gate[p][:], gate[p][:], ACT.Exp).then_inc(gate_ready, 1)

            for p in LANES:
                turned(0, p)
            scan_inputs(0)
            with act.Fori(0, TRIPS - 1) as i:
                ln_den(i, 0)
                for p in LANES:
                    turned(i + 1, p)
                gates(i, 0)
                ln_den(i, 1)
                gates(i, 1)
                scan_inputs(i + 1)
            for p in LANES:
                ln_den(TRIPS - 1, p)
                gates(TRIPS - 1, p)

        @block.tensor
        def _(pe):
            pe.wait_ge(w_in, 80)

            def project(i):
                for p in LANES:
                    pe.wait_ge(z_ready, batch_of(i, p) * TB)
                    for c in range(DC):
                        for n in range(TB):
                            last = nc.tensor.transpose(K(p)[:, c * S + n * P:c * S + (n + 1) * P],
                                                       z[p][:, n, c * P:(c + 1) * P], t["ident"][:])
                    last.then_inc(zT_raw, 1)
                for p in LANES:
                    pe.wait_ge(mixed_ready, batch_of(i, p))
                    for m, out in enumerate((K(p), V(p), R(p))):
                        for e in range(DC):
                            for c in range(DC):
                                last = nc.tensor.matmul(out[:, e * S:(e + 1) * S], w[m][:, c, e * P:(e + 1) * P], mixed[p][m][:, c, :],
                                                        start=c == 0, stop=c == DC - 1)
                    last.then_inc(kvr_ready, 1)

            def output(i):
                for p in LANES:
                    pe.wait_ge(y_ready, batch_of(i, p))
                    for n in range(TB):
                        for c in range(DC):
                            last = nc.tensor.matmul(O(p)[:, n * D:(n + 1) * D], num[p][:, c, n * P:(n + 1) * P], wo[:, c, :],
                                                    start=c == 0, stop=c == DC - 1)
                    last.then_inc(o_raw, 1)

            project(0)
            with pe.Fori(0, TRIPS - 1) as i:
                project(i + 1)
                output(i)
            output(TRIPS - 1)

        @block.vector
        def _(dve):
            dve.wait_ge(wexp, 1)
            nc.vector.memset(decay[:], -1.0).then_inc(steps, 1)
            dve.wait_ge(steps, 1)
            for c in range(DC):
                nc.vector.tensor_scalar(decay[:, c, :], decay[:, c, :], wcol[:, c:c + 1], None, ALU.mult).then_inc(decay_set, 1)
            dve.wait_ge(decay_set, DC)
            dve.wait_ge(setup, INIT)
            dve.wait_ge(w_in, 80)

            def normalise(i):
                for p in LANES:
                    tile = (i * PAIR + p) * TB
                    for c in range(TB):
                        nc.vector.tensor_scalar(z[p][:, c, :], t["X"][:, bass.ds(tile + c, 1), :].rearrange("p o d -> p (o d)"),
                                                t["mean"][:, bass.ds(tile + c, 1)], t["rstd"][:, bass.ds(tile + c, 1)],
                                                ALU.subtract, ALU.mult).then_inc(z_ready, 1)

            def mix(i):
                for p in LANES:
                    dve.wait_ge(diff_ready, batch_of(i, p))
                    for m in range(3):
                        for c in range(DC):
                            last = nc.vector.scalar_tensor_tensor(mixed[p][m][:, c, :], diff[p][:, c, :], cols[:, m, c:c + 1],
                                                                  zT[p][:, c, 0:S], ALU.mult, ALU.add)
                    last.then_inc(mixed_ready, 1)

            def scan(i):
                ch = Chain(dve, steps, PER, i, ONCE)
                for p in LANES:
                    k, v, r = halves(K(p)), halves(V(p)), halves(R(p))
                    dve.wait_ge(kvr_ready, batch_of(i, p))
                    for c in range(DC):
                        ch.did(nc.vector.tensor_tensor_scan(pp[p][:, c, 1:S + 1], decay[:, c, :], k[:, c, :], -1e30, ALU.add, ALU.max))
                    ch.see()
                    for c in range(DC):
                        ch.did(nc.vector.scalar_tensor_tensor(top[p][:, c, :], k[:, c, :], cols[:, 4, c:c + 1], pp[p][:, c, 0:S], ALU.add, ALU.max))
                    ch.did(nc.vector.tensor_tensor(ex[p][:, 0], pp[p][:, :, 0:S], decay[:], ALU.add)).see()
                    nc.vector.tensor_tensor(ex[p][:, 1], k, pp[p][:, :, 1:S + 1], ALU.subtract)
                    nc.vector.tensor_tensor(ex[p][:, 0], ex[p][:, 0], pp[p][:, :, 1:S + 1], ALU.subtract).then_inc(decays_in, 1)
                    nc.vector.tensor_tensor(ex[p][:, 2], pp[p][:, :, 0:S], top[p][:], ALU.subtract)
                    for c in range(DC):
                        last = nc.vector.scalar_tensor_tensor(ex[p][:, 3, c, :], k[:, c, :], cols[:, 4, c:c + 1], top[p][:, c, :], ALU.add, ALU.subtract)
                    last.then_inc(firsts_in, 1)
                    dve.wait_ge(soft_ready, batch_of(i, p))
                    nc.vector.scalar_tensor_tensor(gate[p][:], r, 0.0, rr[p][:, 0], ALU.min, ALU.subtract).then_inc(gate_in, 1)
                for p in LANES:
                    v = halves(V(p))
                    dve.wait_ge(decays, batch_of(i, p))
                    ch.did(nc.vector.tensor_tensor(ev[p][:, 0], ex[p][:, 1], v, ALU.mult))
                    for c in range(DC):
                        last = nc.vector.tensor_tensor_scan(bb[p][:, c, 1:S + 1], ex[p][:, 0, c, :], ex[p][:, 1, c, :], 0.0, ALU.mult, ALU.add)
                    ch.see()
                    for c in range(DC):
                        ch.did(nc.vector.tensor_tensor_scan(aa[p][:, c, 1:S + 1], ex[p][:, 0, c, :], ev[p][:, 0, c, :], 0.0, ALU.mult, ALU.add))
                    dve.wait_ge(firsts, batch_of(i, p))
                    nc.vector.tensor_tensor(ev[p][:, 1], ex[p][:, 3], v, ALU.mult).then_inc(ev_ready, 1)
                ch.end()

            def weigh(i):
                for p in LANES:
                    dve.wait_ge(gate_ready, batch_of(i, p))
                    nc.vector.tensor_tensor(num[p][:], num[p][:], gate[p][:], ALU.mult).then_inc(y_ready, 1)

            def add(i):
                for p in LANES:
                    tile = (i * PAIR + p) * TB
                    x = t["X"][:, bass.ds(tile, TB), :]
                    dve.wait_ge(o_raw, batch_of(i, p))
                    nc.vector.tensor_tensor(x, O(p)[:].rearrange("p (c k) -> p c k", c=TB), x, ALU.add).then_inc(x_done, 1)
                    dve.wait_ge(x_done, batch_of(i, p))
                    update_stats(nc, t, tile, took_wait)

            normalise(0)
            mix(0)
            scan(0)
            normalise(1)
            with dve.Fori(0, TRIPS - 2) as i:
                mix(i + 1)
                weigh(i)
                scan(i + 1)
                normalise(i + 2)
                add(i)
            mix(TRIPS - 1)
            weigh(TRIPS - 2)
            scan(TRIPS - 1)
            add(TRIPS - 2)
            weigh(TRIPS - 1)
            add(TRIPS - 1)


def layer1_stablemax(nc, t, d, bank):
    ctx = ExitStack()
    with ctx:
        sem = signals(nc, ctx, "e_")
        sb = lambda n, shape, dt=FP: ctx.enter_context(nc.sbuf_tensor("e_" + n, shape, dt))
        XH, QUADS, SLOTS, RING = 16, 4, 6, 8
        XD = D // XH
        SIDES = range(3)
        wq, wk, wv, wo = (sb("w" + m, [P, DC, D]) for m in "qkvo")
        cols = sb("cols", [P, 3, DC])
        mask = sb("mask", [P, 2])
        bo = sb("bo", [P, D])
        bq4, bkm = sb("bq4", [P, DC]), sb("bkm", [P, 2, DC])
        z, zT = sb("z", [P, TB, D]), sb("zT", [P, DC, S])
        cT = [sb(f"cT{k}", [P, DC, S]) for k in SIDES]
        qT = [sb(f"qT{k}", [P, DC, S]) for k in SIDES]
        kT = [sb(f"kT{k}", [P, 2, DC, S]) for k in SIDES]
        vx = [sb(f"vx{k}", [P, TB, XH, 32]) for k in SIDES]
        low = [sb(f"low{k}", [P, TB, S]) for k in range(RING)]
        st = [sb(f"st{k}", [P, QUADS, TB, S]) for k in range(2)]
        u = sb("u", [P, QUADS, S])
        rec = sb("rec", [P, 2, XH])
        cn = sb("cn", [P, TB, D])
        oT = sb("oT", [P, DC, S])
        names = ("w_in", "setup", "z", "zT", "q", "k", "v", "neg", "ln", "low", "st", "u", "rec", "cn", "oT", "bo", "x_done", "took_wait", "took_pool_wait", "consts")
        (w_in, setup, z_ready, zT_ready, q_ready, k_ready, v_ready, neg_ready, ln_ready, low_ready, st_ready, u_ready, rec_ready,
         cn_ready, oT_ready, bo_added, x_done, took_wait, took_pool_wait, consts) = (sem(n) for n in names)
        c_in = [sem(f"c_in{k}") for k in SIDES]
        full = [sem(f"full{k}") for k in range(8)]
        free = {k: sem(f"free{k}") for k in (6, 7)}
        halves = lambda b: b[:].rearrange("p (c s) -> p c s", c=DC)
        block = ctx.enter_context(nc.Block())
        W_LOADS, SETUP, CONSTS = 7, 2 * len(SIDES), 3

        EXTRA = {0: (("start_z", 6),), 2: (("pv3_before", 7), ("start_q", 6)), 4: (("end_u0", 7), ("end_u1", 6)),
                 6: (("start_k", 7), ("pv0", 6)), 8: (("end_T", 7),), 10: (("end_o", 6), ("pv1", 7)), 12: (("start_v", 6),), 14: (("pv2", 7),)}
        LATER = {0: (("pv2_before", 7),)} | {k + 2: EXTRA[k] for k in range(0, XH - 2, 2)}
        PROLOGUE = (("start_z", 6), ("start_q", 6), ("start_k", 7), ("start_v", 6))
        EPILOGUE = (("pv3_before", 7), ("end_u0", 7), ("end_u1", 6), ("end_T", 7), ("end_o", 6))

        class Batch:

            def __init__(self, trip, side):
                self.trip, self.side, self.n = trip, side, trip * 3 + side

            def next(self):
                return Batch(self.trip, self.side + 1) if self.side < 2 else Batch(self.trip + 1, 0)

            def last(self):
                return Batch(self.trip, self.side - 1) if self.side else Batch(self.trip - 1, 2)

            def head(self, k):
                n = XH * self.side + k
                return n % SLOTS, self.trip * (3 * XH // SLOTS) + n // SLOTS

        def steps(before, after, extra):
            uses = {6: 0, 7: 0}
            for k in range(0, XH, 2):
                yield "heads", k, None, None
                for what, b in extra[k]:
                    if what.startswith("start") and not after or (what.startswith("end") or what.endswith("before")) and not before:
                        continue
                    yield what, k, b, uses[b]
                    uses[b] += 1

        def whole(engine, body, extra=EXTRA):
            uses = {6: 0, 7: 0}

            def run(batch, list_, base=None):
                for what, k, b, n in list_:
                    body(what, k, batch, b, None if b is None else base[b] + n)

            def alone(batch, list_):
                list_ = list(list_)
                run(batch, list_, dict(uses))
                for _, _, b, n in list_:
                    if b is not None:
                        uses[b] += 1

            def beside(list_):
                seen = {6: 0, 7: 0}
                for what, b in list_:
                    yield what, 0, b, seen[b]
                    seen[b] += 1

            alone(Batch(-1, 2), beside(PROLOGUE))
            alone(Batch(0, 0), steps(False, True, extra))
            with engine.Fori(0, B // 3) as i:
                for h in range(3):
                    run(Batch(i, h + 1) if h < 2 else Batch(i + 1, 0), steps(True, True, extra), {b: uses[b] + (i * 18 + 6 * h) for b in uses})
            for b in uses:
                uses[b] += B // 3 * 18
            last = Batch(B // 3, 1)
            alone(last, steps(True, False, extra))
            alone(last.next(), beside((("pv2_before", 7),) * (extra is LATER) + EPILOGUE))

        @block.sync
        def _(sp):
            for dst, src in ((wq, "ewq"), (wk, "ewk"), (wv, "ewv"), (wo, "ewo"), (cols, "ecols"), (mask, "emask"), (bo, "ebo")):
                sp.dma_start(dst[:], d[src]).then_inc(w_in, 16)
            for k in SIDES:
                sp.dma_start(cT[k][:], d["ctxT"][k]).then_inc(c_in[k], 16)
            with sp.Fori(1, B // 3) as i:
                for k in SIDES:
                    sp.wait_ge(v_ready, 3 * i + (k - 2))
                    sp.dma_start(cT[k][:], d["ctxT"][bass.ds(3 * i + k, 1)].rearrange("o p c s -> p (o c) s")).then_inc(c_in[k], 16)
            for n in range(B // 3 * 3, B):
                sp.wait_ge(v_ready, n - 2)
                sp.dma_start(cT[n % 3][:], d["ctxT"][n]).then_inc(c_in[n % 3], 16)

        @block.gpsimd
        def _(pool):
            for k in SIDES:
                nc.gpsimd.memset(vx[k][:, :, :, XD:32], 0.0).then_inc(setup, 1)
            pool.wait_ge(setup, len(SIDES))
            for k in SIDES:
                nc.gpsimd.memset(vx[k][:, :, :, XD:XD + 1], 1.0).then_inc(setup, 1)
            pool.wait_ge(w_in, 16 * W_LOADS)
            nc.gpsimd.tensor_scalar(bq4[:], cols[:, 0, :], 0.25, None, ALU.mult).then_inc(consts, 1)
            for h in range(2):
                nc.gpsimd.tensor_scalar(bkm[:, h, :], cols[:, 1, :], mask[:, h:h + 1], None, ALU.mult).then_inc(consts, 1)
            with pool.Fori(0, B) as b:
                pool.wait_ge(z_ready, (b + 1) * TB)
                nc.gpsimd.sem_inc(took_pool_wait, 1)
                x = t["X"][:, bass.ds(b * TB, TB), :]
                nc.gpsimd.tensor_tensor(x, x, bo[:, None, :].to_broadcast([P, TB, D]), ALU.add).then_inc(bo_added, 1)

        @block.scalar
        def _(act):
            nc.scalar.preload_act_table_set("natural_log_exp_and_others")
            act.wait_ge(w_in, 16 * W_LOADS)
            act.wait_ge(setup, SETUP)
            act.wait_ge(consts, CONSTS)

            def body(what, k, batch, slot, before):
                b, after, other = batch.n, batch.n + 1, batch.next().side
                here = None if slot is None else bank[slot]
                if what == "heads":
                    for k in (k, k + 1):
                        n = XH * b + (k + 1)
                        act.wait_ge(neg_ready, n)
                        nc.scalar.activation(low[k % RING][:], low[k % RING][:], ACT.Ln, bias=1.0).then_inc(ln_ready, 1)
                    for k in (k - 1, k):
                        act.wait_ge(ln_ready, XH * b + (k + 1))
                        nc.scalar.activation(low[k % RING][:], low[k % RING][:], ACT.Exp, scale=-1.0).then_inc(low_ready, 1)
                if what != "heads" and what not in ("end_u0", "end_u1", "end_o"):
                    act.wait_ge(full[slot], before + 1)
                if what == "start_z":
                    nc.scalar.activation(zT[:], halves(here), ACT.Copy).then_inc(zT_ready, 1)
                    act.wait_ge(zT_ready, after + 1)
                    act.sem_inc(free[slot], 1)
                if what == "start_q":
                    for c in range(DC):
                        nc.scalar.activation(qT[other][:, c, :], here[:, c * S:(c + 1) * S], ACT.Identity,
                                             bias=bq4[:, c:c + 1], scale=0.25).then_inc(q_ready, 1)
                    act.wait_ge(q_ready, (after + 1) * DC)
                    act.sem_inc(free[slot], 1)
                if what == "start_k":
                    for h in range(2):
                        for c in range(DC):
                            nc.scalar.activation(kT[other][:, h, c, :], here[:, c * S:(c + 1) * S], ACT.Identity,
                                                 bias=bkm[:, h, c:c + 1], scale=mask[:, h:h + 1]).then_inc(k_ready, 1)
                    act.wait_ge(k_ready, (after + 1) * 2 * DC)
                    act.sem_inc(free[slot], 1)
                if what == "start_v":
                    nc.scalar.activation(vx[other][:, :, :, 0:XD], here[:].rearrange("p (n h e) -> p n h e", n=TB, h=XH), ACT.Copy).then_inc(v_ready, 1)
                    act.wait_ge(v_ready, after + 1)
                    act.sem_inc(free[slot], 1)
                if what.startswith("pv"):
                    quad, of = (QUADS - 1, b - 1) if what == "pv3_before" else (int(what[2]), b)
                    nc.scalar.activation(u[:, quad, :], here[:, 0:S], ACT.Copy).then_inc(u_ready, 1)
                    act.wait_ge(u_ready, QUADS * of + (quad + 1))
                    act.sem_inc(free[slot], 1)
                if what == "end_T":
                    for c in range(DC):
                        nc.scalar.activation(oT[:, c, :], here[:, c * S:(c + 1) * S], ACT.Identity, bias=cols[:, 2, c:c + 1]).then_inc(oT_ready, 1)
                    act.wait_ge(oT_ready, b * DC)
                    act.sem_inc(free[slot], 1)

            whole(act, body)

        @block.tensor
        def _(pe):
            pe.wait_ge(w_in, 16 * W_LOADS)

            def body(what, k, batch, slot, before):
                b, side, after, other = batch.n, batch.side, batch.n + 1, batch.next().side
                here = None if slot is None else bank[slot]
                if what == "heads":
                    if k == 0:
                        pe.wait_ge(q_ready, (b + 1) * DC)
                        pe.wait_ge(k_ready, (b + 1) * 2 * DC)
                    slots = [batch.head(k + j) for j in range(2)]
                    read = XH * b + k - (SLOTS - 2)
                    if not isinstance(read, int) or read > 0:
                        pe.wait_ge(st_ready, read)
                    for c2 in range(TB):
                        for j in range(2):
                            quad, r = (k + j) // 4, (k + j) % 4
                            c, e, rows_ = quad // 2, quad % 2, slice(32 * r, 32 * r + 32)
                            last = nc.tensor.matmul(bank[slots[j][0]][:, c2 * S:(c2 + 1) * S], kT[side][rows_, e, c, c2 * P:(c2 + 1) * P],
                                                    qT[side][rows_, c, :], start=True, stop=True)
                            if c2 == TB - 1:
                                last.then_inc(full[slots[j][0]], 1)
                if what != "heads":
                    pe.wait_ge(free[slot], before)
                if what == "start_z":
                    pe.wait_ge(z_ready, (after + 1) * TB)
                    for c in range(DC):
                        for n in range(TB):
                            last = nc.tensor.transpose(here[:, c * S + n * P:c * S + (n + 1) * P], z[:, n, c * P:(c + 1) * P], t["ident"][:])
                if what in ("start_q", "start_k"):
                    if what == "start_q":
                        pe.wait_ge(zT_ready, after + 1)
                    else:
                        pe.wait_ge(c_in[other], (batch.next().trip + 1) * 16)
                    w, x = (wq, zT) if what == "start_q" else (wk, cT[other])
                    for e in range(DC):
                        for c in range(DC):
                            last = nc.tensor.matmul(here[:, e * S:(e + 1) * S], w[:, c, e * P:(e + 1) * P], x[:, c, :], start=c == 0, stop=c == DC - 1)
                if what == "start_v":
                    for n in range(TB):
                        for c in range(DC):
                            last = nc.tensor.matmul(here[:, n * D:(n + 1) * D], cT[other][:, c, n * P:(n + 1) * P], wv[:, c, :], start=c == 0, stop=c == DC - 1)
                if what.startswith("pv"):
                    quad, of, s_ = int(what[2]), b, side
                    if what.endswith("before"):
                        of, s_ = b - 1, batch.last().side
                    pe.wait_ge(st_ready, XH * of + 4 * (quad + 1))
                    if quad == 0:
                        pe.wait_ge(v_ready, of + 1)
                    for c2 in range(TB):
                        for r in range(4):
                            last = nc.tensor.matmul(here[32 * r:32 * r + 32, 0:S], vx[s_][:, c2, 4 * quad + r, :],
                                                    st[quad % 2][:, r, c2, :], start=c2 == 0, stop=c2 == TB - 1)
                    last.then_inc(full[slot], 1)
                if what in ("end_u0", "end_u1"):
                    n = int(what[5])
                    pe.wait_ge(u_ready, b * QUADS)
                    for quad in range(QUADS):
                        last = nc.tensor.transpose(here[:, quad * P:(quad + 1) * P], u[:, quad, n * P:(n + 1) * P], t["ident"][:])
                if what == "end_T":
                    pe.wait_ge(cn_ready, b * TB)
                    for c in range(DC):
                        for n in range(TB):
                            last = nc.tensor.transpose(here[:, c * S + n * P:c * S + (n + 1) * P], cn[:, n, c * P:(c + 1) * P], t["ident"][:])
                if what == "end_o":
                    pe.wait_ge(oT_ready, b * DC)
                    for n in range(TB):
                        for c in range(DC):
                            last = nc.tensor.matmul(here[:, n * D:(n + 1) * D], oT[:, c, n * P:(n + 1) * P], wo[:, c, :], start=c == 0, stop=c == DC - 1)
                if what != "heads" and not what.startswith("pv"):
                    last.then_inc(full[slot], 1)

            whole(pe, body, LATER)

        @block.vector
        def _(dve):
            row = lambda n: t["X"][:, bass.ds(n, 1), :].rearrange("p o d -> p (o d)")
            stat = lambda name, n: t[name][:, bass.ds(n, 1)]

            def weigh(k, batch):
                slot, _ = batch.head(k)
                n = XH * batch.n + (k + 1)
                dve.wait_ge(low_ready, n)
                if not (isinstance(batch.n, int) and batch.n == 0 and k < 8):
                    dve.wait_ge(u_ready, QUADS * batch.n + (k // 4 - 1))
                nc.vector.scalar_tensor_tensor(st[(k // 4) % 2][:, k % 4].rearrange("p n s -> p (n s)"), bank[slot][:], 0.0,
                                               low[k % RING][:].rearrange("p n s -> p (n s)"), ALU.max, ALU.add).then_inc(st_ready, 1)

            def body(what, k, batch, slot, before):
                b = batch.n
                here = None if slot is None else bank[slot]
                if what == "heads":
                    read = XH * b + k - (RING - 2)
                    if not isinstance(read, int) or read > 0:
                        dve.wait_ge(st_ready, read)
                    for j in range(2):
                        s_, n = batch.head(k + j)
                        dve.wait_ge(full[s_], n + 1)
                        nc.vector.tensor_scalar(low[(k + j) % RING][:].rearrange("p n s -> p (n s)"), bank[s_][:], -1.0, 0.0, ALU.mult, ALU.max).then_inc(neg_ready, 1)
                    for j in range(2):
                        if k:
                            weigh(k - 2 + j, batch)
                        elif not (isinstance(b, int) and b == 0):
                            weigh(XH - 2 + j, batch.last())
                if what == "pv3_before" and isinstance(b, int) and b == B:
                    for j in range(2):
                        weigh(XH - 2 + j, batch.last())
                if what == "start_z":
                    tile = (b + 1) * TB
                    for c in range(TB):
                        nc.vector.tensor_scalar(z[:, c, :], row(tile + c), stat("mean", tile + c), stat("rstd", tile + c),
                                                ALU.subtract, ALU.mult).then_inc(z_ready, 1)
                if what in ("end_u0", "end_u1"):
                    n = int(what[5])
                    by_head = here[:].rearrange("p (h e) -> p h e", h=XH)
                    dve.wait_ge(full[slot], before + 1)
                    nc.vector.reciprocal(rec[:, n, :], by_head[:, :, XD]).then_inc(rec_ready, 1)
                    dve.wait_ge(rec_ready, (b - 1) * TB + (n + 1))
                    nc.vector.tensor_tensor(cn[:, n, :].rearrange("p (h e) -> p h e", h=XH), by_head[:, :, 0:XD],
                                            rec[:, n, :, None].to_broadcast([P, XH, XD]), ALU.mult).then_inc(cn_ready, 1)
                    dve.wait_ge(cn_ready, (b - 1) * TB + (n + 1))
                    dve.sem_inc(free[slot], 1)
                if what == "end_o":
                    tile = (b - 1) * TB
                    x = t["X"][:, bass.ds(tile, TB), :]
                    dve.wait_ge(full[slot], before + 1)
                    dve.wait_ge(bo_added, b)
                    nc.vector.tensor_tensor(x, halves(here), x, ALU.add).then_inc(x_done, 1)
                    dve.wait_ge(x_done, b)
                    nc.vector.sem_inc(free[slot], 1)
                    update_stats(nc, t, tile, took_wait)

            whole(dve, body)


FF = 1024
FC = FF // P
MAGIC = 1.5 * 2.0 ** 23
ALL_MAX = bass.bass_isa.ReduceOp.max


def layer1_ffn(nc, t, d, bank):
    ctx = ExitStack()
    with ctx:
        sb = lambda n, shape, dt=FP: ctx.enter_context(nc.sbuf_tensor("f_" + n, shape, dt))
        s = {"win": sb("win", [P, DC, FF], BF), "wout": sb("wout", [P, FC, D]), "cols": sb("cols", [P, 3, FC]),
             "bo": sb("bo", [P, D]), "scale": sb("scale", [P, 8]), "top": sb("top", [P, 1])}
        hidden = nc.dram_tensor("hidden", (B, P, FC, S), FP).ap()
        ffn_weights(nc, t, d, bank, s)
        ffn_up(nc, t, d, bank, s, hidden)
        ffn_down(nc, t, d, bank, s, hidden)


def ffn_weights(nc, t, d, bank, s):
    ctx = ExitStack()
    with ctx:
        sem = signals(nc, ctx, "fw_")
        sb = lambda n, shape, dt=FP: ctx.enter_context(nc.sbuf_tensor("fw_" + n, shape, dt))
        w = [sb("wi", [P, FC, D]), s["wout"]]
        hi, lo, amax, inv = (sb(n, [P, 2, FC]) for n in ("hi", "lo", "amax", "inv"))
        xhi, xlo = sb("xhi", [P, NT]), sb("xlo", [P, NT])
        top, topall = sb("top", [P, 1]), sb("topall", [P, 1])
        w_in, steps, wi_ready, wT_raw, wT_ready, top_ready, all_ready = (sem(n) for n in ("w_in", "steps", "wi", "wT_raw", "wT", "top", "all"))
        block = ctx.enter_context(nc.Block())
        QUARTERS = 4

        @block.sync
        def _(sp):
            for dst, src in ((w[0], "fwi"), (w[1], "fwo"), (s["bo"], "fbo")):
                sp.dma_start(dst[:], d[src]).then_inc(w_in, 16)
            sp.dma_start(s["cols"][:, 0, :], d["fbi"]).then_inc(w_in, 16)

        @block.tensor
        def _(pe):
            pe.wait_ge(wi_ready, 1)
            for c in range(DC):
                for f in range(FC):
                    last = nc.tensor.transpose(bank[2 * c + f // 4][:, (f % 4) * P:(f % 4 + 1) * P], w[0][:, f, c * P:(c + 1) * P], t["ident"][:])
            last.then_inc(wT_raw, 1)

        @block.scalar
        def _(act):
            act.wait_ge(wT_raw, 1)
            for k in range(2 * DC):
                c, part = k // 2, slice((k % 2) * 512, (k % 2 + 1) * 512)
                last = nc.scalar.activation(s["win"][:, c, part], bank[k][:], ACT.Copy)
            last.then_inc(wT_ready, 1)

        @block.gpsimd
        def _(pool):
            pool.wait_ge(top_ready, 1)
            nc.gpsimd.partition_all_reduce(topall[:], top[:], P, ALL_MAX).then_inc(all_ready, 1)

        @block.vector
        def _(dve):
            ch = Chain(dve, steps, 29)
            dve.wait_ge(w_in, 64)
            for k in range(2):
                ch.did(nc.vector.tensor_reduce(hi[:, k, :], w[k][:], AX.X, ALU.max))
                ch.did(nc.vector.tensor_reduce(lo[:, k, :], w[k][:], AX.X, ALU.min))
            ch.see()
            ch.did(nc.vector.scalar_tensor_tensor(amax[:], lo[:], -1.0, hi[:], ALU.mult, ALU.max)).see()
            ch.did(nc.vector.tensor_scalar(amax[:], amax[:], 1e-8, None, ALU.max)).see()
            ch.did(nc.vector.reciprocal(inv[:], amax[:])).see()
            ch.did(nc.vector.tensor_scalar(inv[:], inv[:], 127.0, None, ALU.mult))
            ch.did(nc.vector.tensor_scalar(amax[:], amax[:], 1.0 / 127.0, None, ALU.mult)).see()
            for k in range(2):
                by = lambda a: a[:, k, :, None].to_broadcast([P, FC, D])
                ch.did(nc.vector.tensor_tensor(w[k][:], w[k][:], by(inv), ALU.mult)).see()
                last = nc.vector.tensor_scalar(w[k][:], w[k][:], MAGIC, MAGIC, ALU.add, ALU.subtract)
                if k == 0:
                    last.then_inc(wi_ready, 1)
                else:
                    ch.did(last).see()
                    ch.did(nc.vector.tensor_tensor(w[k][:], w[k][:], by(amax), ALU.mult))
            for q in range(QUARTERS):
                part = slice(q * NT // QUARTERS, (q + 1) * NT // QUARTERS)
                ch.did(nc.vector.tensor_reduce(xhi[:, part], t["X"][:, part, :], AX.X, ALU.max))
                ch.did(nc.vector.tensor_reduce(xlo[:, part], t["X"][:, part, :], AX.X, ALU.min))
            ch.see()
            nc.vector.tensor_tensor(xhi[:], xhi[:], t["mean"][:], ALU.subtract)
            ch.did(nc.vector.tensor_tensor(xlo[:], t["mean"][:], xlo[:], ALU.subtract)).see()
            ch.did(nc.vector.tensor_tensor(xhi[:], xhi[:], xlo[:], ALU.max)).see()
            ch.did(nc.vector.tensor_tensor(xhi[:], xhi[:], t["rstd"][:], ALU.mult)).see()
            nc.vector.tensor_reduce(top[:], xhi[:], AX.X, ALU.max).then_inc(top_ready, 1)
            dve.wait_ge(all_ready, 1)
            sx, isx = s["scale"][:, 0:1], s["scale"][:, 1:2]
            quantiser(nc, ch, topall, sx, isx)
            ch.did(nc.vector.tensor_scalar(s["cols"][:, 1, :], amax[:, 0, :], isx, None, ALU.mult)).see()
            dve.wait_ge(wT_ready, 1)
            ch.end()


def quantiser(nc, ch, top, scale, inverse):
    ch.did(nc.vector.tensor_scalar(top[:], top[:], 1e-8, None, ALU.max)).see()
    ch.did(nc.vector.reciprocal(scale, top[:]))
    ch.did(nc.vector.tensor_scalar(inverse, top[:], 1.0 / 32767.0, None, ALU.mult)).see()
    ch.did(nc.vector.tensor_scalar(scale, scale, 32767.0, None, ALU.mult)).see()


def ffn_up(nc, t, d, bank, s, hidden):
    ctx = ExitStack()
    with ctx:
        sem = signals(nc, ctx, "fu_")
        sb = lambda n, shape, dt=FP: ctx.enter_context(nc.sbuf_tensor("fu_" + n, shape, dt))
        LANES = range(PAIR)
        z = [sb(f"z{p}", [P, TB, D]) for p in LANES]
        zq = [[sb(f"z{part}{p}", [P, TB, D], BF) for p in LANES] for part in ("hi", "lo")]
        zT = [[sb(f"zT{part}{p}", [P, DC, S], BF) for p in LANES] for part in ("hi", "lo")]
        h = [sb(f"h{p}", [P, FC, S]) for p in LANES]
        square = sb("square", [P, FC, S])
        one = sb("one", [P, PAIR])
        one_ready, took_wait, z1, hi_ready = (sem(n) for n in ("one", "took_wait", "z1", "hi"))
        z0, z_ready, zT_raw, zT_ready, h_raw, h_ready, top_ready, setup = (sem(n) for n in ("z0", "z", "zT_raw", "zT", "h_raw", "h", "top", "setup"))
        stored = [sem(f"stored{p}") for p in LANES]
        T = lambda p, part: bank[4 * p + part]
        halves = lambda b: b[:].rearrange("p (c s) -> p c s", c=DC)
        block = ctx.enter_context(nc.Block())

        @block.sync
        def _(sp):
            for p in LANES:
                sp.sem_inc(stored[p], 16)
            with sp.Fori(0, TRIPS) as i:
                for p in LANES:
                    sp.wait_ge(h_ready, (batch_of(i, p) + 1) * FC + 1)
                    sp.dma_start(hidden[bass.ds(i * PAIR + p, 1)].rearrange("o p c s -> p (o c) s"), h[p][:]).then_inc(stored[p], 16)
            for p in LANES:
                sp.wait_ge(stored[p], 16 * (TRIPS + 1))

        @block.scalar
        def _(act):
            nc.scalar.preload_act_table(ACT.Gelu)
            act.sem_inc(h_ready, FC + 1)

            def turned(i, p):
                act.wait_ge(zT_raw, batch_of(i, p))
                for part in range(2):
                    nc.scalar.activation(zT[part][p][:], halves(T(p, part)), ACT.Copy).then_inc(zT_ready, 1)

            def gelu(i, p):
                act.wait_ge(h_raw, batch_of(i, p))
                act.wait_ge(stored[p], (i + 1) * 16)
                act.wait_ge(top_ready, batch_of(i, p))
                for f in range(FC):
                    nc.scalar.activation(h[p][:, f, :], bank[4 * p + f // 2][:, (f % 2) * S:(f % 2 + 1) * S], ACT.Gelu,
                                         bias=s["cols"][:, 0, f:f + 1], scale=s["cols"][:, 1, f:f + 1]).then_inc(h_ready, 1)

            turned(0, 0)
            with act.Fori(0, TRIPS - 1) as i:
                turned(i, 1)
                gelu(i, 0)
                turned(i + 1, 0)
                gelu(i, 1)
            turned(TRIPS - 1, 1)
            gelu(TRIPS - 1, 0)
            gelu(TRIPS - 1, 1)

        @block.tensor
        def _(pe):
            AHEAD = 5

            def turn(i, p):
                pe.wait_ge(z_ready, batch_of(i, p))
                pe.wait_ge(h_ready, batch_of(i, p) * FC - (FC - 1))
                for part in range(2):
                    for c in range(DC):
                        for n in range(TB):
                            last = nc.tensor.matmul(T(p, part)[:, c * S + n * P:c * S + (n + 1) * P],
                                                    zq[part][p][:, n, c * P:(c + 1) * P], t["identb"][:], start=True, stop=True)
                last.then_inc(zT_raw, 1)

            def up(i, p, following):
                pe.wait_ge(zT_ready, batch_of(i, p) * 2)
                for f in range(FC):
                    for c in range(DC):
                        for part in range(2):
                            last = nc.tensor.matmul(bank[4 * p + f // 2][:, (f % 2) * S:(f % 2 + 1) * S], s["win"][:, c, f * P:(f + 1) * P],
                                                    zT[part][p][:, c, :], start=c + part == 0, stop=c + part == DC)
                    if f == AHEAD and following:
                        turn(*following)
                last.then_inc(h_raw, 1)

            turn(0, 0)
            with pe.Fori(0, TRIPS - 1) as i:
                up(i, 0, (i, 1))
                up(i, 1, (i + 1, 0))
            up(TRIPS - 1, 0, (TRIPS - 1, 1))
            up(TRIPS - 1, 1, None)

        @block.vector
        def _(dve):
            nc.vector.memset(s["top"][:], 0.0).then_inc(setup, 1)
            nc.vector.sem_inc(top_ready, PAIR)
            dve.wait_ge(setup, 1)
            def rounded(i):
                for p in LANES:
                    if not isinstance(i, int):
                        dve.wait_ge(zT_raw, batch_of(i - 1, p))
                    tile = (i * PAIR + p) * TB
                    for c in range(TB):
                        nc.vector.tensor_scalar(z[p][:, c, :], t["X"][:, bass.ds(tile + c, 1), :].rearrange("p o d -> p (o d)"),
                                                t["mean"][:, bass.ds(tile + c, 1)], t["rstd"][:, bass.ds(tile + c, 1)],
                                                ALU.subtract, ALU.mult).then_inc(z0, 1)
                    dve.wait_ge(z0, batch_of(i, p) * TB)
                    for c in range(TB):
                        nc.vector.tensor_scalar(z[p][:, c, :], z[p][:, c, :], s["scale"][:, 0:1], MAGIC, ALU.mult, ALU.add).then_inc(z1, 1)
                    dve.wait_ge(z1, batch_of(i, p) * TB)
                    nc.vector.tensor_scalar(zq[0][p][:], z[p][:], MAGIC, None, ALU.subtract).then_inc(hi_ready, 1)
                    dve.wait_ge(hi_ready, batch_of(i, p))
                    nc.vector.scalar_tensor_tensor(zq[1][p][:], z[p][:], MAGIC, zq[0][p][:], ALU.subtract, ALU.subtract).then_inc(z_ready, 1)

            def largest(i):
                for p in LANES:
                    dve.wait_ge(h_ready, (batch_of(i, p) + 1) * FC + 1)
                    flat = h[p][:].rearrange("p c s -> p (c s)")
                    dve.wait_ge(top_ready, batch_of(i, p) + 1)
                    nc.vector.sem_inc(took_wait, 1)
                    nc.vector.tensor_tensor_reduce(out=square[:].rearrange("p c s -> p (c s)"), in0=flat, in1=flat, scale=1.0, scalar=0.0,
                                                   op0=ALU.mult, op1=ALU.max, accum_out=one[:, p:p + 1]).then_inc(one_ready, 1)
                    dve.wait_ge(one_ready, batch_of(i, p))
                    nc.vector.tensor_tensor(s["top"][:], s["top"][:], one[:, p:p + 1], ALU.max).then_inc(top_ready, 1)

            rounded(0)
            with dve.Fori(0, TRIPS - 1) as i:
                rounded(i + 1)
                largest(i)
            largest(TRIPS - 1)


def ffn_down(nc, t, d, bank, s, hidden):
    ctx = ExitStack()
    with ctx:
        sem = signals(nc, ctx, "fd_")
        sb = lambda n, shape, dt=FP: ctx.enter_context(nc.sbuf_tensor("fd_" + n, shape, dt))
        LANES = range(PAIR)
        h = [sb(f"h{p}", [P, FC, S]) for p in LANES]
        q = [sb(f"q{p}", [P, FC, S]) for p in LANES]
        top, topall = sb("top", [P, 1]), sb("topall", [P, 1])
        steps, all_ready, root, q0, q_ready, o_raw, x_done, bo_added, took_pool_wait = (
            sem(n) for n in ("steps", "all", "root", "q0", "q", "o_raw", "x_done", "bo", "took_pool_wait"))
        h_in = [sem(f"h_in{p}") for p in LANES]
        O = lambda p: bank[p]
        block = ctx.enter_context(nc.Block())

        @block.sync
        def _(sp):
            with sp.Fori(0, TRIPS) as i:
                for p in LANES:
                    sp.wait_ge(q0, batch_of(i, p))
                    sp.dma_start(h[p][:], hidden[bass.ds(i * PAIR + p, 1)].rearrange("o p c s -> p (o c) s")).then_inc(h_in[p], 16)

        @block.gpsimd
        def _(pool):
            nc.gpsimd.partition_all_reduce(topall[:], s["top"][:], P, ALL_MAX).then_inc(all_ready, 1)
            with pool.Fori(0, B) as b:
                x = t["X"][:, bass.ds(b * TB, TB), :]
                nc.gpsimd.tensor_tensor(x, x, s["bo"][:, None, :].to_broadcast([P, TB, D]), ALU.add).then_inc(bo_added, 1)

        @block.scalar
        def _(act):
            act.wait_ge(all_ready, 1)
            nc.scalar.activation(top[:], topall[:], ACT.Sqrt).then_inc(root, 1)

        @block.tensor
        def _(pe):
            nc.tensor.sem_inc(o_raw, PAIR)
            with pe.Fori(0, TRIPS) as i:
                for p in LANES:
                    pe.wait_ge(q_ready, batch_of(i, p))
                    pe.wait_ge(x_done, batch_of(i, p))
                    for n in range(TB):
                        for f in range(FC):
                            last = nc.tensor.matmul(O(p)[:, n * D:(n + 1) * D], q[p][:, f, n * P:(n + 1) * P], s["wout"][:, f, :],
                                                    start=f == 0, stop=f == FC - 1)
                    last.then_inc(o_raw, 1)

        @block.vector
        def _(dve):
            dve.wait_ge(root, 1)
            ch = Chain(dve, steps, 4)
            sh, ish = s["scale"][:, 2:3], s["scale"][:, 3:4]
            quantiser(nc, ch, top, sh, ish)
            ch.end()
            nc.vector.sem_inc(q0, PAIR)
            nc.vector.sem_inc(x_done, PAIR)

            def whole_numbers(i, p):
                dve.wait_ge(h_in[p], (i + 1) * 16)
                dve.wait_ge(o_raw, batch_of(i, p))
                nc.vector.tensor_scalar(q[p][:], h[p][:], sh, MAGIC, ALU.mult, ALU.add).then_inc(q0, 1)
                dve.wait_ge(q0, batch_of(i, p) + PAIR)
                nc.vector.tensor_scalar(q[p][:], q[p][:], MAGIC, None, ALU.subtract).then_inc(q_ready, 1)

            def add(i, p):
                x = t["X"][:, bass.ds((i * PAIR + p) * TB, TB), :]
                dve.wait_ge(o_raw, batch_of(i, p) + PAIR)
                dve.wait_ge(bo_added, batch_of(i, p))
                nc.vector.scalar_tensor_tensor(x, O(p)[:].rearrange("p (c k) -> p c k", c=TB), ish, x, ALU.mult, ALU.add).then_inc(x_done, 1)

            for p in LANES:
                whole_numbers(0, p)
            with dve.Fori(0, TRIPS - 1) as i:
                for p in LANES:
                    whole_numbers(i + 1, p)
                    add(i, p)
            for p in LANES:
                add(TRIPS - 1, p)
            dve.wait_ge(x_done, B + PAIR)


def store_everything(nc, t, out):
    ctx = ExitStack()
    with ctx:
        x_out = signals(nc, ctx, "st_")("x_out")
        block = ctx.enter_context(nc.Block())
        view = out.rearrange("(n p) d -> p n d", p=P)
        PARTS = 4

        @block.sync
        def _(sp):
            for q in range(PARTS):
                n0 = q * NT // PARTS
                sp.dma_start(view[:, n0:n0 + NT // PARTS, :], t["X"][:, n0:n0 + NT // PARTS, :]).then_inc(x_out, 16)
            sp.wait_ge(x_out, 16 * PARTS)


def build(nc, d, out):
    ctx = ExitStack()
    with ctx:
        sb = lambda n, shape, dt=FP: ctx.enter_context(nc.sbuf_tensor(n, shape, dt))
        t = {"X": sb("X", [P, NT, D]), "mean": sb("mean", [P, NT]), "var": sb("var", [P, NT]), "rstd": sb("rstd", [P, NT]),
             "bn": sb("bn", [P, NT, 6]), "eps": sb("eps", [P, 1]), "ident": sb("ident", [P, P]),
             "identb": sb("identb", [P, P], BF), "maskneg": sb("maskneg", [P, 3 * P], BF)}
        bank = [ctx.enter_context(nc.psum_tensor(f"bank{k}", [P, 512], FP)) for k in range(8)]
        load_everything(nc, t, d)
        LAYERS = [layer0_attention, layer0_mlstm, layer0_experts, layer1_rwkv, layer1_stablemax, layer1_ffn]
        for n, layer in enumerate(LAYERS):
            row_stats(nc, t, f"ln{n}")
            layer(nc, t, d, bank)
        store_everything(nc, t, out)


def kernel(**inputs):
    import numpy as np
    import ml_dtypes
    import concourse.bacc as bacc
    from concourse.bass_utils import run_bass_kernel_spmd

    a = {k: np.asarray(v) for k, v in inputs.items()}

    def by_rows(w):
        return w.reshape(w.shape[0] // P, P, -1).transpose(1, 0, 2)

    def column(v):
        return v.reshape(-1, P).T

    def rows(v):
        return np.broadcast_to(v.reshape(1, -1), (P, v.size))

    qkv, qkv_b = a["L0_attn_qkv_w"], a["L0_attn_qkv_b"]
    key, token = np.arange(P)[:, None], np.arange(P)[None, :]
    causal = np.where(key > token, -1e30, 0.0)
    mask = np.concatenate([causal, np.zeros((P, P)), causal], 1)

    def gate_weights(w):
        g = np.zeros((P, 3 * DC, 2, 32), np.float32)
        by = w.reshape(2, HEADS, 3 * DC, P).transpose(3, 2, 0, 1)
        g[..., 0:HEADS] = by
        g[..., HEADS:2 * HEADS] = by
        return g

    gate_bias = np.zeros((LANES4, 32, 2), np.float32)
    gate_bias[:, 0:HEADS] = gate_bias[:, HEADS:2 * HEADS] = a["L0_xattn_ifgate_b"].reshape(2, HEADS).T
    gate_bias = gate_bias.reshape(P, 2)
    r, h = np.arange(P)[:, None] % 32, np.arange(HEADS)[None, :]
    gate_rows = np.concatenate([r < HEADS, -1.0 * ((r >= HEADS) & (r < 2 * HEADS)), r == HEADS + h, r == h], 1).astype(np.float32)
    quad_order = np.arange(D).reshape(2, 4, 2, 16).transpose(0, 2, 1, 3).reshape(-1)
    data = {
        "x": a["x"].reshape(B * S, D),
        "ident": np.eye(P, dtype=np.float32),
        "identb": np.eye(P).astype(ml_dtypes.bfloat16),
        "maskneg": mask.astype(ml_dtypes.bfloat16),
        "wqk": by_rows(qkv[:2 * D].T), "wv": by_rows(qkv[2 * D:].T), "wproj": by_rows(a["L0_attn_proj_w"].T),
        "acols": np.stack([column(a["L0_attn_norm_w"]), column(a["L0_attn_norm_b"]), column(qkv_b[2 * D:])], 1),
        "bqk": rows(qkv_b[:2 * D]), "bproj": rows(a["L0_attn_proj_b"]),
        "dwk": by_rows(a["L1_attn_Wk"].T), "dwv": by_rows(a["L1_attn_Wv"].T), "dwr": by_rows(a["L1_attn_Wr"].T),
        "dwo": by_rows(a["L1_attn_Wo"].T),
        "dcols": np.stack([column(a["L1_attn_" + n]) for n in ("time_mix_k", "time_mix_v", "time_mix_r", "time_decay", "time_first")], 1),
        "gw": gate_weights(a["L0_xattn_ifgate_w"]), "gbias": gate_bias, "grows": gate_rows,
        "bheads": (key // HD == np.arange(P // HD)[None, :]).astype(np.float32), "outnorm": rows(a["L0_xattn_outnorm_w"]),
        "ctx": a["ctx_1024"].reshape(B, TB, P, D).transpose(0, 2, 1, 3),
        "ctxT": a["ctx_1024"].transpose(0, 2, 1).reshape(B, DC, P, S).transpose(0, 2, 1, 3),
        "ewq": by_rows(a["L1_xattn_Wq"].T), "ewk": by_rows(a["L1_xattn_Wk"].T),
        "ewv": by_rows(a["L1_xattn_Wv"].T[:, quad_order]), "ewo": by_rows(a["L1_xattn_Wo"].T[quad_order]),
        "ecols": np.stack([column(a["L1_xattn_bq"]), column(a["L1_xattn_bk"]), column(a["L1_xattn_bv"][quad_order])], 1),
        "emask": np.concatenate([r < 16, r >= 16], 1).astype(np.float32), "ebo": rows(a["L1_xattn_bo"]),
        "fwi": by_rows(a["L1_ffn_W_in"].T), "fwo": by_rows(a["L1_ffn_W_out"]), "fbi": column(a["L1_ffn_b_in"]),
        "fbo": rows(a["L1_ffn_b_out"]),
        "cw1": a["L0_ffn_w1"].transpose(0, 2, 1).reshape(EX, DC, P, EF).transpose(0, 2, 1, 3),
        "cw2": a["L0_ffn_w2"].transpose(2, 0, 1).reshape(EFC, P, EX, D).transpose(1, 2, 0, 3),
        "cb1": a["L0_ffn_b1"].reshape(EX, EFC, P).transpose(2, 0, 1), "cb2": np.broadcast_to(a["L0_ffn_b2"], (P, EX, D)),
        "cearlier": (key < token).astype(np.float32), "cones": np.ones((P, P), np.float32),
        "cgroup": rows(np.arange(SLOT_GROUPS, dtype=np.float32)), "cstart": rows(np.arange(MAX_GROUPS, dtype=np.float32) * GROUP_ROWS),
        "crouter": by_rows(a["L0_ffn_router_w"].T), "cnumber": rows(np.arange(EX, dtype=np.float32)),
    }
    nc = bacc.Bacc("TRN2", target_bir_lowering=False, num_devices=1)
    arrays, d = {}, {}
    for name, v in data.items():
        arrays[name + "_dram"] = v = np.ascontiguousarray(v)
        d[name] = nc.dram_tensor(name + "_dram", v.shape, mybir.dt.from_np(v.dtype), kind="ExternalInput").ap()
    out = nc.dram_tensor("out_dram", (B * S, D), FP, kind="ExternalOutput").ap()
    build(nc, d, out)
    r = run_bass_kernel_spmd(nc, [arrays], core_ids=[0])
    return r.results[0]["out_dram"].reshape(B, S, D)
```
